# Optimizing a Trainium2 kernel written in Bass

```python
import numpy as np
import jax
import jax.numpy as jnp

def _softmax(x, axis=-1):
    return jax.nn.softmax(x, axis=axis)

def _gelu(x):
    return jax.nn.gelu(x, approximate=True)

def _silu(x):
    return jax.nn.silu(x)

def _sigmoid(x):
    return jax.nn.sigmoid(x)

def _layernorm(x, axis=-1, eps=1e-05):
    m = jnp.mean(x, axis=axis, keepdims=True)
    v = jnp.var(x, axis=axis, keepdims=True)
    return (x - m) / jnp.sqrt(v + eps)

def _scatter_add(tgt, idx, src, axis=0):
    return tgt.at[idx].add(src)

def _segment_sum(src, seg, n):
    return jax.ops.segment_sum(src, seg, n)
kernel_name = 'mk_adaln_d1_jaxref_r4_863b99'

def setup_inputs(seed: int=0):
    np.random.seed(seed)
    _w = jnp.asarray

    def _L0_attn_setup():
        import jax, jax.numpy as jnp
        import numpy as np
        DIM = 256
        NH = 16
        HD = DIM // NH
        DROPE = 16
        MAXSEQ = 512
        LAT = 64
        BATCH = 2
        SEQ = 512

        def _rope_freqs(max_seq, head_dim):
            inv = 1.0 / 10000.0 ** (jnp.arange(0, head_dim, 2, dtype=jnp.float32) / head_dim)
            ang = jnp.arange(max_seq, dtype=jnp.float32)[:, None] * inv[None, :]
            return (jnp.cos(ang), jnp.sin(ang))

        def _apply_decoupled_rope(x, cosf, sinf, d_rope):
            b, d1, d2, hd = x.shape
            half = d_rope // 2
            xr = x[..., :d_rope].astype(jnp.float32).reshape(b, d1, d2, half, 2)
            xa, xb = (xr[..., 0], xr[..., 1])
            c = cosf[:d1, :half][None, :, None, :]
            s = sinf[:d1, :half][None, :, None, :]
            rot = jnp.stack([xa * c - xb * s, xa * s + xb * c], axis=-1)
            rot = rot.reshape(b, d1, d2, d_rope)
            return jnp.concatenate([rot, x[..., d_rope:]], axis=-1)
        key = jax.random.key(seed)
        ks = jax.random.split(key, 8)

        def w(k, o, i):
            return jax.random.normal(k, (o, i), jnp.float32) / np.sqrt(i).astype(np.float32)
        return {'x': jax.random.normal(ks[0], (BATCH, SEQ, DIM), jnp.float32), 'wq': w(ks[1], NH * HD, DIM), 'wk_a': w(ks[2], LAT, DIM), 'wk_b': w(ks[3], NH * HD, LAT), 'wv_a': w(ks[4], LAT, DIM), 'wv_b': w(ks[5], NH * HD, LAT), 'wo': w(ks[6], DIM, NH * HD)}
    _L0_attn_in = _L0_attn_setup()

    def _L0_ffn_setup():
        import jax, jax.numpy as jnp
        import numpy as np
        DIM = 256
        DEPTH = 2
        HEADS = 8
        DIM_HEAD = 64
        WINDOW = 128
        INNER = HEADS * DIM_HEAD
        HID = int(DIM * 4 * 2 / 3)
        B, N = (2, 2048)
        QK_SCALE = 8.0

        def shift_token(t):
            t1, t2 = jnp.split(t, 2, axis=-1)
            t2 = jnp.pad(t2, ((0, 0), (1, 0), (0, 0)))[:, :-1]
            return jnp.concatenate([t1, t2], axis=-1)

        def l2norm(t):
            return t / jnp.clip(jnp.linalg.norm(t, axis=-1, keepdims=True), 1e-12)

        def rotate_half(x):
            x1, x2 = jnp.split(x, 2, axis=-1)
            return jnp.concatenate([-x2, x1], axis=-1)

        def rotary_xpos(q, k):
            n = q.shape[-2]
            half_idx = jnp.arange(0, DIM_HEAD, 2, dtype=jnp.float32)
            inv_freq = 1.0 / 10000.0 ** (half_idx / DIM_HEAD)
            t = jnp.arange(n, dtype=jnp.float32)
            freqs = t[:, None] * inv_freq[None, :]
            freqs = jnp.concatenate([freqs, freqs], axis=-1)
            base = (half_idx + 0.4 * DIM_HEAD) / (1.4 * DIM_HEAD)
            power = (t - n // 2) / float(WINDOW // 2)
            scale = base[None, :] ** power[:, None]
            scale = jnp.concatenate([scale, scale], axis=-1)
            cos, sin = (jnp.cos(freqs), jnp.sin(freqs))
            q = q * cos * scale + rotate_half(q) * sin * scale
            k = k * cos / scale + rotate_half(k) * sin / scale
            return (q, k)

        def local_attention(q, k, v):
            b, h, n, d = q.shape
            w = n // WINDOW
            bq = q.reshape(b, h, w, WINDOW, d) * QK_SCALE
            bk = k.reshape(b, h, w, WINDOW, d)
            bv = v.reshape(b, h, w, WINDOW, d)

            def look_around(t):
                p = jnp.pad(t, ((0, 0), (0, 0), (1, 0), (0, 0), (0, 0)))
                return jnp.concatenate([p[:, :, :w], p[:, :, 1:]], axis=3)
            bk, bv = (look_around(bk), look_around(bv))
            bt = jnp.arange(n).reshape(w, WINDOW)
            btp = jnp.pad(bt, ((1, 0), (0, 0)), constant_values=-1)
            btk = jnp.concatenate([btp[:w], btp[1:]], axis=1)
            sim = jnp.einsum('bhwid,bhwjd->bhwij', bq, bk)
            i = bt[:, :, None]
            j = btk[:, None, :]
            mask = (i < j) | (i > j + WINDOW) | (j == -1)
            sim = jnp.where(mask, -jnp.finfo(sim.dtype).max, sim)
            attn = jax.nn.softmax(sim, axis=-1)
            out = jnp.einsum('bhwij,bhwjd->bhwid', attn, bv)
            return out.reshape(b, h, n, d)

        def _layer(x, wqkv, qs, ksc, wo, lg, lb, w1, b1, w2, b2):
            b, n, _ = x.shape
            h = shift_token(x)
            qkv = h @ wqkv
            q, k, v = jnp.split(qkv, 3, axis=-1)
            to_heads = lambda t: t.reshape(b, n, HEADS, DIM_HEAD).transpose(0, 2, 1, 3)
            q, k, v = (to_heads(q), to_heads(k), to_heads(v))
            q = l2norm(q) * qs
            k = l2norm(k) * ksc
            q, k = rotary_xpos(q, k)
            o = local_attention(q, k, v)
            o = o.transpose(0, 2, 1, 3).reshape(b, n, INNER)
            x = x + o @ wo
            h = shift_token(x)
            mu = h.mean(-1, keepdims=True)
            var = h.var(-1, keepdims=True)
            h = (h - mu) / jnp.sqrt(var + 1e-05) * lg + lb
            h = h @ w1 + b1
            a, g = jnp.split(h, 2, axis=-1)
            h = a * jax.nn.gelu(g, approximate=False)
            x = x + h @ w2 + b2
            return x
        key = jax.random.key(seed)
        ks = jax.random.split(key, 6)
        return {'x': jax.random.normal(ks[0], (B, N, DIM), jnp.float32), 'wqkv': jax.random.normal(ks[1], (DEPTH, DIM, 3 * INNER), jnp.float32) * 0.02, 'q_scale': jnp.ones((DEPTH, DIM_HEAD), jnp.float32), 'k_scale': jnp.ones((DEPTH, DIM_HEAD), jnp.float32), 'wo': jax.random.normal(ks[2], (DEPTH, INNER, DIM), jnp.float32) * 0.02, 'ln_g': jnp.ones((DEPTH, DIM), jnp.float32), 'ln_b': jnp.zeros((DEPTH, DIM), jnp.float32), 'w1': jax.random.normal(ks[3], (DEPTH, DIM, 2 * HID), jnp.float32) * 0.02, 'b1': jnp.zeros((DEPTH, 2 * HID), jnp.float32), 'w2': jax.random.normal(ks[4], (DEPTH, HID, DIM), jnp.float32) * 0.02, 'b2': jnp.zeros((DEPTH, DIM), jnp.float32)}
    _L0_ffn_in = _L0_ffn_setup()
    _L0_c = _w((lambda *s: np.random.randn(*s).astype(np.float32) * 0.05)(8, 256))
    _L0_wmod = _w((lambda *s: np.random.randn(*s).astype(np.float32) * 0.05)(256, 6 * 256) * 256 ** (-0.5))
    _d = {'L0_attn_x': _L0_attn_in['x'], 'L0_attn_wq': _L0_attn_in['wq'], 'L0_attn_wk_a': _L0_attn_in['wk_a'], 'L0_attn_wk_b': _L0_attn_in['wk_b'], 'L0_attn_wv_a': _L0_attn_in['wv_a'], 'L0_attn_wv_b': _L0_attn_in['wv_b'], 'L0_attn_wo': _L0_attn_in['wo'], 'L0_ffn_wqkv': _L0_ffn_in['wqkv'], 'L0_ffn_q_scale': _L0_ffn_in['q_scale'], 'L0_ffn_k_scale': _L0_ffn_in['k_scale'], 'L0_ffn_wo': _L0_ffn_in['wo'], 'L0_ffn_ln_g': _L0_ffn_in['ln_g'], 'L0_ffn_ln_b': _L0_ffn_in['ln_b'], 'L0_ffn_w1': _L0_ffn_in['w1'], 'L0_ffn_b1': _L0_ffn_in['b1'], 'L0_ffn_w2': _L0_ffn_in['w2'], 'L0_ffn_b2': _L0_ffn_in['b2'], 'L0_c': _L0_c, 'L0_wmod': _L0_wmod}
    _x0 = _d['L0_attn_x']
    _d['L0_attn_x'] = jax.random.normal(jax.random.fold_in(jax.random.key(seed), 1), (8, 1024, 256), dtype=_x0.dtype)
    del _x0
    return _d

def reference(L0_attn_x, L0_attn_wq, L0_attn_wk_a, L0_attn_wk_b, L0_attn_wv_a, L0_attn_wv_b, L0_attn_wo, L0_ffn_wqkv, L0_ffn_q_scale, L0_ffn_k_scale, L0_ffn_wo, L0_ffn_ln_g, L0_ffn_ln_b, L0_ffn_w1, L0_ffn_b1, L0_ffn_w2, L0_ffn_b2, L0_c, L0_wmod):

    def _L0_attn_ref(x, wq, wk_a, wk_b, wv_a, wv_b, wo):
        import jax, jax.numpy as jnp
        import numpy as np
        DIM = 256
        NH = 16
        HD = DIM // NH
        DROPE = 16
        MAXSEQ = 512
        LAT = 64
        BATCH = 2
        SEQ = 512

        def _rope_freqs(max_seq, head_dim):
            inv = 1.0 / 10000.0 ** (jnp.arange(0, head_dim, 2, dtype=jnp.float32) / head_dim)
            ang = jnp.arange(max_seq, dtype=jnp.float32)[:, None] * inv[None, :]
            return (jnp.cos(ang), jnp.sin(ang))

        def _apply_decoupled_rope(x, cosf, sinf, d_rope):
            b, d1, d2, hd = x.shape
            half = d_rope // 2
            xr = x[..., :d_rope].astype(jnp.float32).reshape(b, d1, d2, half, 2)
            xa, xb = (xr[..., 0], xr[..., 1])
            c = cosf[:d1, :half][None, :, None, :]
            s = sinf[:d1, :half][None, :, None, :]
            rot = jnp.stack([xa * c - xb * s, xa * s + xb * c], axis=-1)
            rot = rot.reshape(b, d1, d2, d_rope)
            return jnp.concatenate([rot, x[..., d_rope:]], axis=-1)
        b, s, _ = x.shape
        q = (x @ wq.T).reshape(b, s, NH, HD).transpose(0, 2, 1, 3)
        k = (x @ wk_a.T @ wk_b.T).reshape(b, s, NH, HD).transpose(0, 2, 1, 3)
        v = (x @ wv_a.T @ wv_b.T).reshape(b, s, NH, HD).transpose(0, 2, 1, 3)
        cosf, sinf = _rope_freqs(MAXSEQ, HD)
        q = _apply_decoupled_rope(q, cosf, sinf, DROPE)
        k = _apply_decoupled_rope(k, cosf, sinf, DROPE)
        scores = jnp.einsum('bhqd,bhkd->bhqk', q, k) / np.float32(np.sqrt(HD))
        attn = jax.nn.softmax(scores, axis=-1)
        out = jnp.einsum('bhqk,bhkd->bhqd', attn, v)
        out = out.transpose(0, 2, 1, 3).reshape(b, s, NH * HD)
        return out @ wo.T

    def _L0_ffn_ref(x, wqkv, q_scale, k_scale, wo, ln_g, ln_b, w1, b1, w2, b2):
        import jax, jax.numpy as jnp
        import numpy as np
        DIM = 256
        DEPTH = 2
        HEADS = 8
        DIM_HEAD = 64
        WINDOW = 128
        INNER = HEADS * DIM_HEAD
        HID = int(DIM * 4 * 2 / 3)
        B, N = (2, 2048)
        QK_SCALE = 8.0

        def shift_token(t):
            t1, t2 = jnp.split(t, 2, axis=-1)
            t2 = jnp.pad(t2, ((0, 0), (1, 0), (0, 0)))[:, :-1]
            return jnp.concatenate([t1, t2], axis=-1)

        def l2norm(t):
            return t / jnp.clip(jnp.linalg.norm(t, axis=-1, keepdims=True), 1e-12)

        def rotate_half(x):
            x1, x2 = jnp.split(x, 2, axis=-1)
            return jnp.concatenate([-x2, x1], axis=-1)

        def rotary_xpos(q, k):
            n = q.shape[-2]
            half_idx = jnp.arange(0, DIM_HEAD, 2, dtype=jnp.float32)
            inv_freq = 1.0 / 10000.0 ** (half_idx / DIM_HEAD)
            t = jnp.arange(n, dtype=jnp.float32)
            freqs = t[:, None] * inv_freq[None, :]
            freqs = jnp.concatenate([freqs, freqs], axis=-1)
            base = (half_idx + 0.4 * DIM_HEAD) / (1.4 * DIM_HEAD)
            power = (t - n // 2) / float(WINDOW // 2)
            scale = base[None, :] ** power[:, None]
            scale = jnp.concatenate([scale, scale], axis=-1)
            cos, sin = (jnp.cos(freqs), jnp.sin(freqs))
            q = q * cos * scale + rotate_half(q) * sin * scale
            k = k * cos / scale + rotate_half(k) * sin / scale
            return (q, k)

        def local_attention(q, k, v):
            b, h, n, d = q.shape
            w = n // WINDOW
            bq = q.reshape(b, h, w, WINDOW, d) * QK_SCALE
            bk = k.reshape(b, h, w, WINDOW, d)
            bv = v.reshape(b, h, w, WINDOW, d)

            def look_around(t):
                p = jnp.pad(t, ((0, 0), (0, 0), (1, 0), (0, 0), (0, 0)))
                return jnp.concatenate([p[:, :, :w], p[:, :, 1:]], axis=3)
            bk, bv = (look_around(bk), look_around(bv))
            bt = jnp.arange(n).reshape(w, WINDOW)
            btp = jnp.pad(bt, ((1, 0), (0, 0)), constant_values=-1)
            btk = jnp.concatenate([btp[:w], btp[1:]], axis=1)
            sim = jnp.einsum('bhwid,bhwjd->bhwij', bq, bk)
            i = bt[:, :, None]
            j = btk[:, None, :]
            mask = (i < j) | (i > j + WINDOW) | (j == -1)
            sim = jnp.where(mask, -jnp.finfo(sim.dtype).max, sim)
            attn = jax.nn.softmax(sim, axis=-1)
            out = jnp.einsum('bhwij,bhwjd->bhwid', attn, bv)
            return out.reshape(b, h, n, d)

        def _layer(x, wqkv, qs, ksc, wo, lg, lb, w1, b1, w2, b2):
            b, n, _ = x.shape
            h = shift_token(x)
            qkv = h @ wqkv
            q, k, v = jnp.split(qkv, 3, axis=-1)
            to_heads = lambda t: t.reshape(b, n, HEADS, DIM_HEAD).transpose(0, 2, 1, 3)
            q, k, v = (to_heads(q), to_heads(k), to_heads(v))
            q = l2norm(q) * qs
            k = l2norm(k) * ksc
            q, k = rotary_xpos(q, k)
            o = local_attention(q, k, v)
            o = o.transpose(0, 2, 1, 3).reshape(b, n, INNER)
            x = x + o @ wo
            h = shift_token(x)
            mu = h.mean(-1, keepdims=True)
            var = h.var(-1, keepdims=True)
            h = (h - mu) / jnp.sqrt(var + 1e-05) * lg + lb
            h = h @ w1 + b1
            a, g = jnp.split(h, 2, axis=-1)
            h = a * jax.nn.gelu(g, approximate=False)
            x = x + h @ w2 + b2
            return x
        for l in range(DEPTH):
            x = _layer(x, wqkv[l], q_scale[l], k_scale[l], wo[l], ln_g[l], ln_b[l], w1[l], b1[l], w2[l], b2[l])
        return x
    x = L0_attn_x
    mod = (_silu(L0_c) @ L0_wmod).reshape(L0_c.shape[0], 6, 1, -1)
    sa, ca, ga, sb, cb, gb = (mod[:, 0], mod[:, 1], mod[:, 2], mod[:, 3], mod[:, 4], mod[:, 5])
    ga = (2 * (ga >= 0) - 1) * jnp.maximum(jnp.abs(ga), 0.25)
    gb = (2 * (gb >= 0) - 1) * jnp.maximum(jnp.abs(gb), 0.25)
    h = _layernorm(x, axis=-1) * (1 + ca) + sa
    x = x + ga * _L0_attn_ref(h, L0_attn_wq, L0_attn_wk_a, L0_attn_wk_b, L0_attn_wv_a, L0_attn_wv_b, L0_attn_wo)
    h = _layernorm(x, axis=-1) * (1 + cb) + sb
    x = x + gb * _L0_ffn_ref(h, L0_ffn_wqkv, L0_ffn_q_scale, L0_ffn_k_scale, L0_ffn_wo, L0_ffn_ln_g, L0_ffn_ln_b, L0_ffn_w1, L0_ffn_b1, L0_ffn_w2, L0_ffn_b2)
    return x

_drawn_inputs = setup_inputs


def setup_inputs(seed=0):
    import zlib

    import numpy as np

    out = dict(_drawn_inputs(seed))
    spreads = {'L0_ffn_q_scale': (1.0, 0.6),
     'L0_ffn_k_scale': (1.0, 0.6),
     'L0_ffn_ln_g': (1.0, 0.6),
     'L0_ffn_ln_b': (0.0, 0.8),
     'L0_ffn_b1': (0.0, 0.8),
     'L0_ffn_b2': (0.0, 0.469)}
    factors = {'L0_attn_wq': 2.961,
     'L0_attn_wk_a': 2.866,
     'L0_attn_wk_b': 2.847,
     'L0_attn_wv_b': 2.676,
     'L0_attn_wo': 2.688,
     'L0_ffn_wqkv': 6.935,
     'L0_ffn_wo': 6.817,
     'L0_ffn_w1': 4.769,
     'L0_ffn_w2': 4.75}
    for name, (base, spread) in spreads.items():
        noise = np.random.default_rng([zlib.crc32(name.encode()), seed]).standard_normal(out[name].shape)
        drawn = base * np.exp(spread * noise) if base else spread * noise
        out[name] = jnp.asarray(drawn.astype(out[name].dtype))
    for name, factor in factors.items():
        out[name] = (out[name] * factor).astype(out[name].dtype)
    return out
```

```python
from contextlib import ExitStack

import numpy as np

import concourse.bass as bass
from concourse import mybir

ALU = mybir.AluOpType
ACT = mybir.ActivationFunctionType
AX = mybir.AxisListType
F32 = mybir.dt.float32
BF16 = mybir.dt.bfloat16
I32 = mybir.dt.int32

P = 128
B, N, D = 8, 1024, 256
KT = D // P
NH, HD = 16, 16
LAT = 64
DEPTH, HEADS, DH = 2, 8, 64
WIN = 128
NW = N // WIN
INNER = HEADS * DH
HID = D * 4 * 2 // 3
HB = -(-HID // P)
HL = HID - (HB - 1) * P
QK_SCALE = 8.0
LN_EPS = 1e-5
NORM_FLOOR = 1e-24
CT = 4
CH = CT * P
NC = B * N // CH
MASKED = 3.0e38
GH = 4
NG = NH // GH
GROUPS = B * NG
Q_PARTS = (0, 1, 2, 0, 1, 0)
K_PARTS = (0, 0, 0, 1, 1, 2)
SROWS = len(Q_PARTS) * HD
RSQRT_SEED = 1597463007.0
RSQRT_STEPS = 3


class Signal:

    def __init__(self, sem, per=1):
        self.sem, self.per, self.k = sem, per, 0

    def wait(self, eng, n, c=None):
        eng.wait_ge(self.sem, n * self.per + (self.per if c is None else c))

    def begin(self):
        self.k = 0

    def step(self, ins, amount=1):
        ins.then_inc(self.sem, amount)
        self.k += amount

    def settle(self, eng, n):
        eng.wait_ge(self.sem, n * self.per + self.k)


def rsqrt(nc, eng, chain, n, x, y, t):
    chain.step(nc.vector.tensor_scalar(y.bitcast(I32), x.bitcast(I32), -0.5, RSQRT_SEED, ALU.mult, ALU.add))
    for _ in range(RSQRT_STEPS):
        chain.settle(eng, n)
        chain.step(nc.vector.scalar_tensor_tensor(out=t, in0=y, scalar=-0.5, in1=y, op0=ALU.mult, op1=ALU.mult))
        chain.settle(eng, n)
        chain.step(nc.vector.tensor_tensor(t, t, x, ALU.mult))
        chain.settle(eng, n)
        chain.step(nc.vector.scalar_tensor_tensor(out=y, in0=t, scalar=1.5, in1=y, op0=ALU.add, op1=ALU.mult))


class Arrivals:

    def __init__(self, sems, per):
        self.sems, self.per = sems, per

    def wait(self, eng, n, buf):
        eng.wait_ge(self.sems[buf], n // len(self.sems) * self.per + self.per)


RSQRT_INCS = 1 + 3 * RSQRT_STEPS


def constants():
    f = np.float32
    ident = np.eye(P, dtype=f)
    inv = f(1.0) / f(10000.0) ** (np.arange(0, HD, 2, dtype=f) / f(HD))
    ang = np.arange(NH, dtype=f)[:, None] * inv[None, :]
    rope = np.stack([np.cos(ang).reshape(-1), np.sin(ang).reshape(-1)]).astype(f)
    half = np.arange(0, DH, 2, dtype=f)
    inv2 = f(1.0) / f(10000.0) ** (half / f(DH))
    t = np.arange(N, dtype=f)
    fr = t[:, None] * inv2[None, :]
    fr = np.concatenate([fr, fr], -1)
    base = (half + f(0.4 * DH)) / f(1.4 * DH)
    power = (t - f(N // 2)) / f(WIN // 2)
    xs = base[None, :] ** power[:, None]
    xs = np.concatenate([xs, xs], -1)
    sgn = np.concatenate([-np.ones(DH // 2, f), np.ones(DH // 2, f)])
    c, s = np.cos(fr), np.sin(fr) * sgn
    trig = np.concatenate([c * xs * f(-QK_SCALE), c / xs, s * xs * f(-QK_SCALE), s / xs], -1).astype(f)
    trig = trig.reshape(NW, P, 4 * DH)
    i, j = np.arange(P)[:, None], np.arange(P)[None, :]
    own = np.where(j <= i, 0.0, MASKED)
    prev = np.where(j >= i, 0.0, MASKED)
    mask = np.stack([np.concatenate([prev if w else np.full((P, P), MASKED), own], 1) for w in range(NW)])
    return {"ident": ident, "rope": rope, "trig": trig, "mask": mask.astype(f)}


def build(nc, a, out):
    with ExitStack() as ctx:
        def dram(name, shape, dt=F32):
            return nc.dram_tensor(name, shape, dt, kind="Internal").ap()

        mod_d = dram("mod_d", [B, 6, D])
        parts_d = dram("parts_d", [2, 3, D, B, N], BF16)
        v_d = dram("v_d", [B, N, NH * 2 * HD])
        att_d = dram("att_d", [B, N, D])
        x1_d = dram("x1_d", [B, N, D])
        lo_d = [dram(f"lo{s}_d", [B, N, P]) for s in range(2 * DEPTH)]
        hi_d = [dram(f"hi{s}_d", [B, 1 + N, P]) for s in range(2 * DEPTH)]
        trig_d = dram("trig_d", [DEPTH, NW, P, 4 * DH])

        ident = ctx.enter_context(nc.sbuf_tensor("ident", [P, P], F32))
        identb = ctx.enter_context(nc.sbuf_tensor("identb", [P, P], BF16))
        with ExitStack() as first:
            w = {
                "wq": first.enter_context(nc.sbuf_tensor("wqT", [P, KT, D], F32)),
                "wa": first.enter_context(nc.sbuf_tensor("waT", [P, KT, P], F32)),
                "wkb": first.enter_context(nc.sbuf_tensor("wkbT", [P, D], F32)),
                "wvb": first.enter_context(nc.sbuf_tensor("wvbT", [P, D], F32)),
                "wo": first.enter_context(nc.sbuf_tensor("woT", [P, KT, D], F32)),
            }
            setup(nc, a, ident, identb, w, mod_d, trig_d, hi_d)
            projections(nc, a["L0_attn_x"], ident, w, mod_d, parts_d, v_d)
            full_attention(nc, ident, identb, parts_d, v_d, att_d)
            attention_out(nc, a["L0_attn_x"], ident, w, mod_d, att_d, x1_d, lo_d[0], hi_d[0])
        window_sems = ExitStack()
        with window_sems:
            ws = window_signals(nc, window_sems)
            fs = ffn_signals(nc, window_sems)
            for layer in range(DEPTH):
                s = 2 * layer
                window_attention(nc, a, layer, ident, trig_d, (lo_d[s], hi_d[s]), (lo_d[s + 1], hi_d[s + 1]), ws)
                last = layer == DEPTH - 1
                dst = None if last else (lo_d[s + 2], hi_d[s + 2])
                feed_forward(nc, a, layer, ident, (lo_d[s + 1], hi_d[s + 1]), dst, x1_d, mod_d, out, fs)


def rows(x, n):
    flat = x.rearrange("b n c -> (b n) c").rearrange("(q t p) c -> q p t c", p=P, t=CT)
    return flat[bass.ds(n, 1)].rearrange("q p t c -> (q p) t c")


def shifted(x, n, unit):
    per = N // unit
    flat = x[bass.ds(n // per, 1), bass.ds((n % per) * unit, unit), :]
    return flat.rearrange("b (t p) c -> p (b t) c", p=P)


def padded(x, n, unit):
    per = N // unit
    flat = x[bass.ds(n // per, 1), bass.ds((n % per) * unit + 1, unit), :]
    return flat.rearrange("b (t p) c -> p (b t) c", p=P)


def setup(nc, a, ident, identb, w, mod_d, trig_d, hi_d):
    with ExitStack() as ctx:
        def sb(name, shape, dt=F32):
            return ctx.enter_context(nc.sbuf_tensor(name, shape, dt))

        def sem(name):
            return ctx.enter_context(nc.semaphore(name))

        wq_r = sb("wq_r", [P, KT, D])
        wo_r = sb("wo_r", [P, KT, D])
        wa_r = sb("wa_r", [P, D])
        wb_r = sb("wb_r", [P, KT, P])
        rope = sb("rope_b", [P, 2, P])
        ropeq = sb("rope_q", [P, 2, P])
        ta, tb = sb("rope_ta", [P, KT, P]), sb("rope_tb", [P, KT, P])
        cs = sb("c_rows", [B, D])
        ce = sb("c_exp", [B, D])
        cT = sb("c_T", [P, KT, B])
        wmod = sb("wmod_sb", [P, KT, 6 * D])
        mods = sb("mods", [B, 6, D])
        ga, gs = sb("guard_a", [B, 2, D]), sb("guard_s", [B, 2, D])
        trig = sb("trig_base", [P, NW, 4 * DH])
        qks = sb("qk_scales", [P, DEPTH, 4 * DH])
        trl = sb("trig_scaled", [P, DEPTH, NW, 4 * DH])
        zrow = sb("zero_rows", [B, P])
        ps = [ctx.enter_context(nc.psum_tensor(f"ps_set{i}", [P, 512], F32)) for i in range(8)]
        loaded, turned, steps, silu, stored = (sem("set_loaded"), sem("set_turned"), sem("set_steps"),
                                               sem("set_silu"), sem("set_stored"))
        small, modm = sem("set_small"), sem("set_mod")
        n_loads = [0]

        with nc.Block() as block:
            @block.sync
            def _(sp):
                def load(dst, src):
                    sp.dma_start(dst, src).then_inc(loaded, 16)
                    n_loads[0] += 16

                load(ident[:], a["ident"])
                load(cs[:], a["L0_c"])
                load(wmod[:], a["L0_wmod"].rearrange("(k p) n -> p k n", p=P))
                load(wq_r[:], a["L0_attn_wq"].rearrange("(m p) c -> p m c", p=P))
                load(wo_r[:], a["L0_attn_wo"].rearrange("(m p) c -> p m c", p=P))
                load(wa_r[0:LAT, :], a["L0_attn_wk_a"])
                load(wa_r[LAT:P, :], a["L0_attn_wv_a"])
                load(wb_r[:, :, 0:LAT], a["L0_attn_wk_b"].rearrange("(m p) c -> p m c", p=P))
                load(wb_r[:, :, LAT:P], a["L0_attn_wv_b"].rearrange("(m p) c -> p m c", p=P))
                load(rope[:], a["rope"].rearrange("(o t) i -> o t i", o=1).to_broadcast([P, 2, P]))
                load(trig[:], a["trig"].rearrange("w p c -> p w c"))
                hd = DH // 2
                for layer in range(DEPTH):
                    for which, name in enumerate(("L0_ffn_q_scale", "L0_ffn_k_scale")):
                        src = a[name][layer:layer + 1, :]
                        at = which * DH
                        load(qks[:, layer, at:at + DH], src.to_broadcast([P, DH]))
                        at += 2 * DH
                        load(qks[:, layer, at:at + hd], src[:, hd:DH].to_broadcast([P, hd]))
                        load(qks[:, layer, at + hd:at + DH], src[:, 0:hd].to_broadcast([P, hd]))
                sp.wait_ge(small, 1)
                for h in hi_d:
                    sp.dma_start(h[:, 0, :], zrow[:]).then_inc(stored, 16)
                sp.wait_ge(small, 2 + DEPTH)
                sp.dma_start(trig_d.rearrange("l w p c -> p (l w) c"),
                             trl[:].rearrange("p l w c -> p (l w) c")).then_inc(stored, 16)
                sp.wait_ge(modm, 1)
                sp.dma_start(mod_d, mods[:]).then_inc(stored, 16)
                sp.wait_ge(stored, 16 * (len(hi_d) + 2))

            total = n_loads[0]

            @block.scalar
            def _(act):
                act.wait_ge(loaded, total)
                nc.scalar.activation(ce[:], cs[:], ACT.Exp, scale=-1.0).then_inc(silu, 1)

            @block.tensor
            def _(pe):
                pe.wait_ge(loaded, total)
                for k in range(KT):
                    for m in range(KT):
                        nc.tensor.transpose(ps[0][:, k * D + m * P:k * D + (m + 1) * P],
                                            wq_r[:, m, k * P:(k + 1) * P], ident[:])
                        nc.tensor.transpose(ps[1][:, k * D + m * P:k * D + (m + 1) * P],
                                            wo_r[:, m, k * P:(k + 1) * P], ident[:])
                    nc.tensor.transpose(ps[2][:, k * P:(k + 1) * P], wa_r[:, k * P:(k + 1) * P], ident[:])
                    last = nc.tensor.transpose(ps[3][:, k * P:(k + 1) * P], wb_r[:, k, :], ident[:])
                last.then_inc(turned, 1)
                pe.wait_ge(silu, 2)
                for k in range(KT):
                    last = nc.tensor.transpose(ps[4][:, k * B:(k + 1) * B], cs[:, k * P:(k + 1) * P],
                                               ident[0:B, 0:B])
                last.then_inc(turned, 1)
                pe.wait_ge(silu, 3)
                for j in range(3):
                    for k in range(KT):
                        last = nc.tensor.matmul(ps[5 + j][0:B, :], cT[:, k, :], wmod[:, k, j * 512:(j + 1) * 512],
                                                start=(k == 0), stop=(k == KT - 1))
                last.then_inc(turned, 1)

            @block.vector
            def _(dve):
                count = [0]

                def link(ins):
                    ins.then_inc(steps, 1)
                    count[0] += 1
                    dve.wait_ge(steps, count[0])

                link(nc.vector.memset(w["wkb"][:], 0.0))
                link(nc.vector.memset(w["wvb"][:], 0.0))
                nc.vector.memset(zrow[:], 0.0).then_inc(small, 1)
                dve.wait_ge(loaded, total)
                nc.vector.tensor_copy(identb[:], ident[:]).then_inc(small, 1)
                for layer in range(DEPTH):
                    nc.vector.tensor_tensor(trl[:, layer], trig[:],
                                            qks[:, layer, :].unsqueeze(1).to_broadcast([P, NW, 4 * DH]),
                                            ALU.mult).then_inc(small, 1)
                dve.wait_ge(silu, 1)
                link(nc.vector.tensor_scalar(ce[:], ce[:], 1.0, None, ALU.add))
                link(nc.vector.reciprocal(ce[:], ce[:]))
                nc.vector.tensor_tensor(cs[:], cs[:], ce[:], ALU.mult).then_inc(silu, 1)
                dve.wait_ge(turned, 2)
                nc.vector.tensor_copy(cT[:], ps[4][:, 0:KT * B].rearrange("p (k b) -> p k b", k=KT)).then_inc(silu, 1)
                link(nc.vector.tensor_scalar(ropeq[:], rope[:], float(HD) ** -0.5, None, ALU.mult))

                def rotate(dst, src, table, k):
                    cos = table[:, 0, :].unsqueeze(1).to_broadcast([table.shape[0], k, P])
                    sin = table[:, 1, :].unsqueeze(1).to_broadcast([table.shape[0], k, P])
                    pa, pb = ta[0:table.shape[0], 0:k, :], tb[0:table.shape[0], 0:k, :]
                    link(nc.vector.tensor_tensor(pa, src[:, :, :, 0], cos, ALU.mult))
                    link(nc.vector.tensor_tensor(pb, src[:, :, :, 1], sin, ALU.mult))
                    link(nc.vector.tensor_tensor(dst[:, :, :, 0], pa, pb, ALU.subtract))
                    link(nc.vector.tensor_tensor(pa, src[:, :, :, 0], sin, ALU.mult))
                    link(nc.vector.tensor_tensor(pb, src[:, :, :, 1], cos, ALU.mult))
                    link(nc.vector.tensor_tensor(dst[:, :, :, 1], pa, pb, ALU.add))

                rotate(w["wq"][:].rearrange("p k (i e) -> p k i e", e=2),
                       ps[0][:].rearrange("p (k i e) -> p k i e", k=KT, e=2), ropeq, KT)
                rotate(w["wkb"][0:LAT, :].rearrange("p (k i e) -> p k i e", k=1, e=2),
                       ps[3][0:LAT, 0:D].rearrange("p (k i e) -> p k i e", k=1, e=2), rope[0:LAT], 1)
                link(nc.vector.tensor_copy(w["wvb"][LAT:P, :], ps[3][LAT:P, 0:D]))
                link(nc.vector.tensor_copy(w["wo"][:].rearrange("p k n -> p (k n)"), ps[1][:]))
                link(nc.vector.tensor_copy(w["wa"][:].rearrange("p k n -> p (k n)"), ps[2][:, 0:D]))
                dve.wait_ge(turned, 3)
                for j in range(3):
                    link(nc.vector.tensor_copy(mods[:, 2 * j:2 * j + 2, :],
                                               ps[5 + j][0:B, :].rearrange("p (k n) -> p k n", k=2)))
                scale, gate = mods[:, 1:6:3, :], mods[:, 2:6:3, :]
                link(nc.vector.tensor_scalar(scale, scale, 1.0, None, ALU.add))
                link(nc.vector.tensor_scalar(gs[:], gate, 0.0, 2.0, ALU.is_ge, ALU.mult))
                link(nc.vector.tensor_scalar(gs[:], gs[:], -1.0, None, ALU.add))
                link(nc.vector.tensor_scalar(ga[:], gate, -1.0, None, ALU.mult))
                link(nc.vector.tensor_tensor(ga[:], ga[:], gate, ALU.max))
                link(nc.vector.tensor_scalar(ga[:], ga[:], 0.25, None, ALU.max))
                nc.vector.tensor_tensor(gate, ga[:], gs[:], ALU.mult).then_inc(modm, 1)


def layer_norm_stats(nc, dve, chain, n, x, stats, mv, ve, rstd, tmp):
    tiles = x.shape[1]
    for t in range(tiles):
        last = nc.vector.bn_stats(stats[:, t, :], x[:, t, :])
    chain.step(last)
    chain.settle(dve, n)
    nc.vector.memset(tmp, 0.0)
    for t in range(tiles):
        last = nc.vector.bn_aggr(mv[:, t, :], stats[:, t, :])
    chain.step(last)
    chain.settle(dve, n)
    chain.step(nc.vector.tensor_scalar(ve, mv[:, :, 1], LN_EPS, None, ALU.add))
    chain.settle(dve, n)
    rsqrt(nc, dve, chain, n, ve, rstd, tmp)
    chain.settle(dve, n)


LN_INCS = 3 + RSQRT_INCS


def projections(nc, x, ident, w, mod_d, parts_d, v_d):
    with ExitStack() as ctx:
        def sb(name, shape, dt=F32):
            return ctx.enter_context(nc.sbuf_tensor(name, shape, dt))

        def sig(name, per=1):
            return Signal(ctx.enter_context(nc.semaphore("pj_" + name)), per)

        def arrivals(name, per):
            return Arrivals([ctx.enter_context(nc.semaphore(f"pj_{name}{p}")) for p in range(2)], per)

        xt = sb("pj_x", [P, 2, CT, D])
        mrow = sb("pj_mod", [P, 2, 2, D])
        stats, mv = sb("pj_stats", [P, CT, 6]), sb("pj_mv", [P, CT, 2])
        ve, rstd, tmp = sb("pj_ve", [P, CT]), sb("pj_rstd", [P, CT]), sb("pj_tmp", [P, CT])
        xn = sb("pj_xn", [P, 2, CT, D])
        hm = sb("pj_hm", [P, 2, CT, D])
        hT = sb("pj_hT", [P, 2, KT, CH])
        lat = sb("pj_lat", [P, 2, CH])
        parts = sb("pj_parts", [P, 2, 2, 3, KT, CH], BF16)
        res = sb("pj_res", [P, 2, KT, CH])
        vs = sb("pj_v", [P, 2, CT, NH, 2 * HD])
        pH = ctx.enter_context(nc.psum_tensor("pj_pH", [P, KT, CH], F32))
        pL = ctx.enter_context(nc.psum_tensor("pj_pL", [P, CH], F32))
        pQ = ctx.enter_context(nc.psum_tensor("pj_pQ", [P, KT, CH], F32))
        pK = ctx.enter_context(nc.psum_tensor("pj_pK", [P, KT, CH], F32))

        loaded = arrivals("loaded", 32)
        chain = sig("chain", LN_INCS)
        normed = sig("normed")
        modded = sig("modded", 2)
        turned = sig("turned")
        h_ready = sig("h_ready")
        lat_done, lat_ready = sig("lat_done"), sig("lat_ready")
        q_done, k_done, v_done = sig("q_done"), sig("k_done"), sig("v_done")
        hi_ready = sig("hi_ready", 2)
        split = sig("split", 6)
        v_ready = sig("v_ready")
        stored = arrivals("stored", 16 * 7)
        ones = sig("ones")

        def drive(eng, body):
            for n in range(2):
                body(n, n)
            with eng.Fori(1, NC // 2) as i:
                for p in range(2):
                    body(i * 2 + p, p)

        def later(n):
            return not isinstance(n, int) or n >= 2

        def again(n):
            return not isinstance(n, int) or n >= 1

        with nc.Block() as block:
            @block.sync
            def _(sp):
                def load(n, p):
                    if later(n):
                        normed.wait(sp, n - 2)
                        modded.wait(sp, n - 2)
                    sp.dma_start(xt[:, p], rows(x, n)).then_inc(loaded.sems[p], 16)
                    src = mod_d[bass.ds(n // 2, 1), 0:2, :].to_broadcast([P, 2, D])
                    sp.dma_start(mrow[:, p], src).then_inc(loaded.sems[p], 16)

                def store(n, p):
                    split.wait(sp, n)
                    for qk in range(2):
                        for part in range(3):
                            dst = parts_d[qk, part].rearrange("(m p) b t -> p m b t", p=P)
                            dst = dst[:, :, bass.ds(n // 2, 1), bass.ds((n % 2) * CH, CH)]
                            sp.dma_start(dst.rearrange("p m b t -> p m (b t)"),
                                         parts[:, p, qk, part]).then_inc(stored.sems[p], 16)
                    v_ready.wait(sp, n)
                    sp.dma_start(rows(v_d, n), vs[:, p].rearrange("p t h c -> p t (h c)")).then_inc(stored.sems[p], 16)

                load(0, 0)
                load(1, 1)
                store(0, 0)
                load(2, 0)
                with sp.Fori(0, NC // 2 - 2) as i:
                    for q in range(2):
                        store(i * 2 + 1 + q, 1 - q)
                        load(i * 2 + 3 + q, 1 - q)
                store(NC - 3, 1)
                load(NC - 1, 1)
                store(NC - 2, 0)
                store(NC - 1, 1)
                stored.wait(sp, NC - 2, 0)
                stored.wait(sp, NC - 1, 1)

            @block.vector
            def _(dve):
                nc.vector.memset(vs[:, :, :, :, HD:2 * HD], 1.0).then_inc(ones.sem, 1)

                def norm(n, p):
                    chain.begin()
                    loaded.wait(dve, n, p)
                    layer_norm_stats(nc, dve, chain, n, xt[:, p], stats, mv, ve[:], rstd[:], tmp[:])
                    if later(n):
                        modded.wait(dve, n - 2, 1)
                    for t in range(CT):
                        last = nc.vector.tensor_scalar(xn[:, p, t, :], xt[:, p, t, :], mv[:, t, 0:1],
                                                       rstd[:, t:t + 1], ALU.subtract, ALU.mult)
                    last.then_inc(normed.sem, 1)

                def parts_of(n, p):
                    split.begin()
                    for qk, ps in enumerate((pQ, pK)):
                        hi_ready.wait(dve, n, qk + 1)
                        r = res[:, qk].rearrange("p m t -> p (m t)")
                        hi, mid, lo = (parts[:, p, qk, j].rearrange("p m t -> p (m t)") for j in range(3))
                        split.step(nc.vector.tensor_tensor(r, ps[:].rearrange("p m t -> p (m t)"), hi, ALU.subtract))
                        split.settle(dve, n)
                        if later(n) and qk == 0:
                            stored.wait(dve, n - 2, p)
                        split.step(nc.vector.tensor_copy(mid, r))
                        split.settle(dve, n)
                        split.step(nc.vector.tensor_tensor(lo, r, mid, ALU.subtract))

                norm(0, 0)
                for n in range(2):
                    norm(n + 1, (n + 1) % 2)
                    parts_of(n, n)
                with dve.Fori(0, NC // 2 - 2) as i:
                    for p in range(2):
                        norm(i * 2 + 3 + p, 1 - p)
                        parts_of(i * 2 + 2 + p, p)
                norm(NC - 1, 1)
                parts_of(NC - 2, 0)
                parts_of(NC - 1, 1)

            @block.gpsimd
            def _(pool):
                def body(n, p):
                    normed.wait(pool, n)
                    for t_in, t_out, row, op in ((xn, xn, 1, ALU.mult), (xn, hm, 0, ALU.add)):
                        if row == 0:
                            modded.wait(pool, n, 1)
                            if later(n):
                                turned.wait(pool, n - 2)
                        nc.gpsimd.tensor_tensor(t_out[:, p], t_in[:, p],
                                                mrow[:, p, row, :].unsqueeze(1).to_broadcast([P, CT, D]),
                                                op).then_inc(modded.sem, 1)

                drive(pool, body)

            @block.tensor
            def _(pe):
                def body(n, p):
                    modded.wait(pe, n)
                    if again(n):
                        v_ready.wait(pe, n - 1)
                    for t in range(CT):
                        for k in range(KT):
                            last = nc.tensor.transpose(pH[:, k, t * P:(t + 1) * P],
                                                       hm[:, p, t, k * P:(k + 1) * P], ident[:])
                    last.then_inc(turned.sem, 1)
                    h_ready.wait(pe, n)
                    if again(n):
                        lat_ready.wait(pe, n - 1)
                    for k in range(KT):
                        last = nc.tensor.matmul(pL[:], w["wa"][:, k, :], hT[:, p, k, :],
                                                start=(k == 0), stop=(k == KT - 1))
                    last.then_inc(lat_done.sem, 1)
                    if again(n):
                        split.wait(pe, n - 1, 1)
                    for m in range(KT):
                        for k in range(KT):
                            last = nc.tensor.matmul(pQ[:, m, :], w["wq"][:, k, m * P:(m + 1) * P], hT[:, p, k, :],
                                                    start=(k == 0), stop=(k == KT - 1))
                    last.then_inc(q_done.sem, 1)
                    lat_ready.wait(pe, n)
                    if again(n):
                        split.wait(pe, n - 1, 4)
                    for m in range(KT):
                        last = nc.tensor.matmul(pK[:, m, :], w["wkb"][:, m * P:(m + 1) * P], lat[:, p, :],
                                                start=True, stop=True)
                    last.then_inc(k_done.sem, 1)
                    for t in range(CT):
                        last = nc.tensor.matmul(pH[:, t // 2, (t % 2) * D:(t % 2 + 1) * D],
                                                lat[:, p, t * P:(t + 1) * P], w["wvb"][:], start=True, stop=True)
                    last.then_inc(v_done.sem, 1)

                drive(pe, body)

            @block.scalar
            def _(act):
                act.wait_ge(ones.sem, 1)

                def body(n, p):
                    turned.wait(act, n)
                    if later(n):
                        q_done.wait(act, n - 2)
                    nc.scalar.copy(hT[:, p], pH[:]).then_inc(h_ready.sem, 1)
                    lat_done.wait(act, n)
                    if later(n):
                        v_done.wait(act, n - 2)
                    nc.scalar.copy(lat[:, p], pL[:]).then_inc(lat_ready.sem, 1)
                    if later(n):
                        stored.wait(act, n - 2, p)
                    q_done.wait(act, n)
                    nc.scalar.copy(parts[:, p, 0, 0], pQ[:]).then_inc(hi_ready.sem, 1)
                    k_done.wait(act, n)
                    nc.scalar.copy(parts[:, p, 1, 0], pK[:]).then_inc(hi_ready.sem, 1)
                    v_done.wait(act, n)
                    for j in range(2):
                        last = nc.scalar.copy(vs[:, p, 2 * j:2 * j + 2, :, 0:HD],
                                              pH[:, j, :].rearrange("p (t h c) -> p t h c", t=2, h=NH))
                    last.then_inc(v_ready.sem, 1)

                drive(act, body)


def full_attention(nc, ident, identb, parts_d, v_d, att_d):
    KB = N // P
    STEP_EXPS = GH
    ROW_USES = (10, 10, 10, 10, 8, 8, 8, 0)
    MAX_USES = 2 * GH * KB
    assert sum(ROW_USES) == MAX_USES
    NB = 3

    with ExitStack() as ctx:
        def sb(name, shape, dt=F32):
            return ctx.enter_context(nc.sbuf_tensor(name, shape, dt))

        def sem(name):
            return ctx.enter_context(nc.semaphore("fa_" + name))

        Qs = sb("fa_Q", [P, NB, GH, N], BF16)
        Ks = sb("fa_K", [P, NB, GH, N], BF16)
        V = sb("fa_V", [P, NB, KB, GH, 2 * HD])
        Pr = sb("fa_P", [P, 2, GH, N])
        OT = sb("fa_OT", [P, N])
        mx = sb("fa_mx", [P, GH * KB, 2])
        nm = sb("fa_nm", [P, GH * KB])
        nb = sb("fa_nb", [P, KB, 2, GH], BF16)
        nrow = sb("fa_nrow", [2 * GH, NB, N], BF16)
        rec = sb("fa_rec", [P, 2, 4 * GH])
        att = sb("fa_att", [P, KB, GH * HD])
        pS = ctx.enter_context(nc.psum_tensor("fa_pS", [P, 2, N], F32))
        pR = ctx.enter_context(nc.psum_tensor("fa_pR", [P, 2, 512], F32))
        pO = ctx.enter_context(nc.psum_tensor("fa_pO", [P, 2, 512], F32))

        stack_in = Arrivals([sem(f"stack_in{s}") for s in range(NB)], 16 * 12)
        v_in = Arrivals([sem(f"v_in{s}") for s in range(NB)], 16)
        max_in = Arrivals([sem(f"max_in{s}") for s in range(NB)], 32)
        ones = Signal(sem("ones"), 1)
        scored = Signal(sem("scored"), KB * GH)
        exped = Signal(sem("exped"), KB * GH)
        summed = Signal(sem("summed"), KB)
        o_out = Signal(sem("o_out"), 1)
        row_full, row_free = sem("row_full"), sem("row_free")
        neg = Signal(sem("neg"), 4)
        inverse = Signal(sem("inverse"), 2)
        stored = Signal(sem("stored"), 16)

        def first_use(n):
            if isinstance(n, int) and n <= 0:
                return 0 if n < 0 else MAX_USES + 2
            return MAX_USES + (MAX_USES + 4) * n

        def divided_wait(eng, n):
            early = 0 if isinstance(n, int) and n >= GROUPS - 2 else ROW_USES[0] + ROW_USES[1]
            at = first_use(GROUPS - 1) + 2 if is_last(n) else first_use(n + 1) + early
            eng.wait_ge(row_free, at + 2)

        def drive(eng, body):
            body(0, 0)
            with eng.Fori(0, (GROUPS - 2) // NB) as i:
                for j in range(NB):
                    body(i * NB + 1 + j, (1 + j) % NB)
            body(GROUPS - 1, (GROUPS - 1) % NB)

        def is_first(n):
            return isinstance(n, int) and n == 0

        def is_last(n):
            return isinstance(n, int) and n == GROUPS - 1

        with nc.Block() as block:
            @block.sync
            def _(sp):
                def load(n, s):
                    b, g = n // NG, n % NG
                    for stack, qk, order in ((Qs, 0, Q_PARTS), (Ks, 1, K_PARTS)):
                        for slot, part in enumerate(order):
                            src = parts_d[qk, part].rearrange("(g h d) b t -> d g h b t", d=HD, h=GH)
                            src = src[:, bass.ds(g, 1), :, bass.ds(b, 1), :]
                            sp.dma_start(stack[slot * HD:(slot + 1) * HD, s],
                                         src.rearrange("d g h b t -> d (g h) (b t)")).then_inc(stack_in.sems[s], 16)
                    src = v_d[bass.ds(b, 1), :, bass.ds(g * (GH * 2 * HD), GH * 2 * HD)]
                    sp.dma_start(V[:, s].rearrange("p k h c -> p k (h c)"),
                                 src.rearrange("b (k p) c -> p (b k) c", p=P)).then_inc(v_in.sems[s], 16)

                def max_rows(n, s):
                    sp.wait_ge(row_free, first_use(n))
                    for part in range(2):
                        dst = Qs[SROWS + part:SROWS + part + 1, s]
                        sp.dma_start(dst, nrow[part * GH:(part + 1) * GH, s, :]).then_inc(max_in.sems[s], 16)

                def store(n):
                    divided_wait(sp, n)
                    b, g = n // NG, n % NG
                    dst = att_d[bass.ds(b, 1), :, bass.ds(g * (GH * HD), GH * HD)]
                    sp.dma_start(dst.rearrange("b (k p) c -> p (b k) c", p=P), att[:]).then_inc(stored.sem, 16)

                load(0, 0)
                load(1, 1)
                max_rows(0, 0)
                load(2, 2)

                def body(n, s):
                    if not is_first(n):
                        if not (isinstance(n, int) and n + 2 >= GROUPS):
                            scored.wait(sp, n - 1)
                            summed.wait(sp, n - 1)
                            load(n + 2, (s + 2) % NB)
                        store(n - 1)
                    if not is_last(n):
                        max_rows(n + 1, (s + 1) % NB)

                body(0, 0)
                with sp.Fori(0, (GROUPS - 2) // NB - 1) as i:
                    for j in range(NB):
                        body(i * NB + 1 + j, (1 + j) % NB)
                for n in range(GROUPS - 1 - NB, GROUPS):
                    body(n, n % NB)
                store(GROUPS - 1)
                stored.wait(sp, GROUPS - 1)

            @block.tensor
            def _(pe):
                use = [0, 0]

                def row_tile():
                    base, k = use
                    if not (isinstance(base, int) and base + k < 2):
                        pe.wait_ge(row_free, base + k - 1)
                    use[1] += 1
                    return pR[:, k % 2, :]

                def row_scores(n, s, j):
                    h, q, half = j // (2 * KB), j // 2 % KB, j % 2
                    if j == 0:
                        stack_in.wait(pe, n, s)
                    nc.tensor.matmul(row_tile(), Qs[0:SROWS, s, h, q * P:(q + 1) * P],
                                     Ks[0:SROWS, s, h, half * 512:(half + 1) * 512],
                                     start=True, stop=True).then_inc(row_full, 1)

                def turn_max(n):
                    neg.wait(pe, n)
                    for half in range(2):
                        r = row_tile()
                        for q in range(4):
                            last = nc.tensor.matmul(r[0:2 * GH, q * P:(q + 1) * P],
                                                    nb[:, half * 4 + q].rearrange("p a h -> p (a h)"), identb[:],
                                                    start=True, stop=True)
                        last.then_inc(row_full, 1)

                def scores(n, s, k, h):
                    e = k * GH + h
                    if e == 0:
                        max_in.wait(pe, n, s)
                        if is_first(n):
                            ones.wait(pe, 0)
                    if not (is_first(n) and e < 2):
                        pe.wait_ge(exped.sem, n * exped.per + e - 1)
                    for half in range(2):
                        last = nc.tensor.matmul(pS[:, e % 2, half * 512:(half + 1) * 512],
                                                Ks[0:SROWS + 2, s, h, k * P:(k + 1) * P],
                                                Qs[0:SROWS + 2, s, h, half * 512:(half + 1) * 512],
                                                start=True, stop=True)
                    last.then_inc(scored.sem, 1)

                def sums(n, s, k, half):
                    if half == 0:
                        exped.wait(pe, n, (k + 1) * GH)
                        if k == 0:
                            v_in.wait(pe, n, s)
                            if not is_first(n):
                                o_out.wait(pe, n - 1)
                    for h in range(GH):
                        last = nc.tensor.matmul(pO[h * 32:(h + 1) * 32, half, :], V[:, s, k, h, :],
                                                Pr[:, k % 2, h, half * 512:(half + 1) * 512],
                                                start=(k == 0), stop=(k == KB - 1))
                    if half == 1:
                        last.then_inc(summed.sem, 1)

                def turn_sums(n):
                    o_out.wait(pe, n)
                    for half in range(2):
                        r = row_tile()
                        for t in range(4):
                            at = (half * 4 + t) * P
                            last = nc.tensor.transpose(r[:, t * P:(t + 1) * P], OT[:, at:at + P], ident[:])
                        last.then_inc(row_full, 1)

                for j in range(MAX_USES):
                    row_scores(0, 0, j)
                turn_max(0)

                def body(n, s):
                    use[0], use[1] = first_use(n), 0
                    done = 0
                    for k in range(KB):
                        todo = 0 if is_last(n) else ROW_USES[k]
                        for h in range(GH):
                            scores(n, s, k, h)
                            upto = done + todo * (h + 1) // GH - todo * h // GH
                            for j in range(done, upto):
                                row_scores(n + 1, (s + 1) % NB, j)
                            done = upto
                            if h in (1, 2):
                                if k > 0:
                                    sums(n, s, k - 1, h - 1)
                                elif not is_first(n):
                                    sums(n - 1, (s - 1) % NB, KB - 1, h - 1)
                        if k == 1 and not is_first(n):
                            turn_sums(n - 1)
                    if not is_last(n):
                        turn_max(n + 1)

                drive(pe, body)
                for half in range(2):
                    sums(GROUPS - 1, (GROUPS - 1) % NB, KB - 1, half)
                use[0], use[1] = first_use(GROUPS - 1) + 2, 0
                turn_sums(GROUPS - 1)

            @block.scalar
            def _(act):
                def copy_out(n):
                    summed.wait(act, n)
                    if not is_first(n):
                        divided_wait(act, n - 1)
                    nc.scalar.copy(OT[:], pO[:].rearrange("p a q -> p (a q)")).then_inc(o_out.sem, 1)

                def body(n, s):
                    for k in range(KB):
                        for h in range(GH):
                            e = k * GH + h
                            scored.wait(act, n, e + 1)
                            if h == 0 and not (is_first(n) and k < 2):
                                act.wait_ge(summed.sem, n * KB + k - 1)
                            nc.scalar.activation(Pr[:, k % 2, h, :], pS[:, e % 2, :], ACT.Exp).then_inc(exped.sem, 1)
                        if k == 0 and not is_first(n):
                            copy_out(n - 1)

                drive(act, body)
                copy_out(GROUPS - 1)

            @block.vector
            def _(dve):
                use = [0, 0]
                for s in range(NB):
                    last = nc.vector.memset(Ks[SROWS:SROWS + 2, s], 1.0)
                last.then_inc(ones.sem, 1)

                def row_tile():
                    base, k = use
                    dve.wait_ge(row_full, base + k + 1)
                    use[1] += 1
                    return pR[:, k % 2, :]

                def row_max(j):
                    nc.vector.tensor_reduce(mx[:, j // 2, j % 2:j % 2 + 1], row_tile(), AX.X,
                                            ALU.max).then_inc(row_free, 1)

                def negative(n):
                    neg.begin()
                    dve.wait_ge(row_free, use[0] + use[1])
                    neg.step(nc.vector.tensor_reduce(nm[:], mx[:], AX.X, ALU.max, negate=True))
                    neg.settle(dve, n)
                    hi = nb[:, :, 0, :].rearrange("p q h -> p h q")
                    lo = nb[:, :, 1, :].rearrange("p q h -> p h q")
                    m = nm[:].rearrange("p (h q) -> p h q", h=GH)
                    neg.step(nc.vector.tensor_copy(hi, m))
                    neg.settle(dve, n)
                    neg.step(nc.vector.tensor_tensor(m, m, hi, ALU.subtract))
                    neg.settle(dve, n)
                    neg.step(nc.vector.tensor_copy(lo, m))

                def max_out(n, s):
                    for half in range(2):
                        r = row_tile()
                        nc.vector.tensor_copy(nrow[:, s, half * 512:(half + 1) * 512],
                                              r[0:2 * GH, :]).then_inc(row_free, 1)

                def divide(n):
                    inverse.begin()
                    for half in range(2):
                        r = row_tile().rearrange("p (a c) -> p a c", c=2 * HD)
                        if half == 0 and not is_first(n):
                            stored.wait(dve, n - 1)
                        inverse.step(nc.vector.reciprocal(rec[:, half, :], r[:, :, HD]))
                        inverse.settle(dve, n)
                        dst = att[:, half * 4:(half + 1) * 4, :].rearrange("p t (h c) -> p (t h) c", c=HD)
                        nc.vector.tensor_tensor(dst, r[:, :, 0:HD],
                                                rec[:, half, :].unsqueeze(2).to_broadcast([P, 4 * GH, HD]),
                                                ALU.mult).then_inc(row_free, 1)

                for j in range(MAX_USES):
                    row_max(j)
                negative(0)
                max_out(0, 0)

                def body(n, s):
                    use[0], use[1] = first_use(n), 0
                    done = 0
                    for k in range(KB):
                        todo = 0 if is_last(n) else ROW_USES[k]
                        for j in range(done, done + todo):
                            row_max(j)
                        done += todo
                        if k == 1 and not is_first(n):
                            divide(n - 1)
                    if not is_last(n):
                        negative(n + 1)
                        max_out(n + 1, (s + 1) % NB)

                drive(dve, body)
                use[0], use[1] = first_use(GROUPS - 1) + 2, 0
                divide(GROUPS - 1)


def attention_out(nc, x, ident, w, mod_d, att_d, x1_d, lo_dst, hi_dst):
    with ExitStack() as ctx:
        def sb(name, shape, dt=F32):
            return ctx.enter_context(nc.sbuf_tensor(name, shape, dt))

        def sig(name, per=1):
            return Signal(ctx.enter_context(nc.semaphore("ao_" + name)), per)

        def arrivals(name, per):
            return Arrivals([ctx.enter_context(nc.semaphore(f"ao_{name}{p}")) for p in range(2)], per)

        at = sb("ao_att", [P, 2, CT, D])
        xt = sb("ao_x", [P, 2, CT, D])
        mrow = sb("ao_mod", [P, 2, 3, D])
        aT = sb("ao_aT", [P, KT, CH])
        x1 = sb("ao_x1", [P, 2, CT, D])
        stats, mv = sb("ao_stats", [P, CT, 6]), sb("ao_mv", [P, CT, 2])
        ve, rstd, tmp = sb("ao_ve", [P, CT]), sb("ao_rstd", [P, CT]), sb("ao_tmp", [P, CT])
        xn = sb("ao_xn", [P, 2, CT, D])
        hm = sb("ao_hm", [P, 2, CT, D])
        pT = ctx.enter_context(nc.psum_tensor("ao_pT", [P, KT, CH], F32))
        pY = ctx.enter_context(nc.psum_tensor("ao_pY", [P, CT, D], F32))

        loaded = arrivals("loaded", 48)
        turned, aT_ready, projected = sig("turned"), sig("aT_ready"), sig("projected")
        gated = sig("gated", 2)
        chain = sig("chain", LN_INCS)
        normed = sig("normed")
        modded = sig("modded", 2)
        stored = arrivals("stored", 48)

        def later(n):
            return not isinstance(n, int) or n >= 2

        def again(n):
            return not isinstance(n, int) or n >= 1

        def drive(eng, body):
            for n in range(2):
                body(n, n)
            with eng.Fori(1, NC // 2) as i:
                for p in range(2):
                    body(i * 2 + p, p)

        with nc.Block() as block:
            @block.sync
            def _(sp):
                def load(n, p):
                    if later(n):
                        modded.wait(sp, n - 2)
                    sp.dma_start(at[:, p], rows(att_d, n)).then_inc(loaded.sems[p], 16)
                    sp.dma_start(xt[:, p], rows(x, n)).then_inc(loaded.sems[p], 16)
                    src = mod_d[bass.ds(n // 2, 1), 2:5, :].to_broadcast([P, 3, D])
                    sp.dma_start(mrow[:, p], src).then_inc(loaded.sems[p], 16)

                def store(n, p):
                    gated.wait(sp, n)
                    sp.dma_start(rows(x1_d, n), x1[:, p]).then_inc(stored.sems[p], 16)
                    modded.wait(sp, n)
                    sp.dma_start(rows(lo_dst, n), hm[:, p, :, 0:P]).then_inc(stored.sems[p], 16)
                    sp.dma_start(padded(hi_dst, n, CH), hm[:, p, :, P:D]).then_inc(stored.sems[p], 16)

                load(0, 0)
                load(1, 1)
                store(0, 0)
                load(2, 0)
                with sp.Fori(0, NC // 2 - 2) as i:
                    for q in range(2):
                        store(i * 2 + 1 + q, 1 - q)
                        load(i * 2 + 3 + q, 1 - q)
                store(NC - 3, 1)
                load(NC - 1, 1)
                store(NC - 2, 0)
                store(NC - 1, 1)
                stored.wait(sp, NC - 2, 0)
                stored.wait(sp, NC - 1, 1)

            @block.tensor
            def _(pe):
                def body(n, p):
                    loaded.wait(pe, n, p)
                    if again(n):
                        aT_ready.wait(pe, n - 1)
                    for t in range(CT):
                        for k in range(KT):
                            last = nc.tensor.transpose(pT[:, k, t * P:(t + 1) * P],
                                                       at[:, p, t, k * P:(k + 1) * P], ident[:])
                    last.then_inc(turned.sem, 1)
                    aT_ready.wait(pe, n)
                    if again(n):
                        gated.wait(pe, n - 1, 1)
                    for t in range(CT):
                        for k in range(KT):
                            last = nc.tensor.matmul(pY[:, t, :], aT[:, k, t * P:(t + 1) * P], w["wo"][:, k, :],
                                                    start=(k == 0), stop=(k == KT - 1))
                    last.then_inc(projected.sem, 1)

                drive(pe, body)

            @block.scalar
            def _(act):
                def body(n, p):
                    turned.wait(act, n)
                    if again(n):
                        projected.wait(act, n - 1)
                    nc.scalar.copy(aT[:], pT[:]).then_inc(aT_ready.sem, 1)

                drive(act, body)

            @block.vector
            def _(dve):
                def body(n, p):
                    chain.begin()
                    loaded.wait(dve, n, p)
                    projected.wait(dve, n)
                    if later(n):
                        stored.wait(dve, n - 2, p)
                    gate = mrow[:, p, 0, :].unsqueeze(1).to_broadcast([P, CT, D])
                    nc.vector.tensor_tensor(x1[:, p], pY[:], gate, ALU.mult).then_inc(gated.sem, 1)
                    gated.wait(dve, n, 1)
                    nc.vector.tensor_tensor(x1[:, p], x1[:, p], xt[:, p], ALU.add).then_inc(gated.sem, 1)
                    gated.wait(dve, n)
                    layer_norm_stats(nc, dve, chain, n, x1[:, p], stats, mv, ve[:], rstd[:], tmp[:])
                    if later(n):
                        modded.wait(dve, n - 2, 1)
                    for t in range(CT):
                        last = nc.vector.tensor_scalar(xn[:, p, t, :], x1[:, p, t, :], mv[:, t, 0:1],
                                                       rstd[:, t:t + 1], ALU.subtract, ALU.mult)
                    last.then_inc(normed.sem, 1)

                drive(dve, body)

            @block.gpsimd
            def _(pool):
                def body(n, p):
                    normed.wait(pool, n)
                    for t_in, t_out, row, op in ((xn, xn, 2, ALU.mult), (xn, hm, 1, ALU.add)):
                        if row == 1:
                            modded.wait(pool, n, 1)
                            if later(n):
                                stored.wait(pool, n - 2, p)
                        nc.gpsimd.tensor_tensor(t_out[:, p], t_in[:, p],
                                                mrow[:, p, row, :].unsqueeze(1).to_broadcast([P, CT, D]),
                                                op).then_inc(modded.sem, 1)

                drive(pool, body)


def window_signals(nc, ctx):
    per = dict(
        x_turned=1, xT_ready=1,
        qk_done=1, v_done=1, v_ready=1,
        squared=1, chain=2 + RSQRT_INCS, scaled=1, rotated=4,
        q_turned=1, k_turned=1, q_ready=1, k_ready=2,
        scored=HEADS // 2, masked=HEADS // 2, exped=HEADS // 2, inverse=HEADS // 2, weighted=HEADS // 2,
        p_turned=HEADS // 2, pT_ready=HEADS // 2, summed=HEADS // 2, o_ready=1,
        projected=1, added=1,
    )
    signals = {name: Signal(ctx.enter_context(nc.semaphore("wa_" + name)), k) for name, k in per.items()}
    for name, k in dict(x_in=32, own_in=16, trig_in=16, mask_in=16, stored=32).items():
        signals[name] = Arrivals([ctx.enter_context(nc.semaphore(f"wa_{name}{p}")) for p in range(2)], k)
    return signals


def window_attention(nc, a, layer, ident, trig_d, src, dst, sg):
    TILES = B * NW
    PAIRS = HEADS // 2
    R = 4
    base = layer * TILES
    lo_s, hi_s = src
    lo_t, hi_t = dst

    s = sg

    with ExitStack() as ctx:
        def sb(name, shape, dt=F32):
            return ctx.enter_context(nc.sbuf_tensor(f"wa{layer}_{name}", shape, dt))

        def pb(name, shape):
            return ctx.enter_context(nc.psum_tensor(f"wa{layer}_{name}", shape, F32))

        wqkv = sb("wqkv", [P, KT, 3 * INNER])
        wo = sb("wo", [P, INNER // P, D])
        xs = sb("xs", [P, 2, 2, P])
        xo = sb("xo", [P, 2, P])
        xT = sb("xT", [P, KT, P])
        trig = sb("trig", [P, 2, 4, DH])
        mask = sb("mask", [P, 2, 2 * WIN])
        sq = sb("sq", [P, 2 * INNER])
        ss, rn, rt = sb("ss", [P, 2 * HEADS]), sb("rn", [P, 2 * HEADS]), sb("rt", [P, 2 * HEADS])
        qn = sb("qn", [P, 2, HEADS, DH])
        qa = sb("qa", [P, 2, HEADS, DH])
        qb = sb("qb", [P, 2, HEADS, DH])
        qT = sb("qT", [P, 2, PAIRS, P])
        kT = sb("kT", [P, R, PAIRS, 2, P])
        V = sb("V", [P, R, HEADS, DH])
        sm = sb("sm", [P, 2, 2, 2 * WIN])
        mn = sb("mn", [P, 2, HEADS])
        pr = sb("pr", [P, 2, 2, 2 * WIN])
        rs, ri = sb("rs", [P, 2, HEADS]), sb("ri", [P, 2, HEADS])
        pn = sb("pn", [P, 2, 2, 2 * WIN])
        pT = sb("pT", [P, 2, 2, 2, P])
        oT = sb("oT", [P, PAIRS, P])
        x2 = sb("x2", [P, 2, 2, P])
        gate = sb("gate", [P, PAIRS])
        pQK, pV, pM = pb("pQK", [P, 2, INNER]), pb("pV", [P, INNER]), pb("pM", [P, 512])
        pS, pP, pO = pb("pS", [P, 2, 512]), pb("pP", [P, 512]), pb("pO", [P, PAIRS, P])
        w_in = ctx.enter_context(nc.semaphore(f"wa{layer}_w_in"))
        zeroed = ctx.enter_context(nc.semaphore(f"wa{layer}_zeroed"))

        def g(n):
            return n + base

        def early(n, k):
            return isinstance(n, int) and n < k

        def drive(eng, body):
            for i in range(R):
                body(i, i, True, i > 0)
            with eng.Fori(1, TILES // R) as i:
                for r in range(R):
                    body(i * R + r, r, True, True)
            body(TILES, 0, False, True)

        with nc.Block() as block:
            @block.sync
            def _(sp):
                sp.dma_start(wqkv[:], a["L0_ffn_wqkv"][layer].rearrange("(k p) n -> p k n", p=P)).then_inc(w_in, 16)
                sp.dma_start(wo[:], a["L0_ffn_wo"][layer].rearrange("(k p) n -> p k n", p=P)).then_inc(w_in, 16)

                def load(n, p):
                    if not early(n, 2):
                        s["added"].wait(sp, g(n - 2))
                    b, t = n // NW, n % NW
                    flat = lo_s[bass.ds(b, 1), bass.ds(t * P, P), :].rearrange("b p c -> (b p) c")
                    sp.dma_start(xs[:, p, 0, :], flat).then_inc(s["x_in"].sems[p], 16)
                    flat = hi_s[bass.ds(b, 1), bass.ds(t * P, P), :].rearrange("b p c -> (b p) c")
                    sp.dma_start(xs[:, p, 1, :], flat).then_inc(s["x_in"].sems[p], 16)
                    flat = hi_s[bass.ds(b, 1), bass.ds(t * P + 1, P), :].rearrange("b p c -> (b p) c")
                    sp.dma_start(xo[:, p, :], flat).then_inc(s["own_in"].sems[p], 16)
                    flat = trig_d[layer, bass.ds(t, 1)].rearrange("w p c -> (w p) c")
                    sp.dma_start(trig[:, p].rearrange("p a c -> p (a c)"), flat).then_inc(s["trig_in"].sems[p], 16)
                    flat = a["mask"][bass.ds(t, 1)].rearrange("w p c -> (w p) c")
                    sp.dma_start(mask[:, p, :], flat).then_inc(s["mask_in"].sems[p], 16)

                def store(n, p):
                    s["added"].wait(sp, g(n))
                    b, t = n // NW, n % NW
                    flat = lo_t[bass.ds(b, 1), bass.ds(t * P, P), :].rearrange("b p c -> (b p) c")
                    sp.dma_start(flat, x2[:, p, 0, :]).then_inc(s["stored"].sems[p], 16)
                    flat = hi_t[bass.ds(b, 1), bass.ds(t * P + 1, P), :].rearrange("b p c -> (b p) c")
                    sp.dma_start(flat, x2[:, p, 1, :]).then_inc(s["stored"].sems[p], 16)

                load(0, 0)
                load(1, 1)
                with sp.Fori(0, TILES // 2 - 1) as i:
                    for p in range(2):
                        store(i * 2 + p, p)
                        load(i * 2 + 2 + p, p)
                store(TILES - 2, 0)
                store(TILES - 1, 1)
                s["stored"].wait(sp, g(TILES - 2), 0)
                s["stored"].wait(sp, g(TILES - 1), 1)

            @block.tensor
            def _(pe):
                def turn_x(n, p):
                    s["x_in"].wait(pe, g(n), p)
                    if not early(n, 1):
                        s["q_ready"].wait(pe, g(n - 1))
                    for k in range(KT):
                        last = nc.tensor.transpose(pM[:, k * P:(k + 1) * P], xs[:, p, k, :], ident[:])
                    last.then_inc(s["x_turned"].sem, 1)

                def project(n, j):
                    if j == 0:
                        if isinstance(n, int) and n == 0:
                            pe.wait_ge(w_in, 32)
                        s["xT_ready"].wait(pe, g(n))
                        if not early(n, 1):
                            s["scaled"].wait(pe, g(n - 1))
                    if j == 2 and not early(n, 1):
                        s["k_ready"].wait(pe, g(n - 1))
                    for k in range(KT):
                        out = pQK[:, j, :] if j < 2 else pV[:]
                        last = nc.tensor.matmul(out, xT[:, k, :], wqkv[:, k, j * INNER:(j + 1) * INNER],
                                                start=(k == 0), stop=(k == KT - 1))
                    if j == 1:
                        last.then_inc(s["qk_done"].sem, 1)
                    if j == 2:
                        last.then_inc(s["v_done"].sem, 1)

                def turn_qk(n, j):
                    if j == 0:
                        s["rotated"].wait(pe, g(n))
                        if not early(n, 1):
                            s["added"].wait(pe, g(n - 1))
                    else:
                        s["v_ready"].wait(pe, g(n))
                    dst = pM if j == 0 else pV
                    for hp in range(PAIRS):
                        last = nc.tensor.transpose(dst[:, hp * P:(hp + 1) * P],
                                                   qn[:, j, 2 * hp:2 * hp + 2, :].rearrange("p h c -> p (h c)"),
                                                   ident[:])
                    last.then_inc(s["q_turned" if j == 0 else "k_turned"].sem, 1)

                def scores(n, r, hp):
                    if hp == 0:
                        s["q_ready"].wait(pe, g(n))
                        s["k_ready"].wait(pe, g(n))
                        if isinstance(n, int) and n == 0:
                            pe.wait_ge(zeroed, 2)
                    if not (early(n, 1) and layer == 0 and hp < 2):
                        pe.wait_ge(s["masked"].sem, g(n) * PAIRS + hp - 1)
                    for hh in range(2):
                        for w, kr in enumerate(((r - 1) % R, r)):
                            at = hh * 2 * WIN + w * WIN
                            last = nc.tensor.matmul(pS[:, hp % 2, at:at + WIN], qT[:, r % 2, hp, :],
                                                    kT[:, kr, hp, hh, :], start=True, stop=True)
                    last.then_inc(s["scored"].sem, 1)

                def turn_p(n, hp):
                    s["weighted"].wait(pe, g(n), hp + 1)
                    if not (early(n, 1) and layer == 0 and hp == 0):
                        pe.wait_ge(s["pT_ready"].sem, g(n) * PAIRS + hp)
                    for hh in range(2):
                        for w in range(2):
                            at = (hh * 2 + w) * P
                            last = nc.tensor.transpose(pP[:, at:at + P], pn[:, hp % 2, hh, w * WIN:(w + 1) * WIN],
                                                       ident[:])
                    last.then_inc(s["p_turned"].sem, 1)

                def values(n, r, hp):
                    s["pT_ready"].wait(pe, g(n), hp + 1)
                    if hp == 0:
                        s["v_ready"].wait(pe, g(n))
                        if not early(n, 1):
                            s["o_ready"].wait(pe, g(n - 1))
                    for w, kr in enumerate(((r - 1) % R, r)):
                        for hh in range(2):
                            last = nc.tensor.matmul(pO[hh * DH:(hh + 1) * DH, hp, :], V[:, kr, 2 * hp + hh, :],
                                                    pT[:, hp % 2, hh, w, :], start=(w == 0), stop=(w == 1))
                    last.then_inc(s["summed"].sem, 1)

                def project_out(n):
                    s["o_ready"].wait(pe, g(n))
                    for hp in range(PAIRS):
                        last = nc.tensor.matmul(pM[:, 0:D], oT[:, hp, :], wo[:, hp, :],
                                                start=(hp == 0), stop=(hp == PAIRS - 1))
                    last.then_inc(s["projected"].sem, 1)

                def body(i, r, front, back):
                    n, q = i - 1, (r - 1) % R
                    if front:
                        turn_x(i, r % 2)
                    if back:
                        scores(n, q, 0)
                        scores(n, q, 1)
                    if front:
                        project(i, 0)
                        project(i, 1)
                    if back:
                        turn_p(n, 0)
                        scores(n, q, 2)
                    if front:
                        project(i, 2)
                    if back:
                        turn_p(n, 1)
                        values(n, q, 0)
                        scores(n, q, 3)
                        turn_p(n, 2)
                        values(n, q, 1)
                        turn_p(n, 3)
                        values(n, q, 2)
                        values(n, q, 3)
                        project_out(n)
                    if front:
                        turn_qk(i, 0)
                        turn_qk(i, 1)

                drive(pe, body)

            @block.scalar
            def _(act):
                def x_out(n):
                    s["x_turned"].wait(act, g(n))
                    if not early(n, 1):
                        s["v_done"].wait(act, g(n - 1))
                    nc.scalar.copy(xT[:].rearrange("p k t -> p (k t)"),
                                   pM[:, 0:KT * P]).then_inc(s["xT_ready"].sem, 1)

                def square(n):
                    s["qk_done"].wait(act, g(n))
                    if not early(n, 1):
                        s["chain"].wait(act, g(n - 1), 1)
                    nc.scalar.activation(sq[:].rearrange("p (a c) -> p a c", a=2), pQK[:],
                                         ACT.Square).then_inc(s["squared"].sem, 1)

                def v_out(n, r):
                    s["v_done"].wait(act, g(n))
                    if isinstance(n, int) and n == 0:
                        act.wait_ge(zeroed, 2)
                    if not early(n, R - 1):
                        s["summed"].wait(act, g(n - R + 1))
                    nc.scalar.copy(V[:, r].rearrange("p h c -> p (h c)"), pV[:]).then_inc(s["v_ready"].sem, 1)

                def qk_out(n, r):
                    s["q_turned"].wait(act, g(n))
                    if not early(n, 2):
                        s["scored"].wait(act, g(n - 2))
                    nc.scalar.copy(qT[:, r % 2].rearrange("p a t -> p (a t)"), pM[:]).then_inc(s["q_ready"].sem, 1)
                    s["k_turned"].wait(act, g(n))
                    if isinstance(n, int) and n == 0:
                        act.wait_ge(zeroed, 2)
                    if not early(n, R - 1):
                        s["scored"].wait(act, g(n - R + 1))
                    for hh in range(2):
                        at = hh * DH
                        nc.scalar.copy(kT[at:at + DH, r, :, hh, :],
                                       pV[at:at + DH, :].rearrange("p (a t) -> p a t", a=PAIRS))\
                            .then_inc(s["k_ready"].sem, 1)

                def exponentials(n, q, hp):
                    s["masked"].wait(act, g(n), hp + 1)
                    if not (early(n, 1) and layer == 0 and hp < 2):
                        act.wait_ge(s["weighted"].sem, g(n) * PAIRS + hp - 1)
                    for hh in range(2):
                        h = 2 * hp + hh
                        last = nc.scalar.activation(pr[:, hp % 2, hh, :], sm[:, hp % 2, hh, :], ACT.Exp,
                                                    bias=mn[:, q % 2, h:h + 1], scale=-1.0,
                                                    accum_out=rs[:, q % 2, h:h + 1])
                    last.then_inc(s["exped"].sem, 1)

                def p_out(n, hp):
                    s["p_turned"].wait(act, g(n), hp + 1)
                    if not (early(n, 1) and layer == 0 and hp < 2):
                        act.wait_ge(s["summed"].sem, g(n) * PAIRS + hp - 1)
                    nc.scalar.copy(pT[:, hp % 2].rearrange("p h w t -> p (h w t)"),
                                   pP[:]).then_inc(s["pT_ready"].sem, 1)

                def o_out(n):
                    s["summed"].wait(act, g(n))
                    if not early(n, 1):
                        s["projected"].wait(act, g(n - 1))
                    nc.scalar.copy(oT[:], pO[:]).then_inc(s["o_ready"].sem, 1)

                def body(i, r, front, back):
                    n, q = i - 1, (r - 1) % R
                    if front:
                        x_out(i)
                    if back:
                        exponentials(n, q, 0)
                        exponentials(n, q, 1)
                    if front:
                        square(i)
                    if back:
                        p_out(n, 0)
                        exponentials(n, q, 2)
                    if front:
                        v_out(i, r)
                    if back:
                        p_out(n, 1)
                        exponentials(n, q, 3)
                        p_out(n, 2)
                        p_out(n, 3)
                        o_out(n)
                    if front:
                        qk_out(i, r)

                drive(act, body)

            @block.gpsimd
            def _(pool):
                def weigh(n, q, hp):
                    s["inverse"].wait(pool, g(n), hp + 1)
                    s["exped"].wait(pool, g(n), hp + 1)
                    if not (early(n, 1) and layer == 0 and hp < 2):
                        pool.wait_ge(s["p_turned"].sem, g(n) * PAIRS + hp - 1)
                    inv = ri[:, q % 2, 2 * hp:2 * hp + 2].unsqueeze(2).to_broadcast([P, 2, 2 * WIN])
                    nc.gpsimd.tensor_tensor(pn[:, hp % 2], pr[:, hp % 2], inv, ALU.mult).then_inc(s["weighted"].sem, 1)

                def body(i, r, front, back):
                    if back:
                        for hp in range(PAIRS):
                            weigh(i - 1, (r - 1) % R, hp)

                drive(pool, body)

            @block.vector
            def _(dve):
                nc.vector.memset(kT[:], 0.0).then_inc(zeroed, 1)
                nc.vector.memset(V[:, R - 1], 0.0).then_inc(zeroed, 1)

                def masks(n, q, hp):
                    s["scored"].wait(dve, g(n), hp + 1)
                    if hp == 0:
                        s["mask_in"].wait(dve, g(n), q % 2)
                    if not (early(n, 1) and layer == 0 and hp < 2):
                        dve.wait_ge(s["exped"].sem, g(n) * PAIRS + hp - 1)
                    nc.vector.memset(gate[:, hp:hp + 1], 0.0)
                    for hh in range(2):
                        h = 2 * hp + hh
                        last = nc.vector.tensor_tensor_reduce(
                            out=sm[:, hp % 2, hh, :], in0=pS[:, hp % 2, hh * 2 * WIN:(hh + 1) * 2 * WIN],
                            in1=mask[:, q % 2, :], scale=1.0, scalar=MASKED, op0=ALU.add, op1=ALU.min,
                            accum_out=mn[:, q % 2, h:h + 1])
                    last.then_inc(s["masked"].sem, 1)

                def inverse(n, q, hp):
                    s["exped"].wait(dve, g(n), hp + 1)
                    nc.vector.reciprocal(ri[:, q % 2, 2 * hp:2 * hp + 2],
                                         rs[:, q % 2, 2 * hp:2 * hp + 2]).then_inc(s["inverse"].sem, 1)

                def norms(n):
                    c = s["chain"]
                    s["squared"].wait(dve, g(n))
                    c.begin()
                    c.step(nc.vector.tensor_reduce(ss[:], sq[:].rearrange("p (h c) -> p h c", c=DH), AX.X, ALU.add))
                    c.settle(dve, g(n))
                    c.step(nc.vector.tensor_scalar(ss[:], ss[:], NORM_FLOOR, None, ALU.max))
                    c.settle(dve, g(n))
                    rsqrt(nc, dve, c, g(n), ss[:], rn[:], rt[:])
                    c.settle(dve, g(n))

                def scale(n):
                    if not early(n, 1):
                        s["k_turned"].wait(dve, g(n - 1))
                    nc.vector.tensor_tensor(qa[:].rearrange("p a h c -> p (a h) c"),
                                            pQK[:].rearrange("p a (h c) -> p (a h) c", c=DH),
                                            rn[:].unsqueeze(2).to_broadcast([P, 2 * HEADS, DH]),
                                            ALU.mult).then_inc(s["scaled"].sem, 1)

                def rotate(n, p):
                    c = s["rotated"]
                    c.begin()
                    s["scaled"].wait(dve, g(n))
                    s["trig_in"].wait(dve, g(n), p)
                    hd = DH // 2
                    for half in range(2):
                        at, other = half * hd, hd - half * hd
                        c.step(nc.vector.tensor_tensor(
                            qb[:, :, :, at:at + hd], qa[:, :, :, other:other + hd],
                            trig[:, p, 2:4, at:at + hd].unsqueeze(2).to_broadcast([P, 2, HEADS, hd]), ALU.mult))
                    c.settle(dve, g(n))
                    c.step(nc.vector.tensor_tensor(
                        qa[:], qa[:], trig[:, p, 0:2, :].unsqueeze(2).to_broadcast([P, 2, HEADS, DH]), ALU.mult))
                    c.settle(dve, g(n))
                    c.step(nc.vector.tensor_tensor(qn[:], qa[:], qb[:], ALU.add))

                def add(n, p):
                    s["projected"].wait(dve, g(n))
                    s["own_in"].wait(dve, g(n), p)
                    s["x_in"].wait(dve, g(n), p)
                    if not early(n, 2):
                        s["stored"].wait(dve, g(n - 2), p)
                    nc.vector.tensor_tensor(x2[:, p, 0, :], pM[:, 0:P], xs[:, p, 0, :], ALU.add)
                    nc.vector.tensor_tensor(x2[:, p, 1, :], pM[:, P:D], xo[:, p, :],
                                            ALU.add).then_inc(s["added"].sem, 1)

                def body(i, r, front, back):
                    n, q = i - 1, (r - 1) % R
                    if back:
                        masks(n, q, 0)
                        masks(n, q, 1)
                        inverse(n, q, 0)
                        inverse(n, q, 1)
                    if front:
                        norms(i)
                    if back:
                        masks(n, q, 2)
                        inverse(n, q, 2)
                    if front:
                        scale(i)
                    if back:
                        masks(n, q, 3)
                    if front:
                        rotate(i, r % 2)
                    if back:
                        inverse(n, q, 3)
                        add(n, q % 2)

                drive(dve, body)


def ffn_signals(nc, ctx):
    per = dict(
        chain=LN_INCS, normed=1, biased=2, turned=1, hT_ready=2,
        gated=HB, lifted=HB, gelu=HB, mixed=HB, y_done=1, summed=1, scaled=1, final=1,
    )
    signals = {name: Signal(ctx.enter_context(nc.semaphore("ff_" + name)), k) for name, k in per.items()}
    for name, k in dict(x_in=48, last_in=32, stored=32).items():
        signals[name] = Arrivals([ctx.enter_context(nc.semaphore(f"ff_{name}{p}")) for p in range(2)], k)
    return signals


def feed_forward(nc, a, layer, ident, src, dst, x1_d, mod_d, out, s):
    base = layer * NC
    lo_s, hi_s = src
    final = dst is None

    with ExitStack() as ctx:
        def sb(name, shape, dt=F32):
            return ctx.enter_context(nc.sbuf_tensor(f"ff{layer}_{name}", shape, dt))

        w1 = sb("w1", [P, KT, 2, HB * P])
        w2 = sb("w2", [P, HB, D])
        b1 = sb("b1", [P, 2, HB])
        b2 = sb("b2", [P, D])
        lg, lb = sb("lg", [P, KT]), sb("lb", [P, KT])
        hx = sb("hx", [P, 2, CT, D])
        xo = sb("xo", [P, 2, CT, P])
        xb = sb("xb", [P, 2, CT, D])
        stats, mv = sb("stats", [P, CT, 6]), sb("mv", [P, CT, 2])
        ve, rstd, tmp = sb("ve", [P, CT]), sb("rstd", [P, CT]), sb("tmp", [P, CT])
        hn = sb("hn", [P, 2, CT, D])
        hT = sb("hT", [P, 2, KT, CH])
        gl = sb("gl", [P, 2, CH])
        u = sb("u", [P, HB, CH])
        y = sb("y", [P, 2, CT, D])
        if final:
            x1 = sb("x1", [P, 2, CT, D])
            gb = sb("gb", [P, 2, D])
            yg = sb("yg", [P, CT, D])
            yo = sb("yo", [P, 2, CT, D])
        pH = ctx.enter_context(nc.psum_tensor(f"ff{layer}_pH", [P, KT, CH], F32))
        pG = ctx.enter_context(nc.psum_tensor(f"ff{layer}_pG", [P, 2, CH], F32))
        pA = ctx.enter_context(nc.psum_tensor(f"ff{layer}_pA", [P, 2, CH], F32))
        pY = ctx.enter_context(nc.psum_tensor(f"ff{layer}_pY", [P, CT, D], F32))
        w_in = ctx.enter_context(nc.semaphore(f"ff{layer}_w_in"))
        zeroed = ctx.enter_context(nc.semaphore(f"ff{layer}_zeroed"))
        full = (HB - 1) * P
        LOADS = 10

        def g(n):
            return n + base

        def early(n, k):
            return isinstance(n, int) and n < k

        def drive(eng, body):
            for n in range(2):
                body(n, n)
            with eng.Fori(1, NC // 2) as i:
                for p in range(2):
                    body(i * 2 + p, p)

        with nc.Block() as block:
            @block.sync
            def _(sp):
                sp.wait_ge(zeroed, 3)
                loads = [
                    (w2[:, 0:HB - 1, :], a["L0_ffn_w2"][layer, 0:full].rearrange("(k p) n -> p k n", p=P)),
                    (w2[0:HL, HB - 1, :], a["L0_ffn_w2"][layer, full:HID]),
                    (b2[:], a["L0_ffn_b2"][layer:layer + 1, :].to_broadcast([P, D])),
                ]
                for half in range(2):
                    loads.append((w1[:, :, half, 0:HID],
                                  a["L0_ffn_w1"][layer, :, half * HID:(half + 1) * HID]
                                  .rearrange("(k p) n -> p k n", p=P)))
                for d_, s_ in loads:
                    sp.dma_start(d_, s_).then_inc(w_in, 16)
                with nc.allow_non_contiguous_dma(reason="short vectors, once per layer"):
                    for half in range(2):
                        row = a["L0_ffn_b1"][layer, half * HID:(half + 1) * HID]
                        sp.dma_start(b1[:, half, 0:HB - 1],
                                     row[0:full].rearrange("(k p) -> p k", p=P)).then_inc(w_in, 16)
                        sp.dma_start(b1[0:HL, half, HB - 1:HB],
                                     row[full:HID].rearrange("(p k) -> p k", k=1)).then_inc(w_in, 16)
                    sp.dma_start(lg[:], a["L0_ffn_ln_g"][layer].rearrange("(k p) -> p k", p=P)).then_inc(w_in, 16)
                    sp.dma_start(lb[:], a["L0_ffn_ln_b"][layer].rearrange("(k p) -> p k", p=P)).then_inc(w_in, 16)

                def load(n, p):
                    if not early(n, 2):
                        s["normed"].wait(sp, g(n - 2))
                        if final:
                            s["final"].wait(sp, n - 2)
                        else:
                            s["biased"].wait(sp, g(n - 2))
                    sp.dma_start(hx[:, p, :, 0:P], rows(lo_s, n)).then_inc(s["x_in"].sems[p], 16)
                    sp.dma_start(hx[:, p, :, P:D], shifted(hi_s, n, CH)).then_inc(s["x_in"].sems[p], 16)
                    sp.dma_start(xo[:, p], padded(hi_s, n, CH)).then_inc(s["x_in"].sems[p], 16)
                    if final:
                        sp.dma_start(x1[:, p], rows(x1_d, n)).then_inc(s["last_in"].sems[p], 16)
                        src_ = mod_d[bass.ds(n // 2, 1), 5, :].to_broadcast([P, D])
                        sp.dma_start(gb[:, p, :], src_).then_inc(s["last_in"].sems[p], 16)

                def store(n, p):
                    if final:
                        s["final"].wait(sp, n)
                        for half in range(2):
                            sp.dma_start(rows(out, n)[:, 2 * half:2 * half + 2],
                                         yo[:, p, 2 * half:2 * half + 2]).then_inc(s["stored"].sems[p], 16)
                    else:
                        s["summed"].wait(sp, g(n))
                        sp.dma_start(rows(dst[0], n), y[:, p, :, 0:P]).then_inc(s["stored"].sems[p], 16)
                        sp.dma_start(padded(dst[1], n, CH), y[:, p, :, P:D]).then_inc(s["stored"].sems[p], 16)

                load(0, 0)
                load(1, 1)
                store(0, 0)
                load(2, 0)
                with sp.Fori(0, NC // 2 - 2) as i:
                    for q in range(2):
                        store(i * 2 + 1 + q, 1 - q)
                        load(i * 2 + 3 + q, 1 - q)
                store(NC - 3, 1)
                load(NC - 1, 1)
                store(NC - 2, 0)
                store(NC - 1, 1)
                s["stored"].wait(sp, g(NC - 2), 0)
                s["stored"].wait(sp, g(NC - 1), 1)

            @block.vector
            def _(dve):
                nc.vector.memset(w1[:, :, :, full:HB * P], 0.0).then_inc(zeroed, 1)
                nc.vector.memset(w2[:, HB - 1, :], 0.0).then_inc(zeroed, 1)
                nc.vector.memset(b1[:], 0.0).then_inc(zeroed, 1)

                def norm(n, p):
                    c = s["chain"]
                    c.begin()
                    s["x_in"].wait(dve, g(n), p)
                    layer_norm_stats(nc, dve, c, g(n), hx[:, p], stats, mv, ve[:], rstd[:], tmp[:])
                    if not early(n, 2):
                        s["turned"].wait(dve, g(n - 2))
                    for t in range(CT):
                        last = nc.vector.tensor_scalar(hn[:, p, t, :], hx[:, p, t, :], mv[:, t, 0:1],
                                                       rstd[:, t:t + 1], ALU.subtract, ALU.mult)
                    last.then_inc(s["normed"].sem, 1)

                def mix(n, p):
                    if isinstance(n, int) and n == 0:
                        dve.wait_ge(w_in, 16 * 11)
                    for j in range(HB):
                        s["gelu"].wait(dve, g(n), j + 1)
                        s["lifted"].wait(dve, g(n), j + 1)
                        if j == 0 and not early(n, 1):
                            s["y_done"].wait(dve, g(n - 1))
                        nc.vector.scalar_tensor_tensor(out=u[:, j, :], in0=pA[:, j % 2, :], scalar=b1[:, 0, j:j + 1],
                                                       in1=gl[:, j % 2, :], op0=ALU.add,
                                                       op1=ALU.mult).then_inc(s["mixed"].sem, 1)

                def finish(n, p):
                    s["y_done"].wait(dve, g(n))
                    s["biased"].wait(dve, g(n))
                    if not early(n, 2):
                        if final:
                            s["final"].wait(dve, n - 2)
                        else:
                            s["stored"].wait(dve, g(n - 2), p)
                    nc.vector.tensor_tensor(y[:, p], pY[:], xb[:, p], ALU.add).then_inc(s["summed"].sem, 1)

                norm(0, 0)
                for n in range(2):
                    norm(n + 1, (n + 1) % 2)
                    mix(n, n)
                    finish(n, n)
                with dve.Fori(0, NC // 2 - 2) as i:
                    for p in range(2):
                        norm(i * 2 + 3 + p, 1 - p)
                        mix(i * 2 + 2 + p, p)
                        finish(i * 2 + 2 + p, p)
                norm(NC - 1, 1)
                for n in (NC - 2, NC - 1):
                    mix(n, n % 2)
                    finish(n, n % 2)

            @block.gpsimd
            def _(pool):
                pool.wait_ge(w_in, 16 * 11)

                def body(n, p):
                    s["x_in"].wait(pool, g(n), p)
                    if not early(n, 2):
                        s["summed"].wait(pool, g(n - 2))
                    for half, x in ((0, hx[:, p, :, 0:P]), (1, xo[:, p])):
                        nc.gpsimd.tensor_tensor(xb[:, p, :, half * P:(half + 1) * P], x,
                                                b2[:, half * P:(half + 1) * P].unsqueeze(1).to_broadcast([P, CT, P]),
                                                ALU.add).then_inc(s["biased"].sem, 1)
                    if final:
                        s["summed"].wait(pool, g(n))
                        s["last_in"].wait(pool, n, p)
                        if not early(n, 1):
                            s["final"].wait(pool, n - 1)
                        nc.gpsimd.tensor_tensor(yg[:], y[:, p], gb[:, p, :].unsqueeze(1).to_broadcast([P, CT, D]),
                                                ALU.mult).then_inc(s["scaled"].sem, 1)
                        s["scaled"].wait(pool, n)
                        if not early(n, 2):
                            s["stored"].wait(pool, g(n - 2), p)
                        nc.gpsimd.tensor_tensor(yo[:, p], yg[:], x1[:, p], ALU.add).then_inc(s["final"].sem, 1)

                drive(pool, body)

            @block.tensor
            def _(pe):
                pe.wait_ge(w_in, 16 * 11)

                def turn(n, p):
                    s["normed"].wait(pe, g(n))
                    if not early(n, 1):
                        s["hT_ready"].wait(pe, g(n - 1))
                    for t in range(CT):
                        for k in range(KT):
                            last = nc.tensor.transpose(pH[:, k, t * P:(t + 1) * P],
                                                       hn[:, p, t, k * P:(k + 1) * P], ident[:])
                    last.then_inc(s["turned"].sem, 1)

                def up(n, p):
                    s["hT_ready"].wait(pe, g(n))
                    for j in range(HB):
                        for half, ps, done, freed in ((1, pG, "gated", "gelu"), (0, pA, "lifted", "mixed")):
                            if not (early(n, 1) and layer == 0 and j < 2):
                                pe.wait_ge(s[freed].sem, g(n) * HB + j - 1)
                            for k in range(KT):
                                last = nc.tensor.matmul(ps[:, j % 2, :], w1[:, k, half, j * P:(j + 1) * P],
                                                        hT[:, p, k, :], start=(k == 0), stop=(k == KT - 1))
                            last.then_inc(s[done].sem, 1)

                def down(n, p):
                    s["mixed"].wait(pe, g(n))
                    if not early(n, 1):
                        s["summed"].wait(pe, g(n - 1))
                    for t in range(CT):
                        for j in range(HB):
                            last = nc.tensor.matmul(pY[:, t, :], u[:, j, t * P:(t + 1) * P], w2[:, j, :],
                                                    start=(j == 0), stop=(j == HB - 1))
                    last.then_inc(s["y_done"].sem, 1)

                turn(0, 0)
                for n in range(2):
                    up(n, n)
                    turn(n + 1, (n + 1) % 2)
                    down(n, n)
                with pe.Fori(0, NC // 2 - 2) as i:
                    for p in range(2):
                        up(i * 2 + 2 + p, p)
                        turn(i * 2 + 3 + p, 1 - p)
                        down(i * 2 + 2 + p, p)
                up(NC - 2, 0)
                turn(NC - 1, 1)
                down(NC - 2, 0)
                up(NC - 1, 1)
                down(NC - 1, 1)

            @block.scalar
            def _(act):
                act.wait_ge(w_in, 16 * 11)

                def h_out(n, p):
                    s["turned"].wait(act, g(n))
                    if not early(n, 2):
                        s["lifted"].wait(act, g(n - 2))
                    for k in range(KT):
                        nc.scalar.activation(hT[:, p, k, :], pH[:, k, :], ACT.Identity, bias=lb[:, k:k + 1],
                                             scale=lg[:, k:k + 1]).then_inc(s["hT_ready"].sem, 1)

                def gelus(n, p):
                    for j in range(HB):
                        s["gated"].wait(act, g(n), j + 1)
                        if not (early(n, 1) and layer == 0 and j < 2):
                            act.wait_ge(s["mixed"].sem, g(n) * HB + j - 1)
                        nc.scalar.activation(gl[:, j % 2, :], pG[:, j % 2, :], ACT.Gelu,
                                             bias=b1[:, 1, j:j + 1]).then_inc(s["gelu"].sem, 1)

                h_out(0, 0)
                for n in range(2):
                    gelus(n, n)
                    h_out(n + 1, (n + 1) % 2)
                with act.Fori(0, NC // 2 - 2) as i:
                    for p in range(2):
                        gelus(i * 2 + 2 + p, p)
                        h_out(i * 2 + 3 + p, 1 - p)
                gelus(NC - 2, 0)
                h_out(NC - 1, 1)
                gelus(NC - 1, 1)


_INS = ["L0_attn_x", "L0_attn_wq", "L0_attn_wk_a", "L0_attn_wk_b", "L0_attn_wv_a", "L0_attn_wv_b", "L0_attn_wo",
        "L0_ffn_wqkv", "L0_ffn_q_scale", "L0_ffn_k_scale", "L0_ffn_wo", "L0_ffn_ln_g", "L0_ffn_ln_b", "L0_ffn_w1",
        "L0_ffn_b1", "L0_ffn_w2", "L0_ffn_b2", "L0_c", "L0_wmod"]


def kernel(**inputs):
    import concourse.bacc as bacc
    from concourse.bass_utils import run_bass_kernel_spmd

    nc = bacc.Bacc("TRN2", target_bir_lowering=False, num_devices=1)
    given = {name: np.ascontiguousarray(inputs[name]) for name in _INS}
    given.update(constants())
    arrays, args = {}, {}
    for name, array in given.items():
        arrays[f"in_{name}"] = array
        args[name] = nc.dram_tensor(f"in_{name}", array.shape, mybir.dt.from_np(array.dtype),
                                    kind="ExternalInput").ap()
    out = nc.dram_tensor("out", (B, N, D), F32, kind="ExternalOutput").ap()
    build(nc, args, out)
    r = run_bass_kernel_spmd(nc, [arrays], core_ids=[0])
    return r.results[0]["out"]
```

```python
from contextlib import ExitStack

import numpy as np

import concourse.bass as bass
from concourse import mybir

ALU = mybir.AluOpType
ACT = mybir.ActivationFunctionType
AX = mybir.AxisListType
F32 = mybir.dt.float32
BF16 = mybir.dt.bfloat16
I32 = mybir.dt.int32

P = 128
B, N, D = 8, 1024, 256
KT = D // P
NH, HD = 16, 16
LAT = 64
DEPTH, HEADS, DH = 2, 8, 64
WIN = 128
NW = N // WIN
INNER = HEADS * DH
HID = D * 4 * 2 // 3
HB = -(-HID // P)
HL = HID - (HB - 1) * P
QK_SCALE = 8.0
LN_EPS = 1e-5
NORM_FLOOR = 1e-24
CT = 4
CH = CT * P
NC = B * N // CH
MASKED = 3.0e38
GH = 4
NG = NH // GH
GROUPS = B * NG
Q_PARTS = (0, 1, 2, 0, 1, 0)
K_PARTS = (0, 0, 0, 1, 1, 2)
SROWS = len(Q_PARTS) * HD
RSQRT_SEED = 1597463007.0
RSQRT_STEPS = 3
RSQRT_INCS = 1 + 3 * RSQRT_STEPS
WIN_BUFS = 4


class Signal:

    def __init__(self, sem, per=1):
        self.sem, self.per, self.k = sem, per, 0

    def upto(self, n, c=None):
        return n * self.per + (self.per if c is None else c)

    def begin(self):
        self.k = 0

    def counted(self):
        self.k += 1
        return self.sem

    def so_far(self, n):
        return n * self.per + self.k


def rsqrt_step(nc, k, x, y, t):
    if k == 0:
        return nc.vector.tensor_scalar(y.bitcast(I32), x.bitcast(I32), -0.5, RSQRT_SEED, ALU.mult, ALU.add)
    if k % 3 == 1:
        return nc.vector.scalar_tensor_tensor(out=t, in0=y, scalar=-0.5, in1=y, op0=ALU.mult, op1=ALU.mult)
    if k % 3 == 2:
        return nc.vector.tensor_tensor(t, t, x, ALU.mult)
    return nc.vector.scalar_tensor_tensor(out=y, in0=t, scalar=1.5, in1=y, op0=ALU.add, op1=ALU.mult)


class Arrivals:

    def __init__(self, sems, per):
        self.sems, self.per = sems, per

    def upto(self, n):
        return n // len(self.sems) * self.per + self.per



def constants():
    f = np.float32
    ident = np.eye(P, dtype=f)
    inv = f(1.0) / f(10000.0) ** (np.arange(0, HD, 2, dtype=f) / f(HD))
    ang = np.arange(NH, dtype=f)[:, None] * inv[None, :]
    rope = np.stack([np.cos(ang).reshape(-1), np.sin(ang).reshape(-1)]).astype(f)
    half = np.arange(0, DH, 2, dtype=f)
    inv2 = f(1.0) / f(10000.0) ** (half / f(DH))
    t = np.arange(N, dtype=f)
    fr = t[:, None] * inv2[None, :]
    fr = np.concatenate([fr, fr], -1)
    base = (half + f(0.4 * DH)) / f(1.4 * DH)
    power = (t - f(N // 2)) / f(WIN // 2)
    xs = base[None, :] ** power[:, None]
    xs = np.concatenate([xs, xs], -1)
    sgn = np.concatenate([-np.ones(DH // 2, f), np.ones(DH // 2, f)])
    c, s = np.cos(fr), np.sin(fr) * sgn
    trig = np.concatenate([c * xs * f(-QK_SCALE), c / xs, s * xs * f(-QK_SCALE), s / xs], -1).astype(f)
    trig = trig.reshape(NW, P, 4 * DH)
    i, j = np.arange(P)[:, None], np.arange(P)[None, :]
    own = np.where(j <= i, 0.0, MASKED)
    prev = np.where(j >= i, 0.0, MASKED)
    mask = np.stack([np.concatenate([prev if w else np.full((P, P), MASKED), own], 1) for w in range(2)])
    return {"ident": ident, "rope": rope, "trig": trig, "mask": mask.astype(f)}


def build(nc, a, out):
    with ExitStack() as ctx:
        def dram(name, shape, dt=F32):
            return nc.dram_tensor(name, shape, dt, kind="Internal").ap()

        mod_d = dram("mod_d", [B, 6, D])
        parts_d = dram("parts_d", [2, 3, D, B, N], BF16)
        v_d = dram("v_d", [B, N, NH * 2 * HD])
        att_d = dram("att_d", [B, N, D])
        x1_d = dram("x1_d", [B, N, D])
        lo_d = [dram(f"lo{s}_d", [B, N, P]) for s in range(2 * DEPTH)]
        hi_d = [dram(f"hi{s}_d", [B, 1 + N, P]) for s in range(2 * DEPTH)]
        trig_d = dram("trig_d", [DEPTH, NW, P, 4 * DH])

        ident = ctx.enter_context(nc.sbuf_tensor("ident", [P, P], F32))
        identb = ctx.enter_context(nc.sbuf_tensor("identb", [P, P], BF16))
        with ExitStack() as first:
            w = {
                "wq": first.enter_context(nc.sbuf_tensor("wqT", [P, KT, D], F32)),
                "wa": first.enter_context(nc.sbuf_tensor("waT", [P, KT, P], F32)),
                "wkb": first.enter_context(nc.sbuf_tensor("wkbT", [P, D], F32)),
                "wvb": first.enter_context(nc.sbuf_tensor("wvbT", [P, D], F32)),
                "wo": first.enter_context(nc.sbuf_tensor("woT", [P, KT, D], F32)),
            }
            setup(nc, a, ident, identb, w, mod_d, trig_d, hi_d)
            projections(nc, a["L0_attn_x"], ident, w, mod_d, parts_d, v_d)
            full_attention(nc, ident, identb, parts_d, v_d, att_d)
            attention_out(nc, a["L0_attn_x"], ident, w, mod_d, att_d, x1_d, lo_d[0], hi_d[0])
        window_sems = ExitStack()
        with window_sems:
            ws = window_signals(nc, window_sems)
            fs = ffn_signals(nc, window_sems)
            for layer in range(DEPTH):
                s = 2 * layer
                window_attention(nc, a, layer, ident, trig_d, (lo_d[s], hi_d[s]), (lo_d[s + 1], hi_d[s + 1]), ws)
                last = layer == DEPTH - 1
                dst = None if last else (lo_d[s + 2], hi_d[s + 2])
                feed_forward(nc, a, layer, ident, (lo_d[s + 1], hi_d[s + 1]), dst, x1_d, mod_d, out, fs)


def rows(x, n):
    flat = x.rearrange("b n c -> (b n) c").rearrange("(q t p) c -> q p t c", p=P, t=CT)
    return flat[bass.ds(n, 1)].rearrange("q p t c -> (q p) t c")


def shifted(x, n, unit):
    per = N // unit
    flat = x[bass.ds(n // per, 1), bass.ds((n % per) * unit, unit), :]
    return flat.rearrange("b (t p) c -> p (b t) c", p=P)


def padded(x, n, unit):
    per = N // unit
    flat = x[bass.ds(n // per, 1), bass.ds((n % per) * unit + 1, unit), :]
    return flat.rearrange("b (t p) c -> p (b t) c", p=P)


def setup(nc, a, ident, identb, w, mod_d, trig_d, hi_d):
    with ExitStack() as ctx:
        def sb(name, shape, dt=F32):
            return ctx.enter_context(nc.sbuf_tensor(name, shape, dt))

        def sem(name):
            return ctx.enter_context(nc.semaphore(name))

        wq_r = sb("wq_r", [P, KT, D])
        wo_r = sb("wo_r", [P, KT, D])
        wa_r = sb("wa_r", [P, D])
        wb_r = sb("wb_r", [P, KT, P])
        rope = sb("rope_b", [P, 2, P])
        ropeq = sb("rope_q", [P, 2, P])
        ta, tb = sb("rope_ta", [P, KT, P]), sb("rope_tb", [P, KT, P])
        cs = sb("c_rows", [B, D])
        ce = sb("c_exp", [B, D])
        cT = sb("c_T", [P, KT, B])
        wmod = sb("wmod_sb", [P, KT, 6 * D])
        mods = sb("mods", [B, 6, D])
        ga, gs = sb("guard_a", [B, 2, D]), sb("guard_s", [B, 2, D])
        trig = sb("trig_base", [P, NW, 4 * DH])
        qks = sb("qk_scales", [P, DEPTH, 4 * DH])
        trl = sb("trig_scaled", [P, DEPTH, NW, 4 * DH])
        zrow = sb("zero_rows", [B, P])
        ps = [ctx.enter_context(nc.psum_tensor(f"ps_set{i}", [P, 512], F32)) for i in range(8)]
        loaded, turned, steps, silu, stored = (sem("set_loaded"), sem("set_turned"), sem("set_steps"),
                                               sem("set_silu"), sem("set_stored"))
        small, modm = sem("set_small"), sem("set_mod")
        n_loads = [0]

        with nc.Block() as block:
            @block.sync
            def _(sp):
                def load(dst, src):
                    sp.dma_start(dst, src).then_inc(loaded, 16)
                    n_loads[0] += 16

                load(ident[:], a["ident"])
                load(cs[:], a["L0_c"])
                load(wmod[:], a["L0_wmod"].rearrange("(k p) n -> p k n", p=P))
                load(wq_r[:], a["L0_attn_wq"].rearrange("(m p) c -> p m c", p=P))
                load(wo_r[:], a["L0_attn_wo"].rearrange("(m p) c -> p m c", p=P))
                load(wa_r[0:LAT, :], a["L0_attn_wk_a"])
                load(wa_r[LAT:P, :], a["L0_attn_wv_a"])
                load(wb_r[:, :, 0:LAT], a["L0_attn_wk_b"].rearrange("(m p) c -> p m c", p=P))
                load(wb_r[:, :, LAT:P], a["L0_attn_wv_b"].rearrange("(m p) c -> p m c", p=P))
                load(rope[:], a["rope"].rearrange("(o t) i -> o t i", o=1).to_broadcast([P, 2, P]))
                load(trig[:], a["trig"].rearrange("w p c -> p w c"))
                hd = DH // 2
                for layer in range(DEPTH):
                    for which, name in enumerate(("L0_ffn_q_scale", "L0_ffn_k_scale")):
                        src = a[name][layer:layer + 1, :]
                        at = which * DH
                        load(qks[:, layer, at:at + DH], src.to_broadcast([P, DH]))
                        at += 2 * DH
                        load(qks[:, layer, at:at + hd], src[:, hd:DH].to_broadcast([P, hd]))
                        load(qks[:, layer, at + hd:at + DH], src[:, 0:hd].to_broadcast([P, hd]))
                sp.wait_ge(small, 1)
                for h in hi_d:
                    sp.dma_start(h[:, 0, :], zrow[:]).then_inc(stored, 16)
                sp.wait_ge(small, 2 + DEPTH)
                sp.dma_start(trig_d.rearrange("l w p c -> p (l w) c"),
                             trl[:].rearrange("p l w c -> p (l w) c")).then_inc(stored, 16)
                sp.wait_ge(modm, 1)
                sp.dma_start(mod_d, mods[:]).then_inc(stored, 16)
                sp.wait_ge(stored, 16 * (len(hi_d) + 2))

            total = n_loads[0]

            @block.scalar
            def _(act):
                act.wait_ge(loaded, total)
                nc.scalar.activation(ce[:], cs[:], ACT.Exp, scale=-1.0).then_inc(silu, 1)

            @block.tensor
            def _(pe):
                pe.wait_ge(loaded, total)
                for k in range(KT):
                    for m in range(KT):
                        nc.tensor.transpose(ps[0][:, k * D + m * P:k * D + (m + 1) * P],
                                            wq_r[:, m, k * P:(k + 1) * P], ident[:])
                        nc.tensor.transpose(ps[1][:, k * D + m * P:k * D + (m + 1) * P],
                                            wo_r[:, m, k * P:(k + 1) * P], ident[:])
                    nc.tensor.transpose(ps[2][:, k * P:(k + 1) * P], wa_r[:, k * P:(k + 1) * P], ident[:])
                    last = nc.tensor.transpose(ps[3][:, k * P:(k + 1) * P], wb_r[:, k, :], ident[:])
                last.then_inc(turned, 1)
                pe.wait_ge(silu, 2)
                for k in range(KT):
                    last = nc.tensor.transpose(ps[4][:, k * B:(k + 1) * B], cs[:, k * P:(k + 1) * P],
                                               ident[0:B, 0:B])
                last.then_inc(turned, 1)
                pe.wait_ge(silu, 3)
                for j in range(3):
                    for k in range(KT):
                        last = nc.tensor.matmul(ps[5 + j][0:B, :], cT[:, k, :], wmod[:, k, j * 512:(j + 1) * 512],
                                                start=(k == 0), stop=(k == KT - 1))
                last.then_inc(turned, 1)

            @block.vector
            def _(dve):
                count = [0]

                def link(ins):
                    ins.then_inc(steps, 1)
                    count[0] += 1
                    dve.wait_ge(steps, count[0])

                link(nc.vector.memset(w["wkb"][:], 0.0))
                link(nc.vector.memset(w["wvb"][:], 0.0))
                nc.vector.memset(zrow[:], 0.0).then_inc(small, 1)
                dve.wait_ge(loaded, total)
                nc.vector.tensor_copy(identb[:], ident[:]).then_inc(small, 1)
                for layer in range(DEPTH):
                    nc.vector.tensor_tensor(trl[:, layer], trig[:],
                                            qks[:, layer, :].unsqueeze(1).to_broadcast([P, NW, 4 * DH]),
                                            ALU.mult).then_inc(small, 1)
                dve.wait_ge(silu, 1)
                link(nc.vector.tensor_scalar(ce[:], ce[:], 1.0, None, ALU.add))
                link(nc.vector.reciprocal(ce[:], ce[:]))
                nc.vector.tensor_tensor(cs[:], cs[:], ce[:], ALU.mult).then_inc(silu, 1)
                dve.wait_ge(turned, 2)
                nc.vector.tensor_copy(cT[:], ps[4][:, 0:KT * B].rearrange("p (k b) -> p k b", k=KT)).then_inc(silu, 1)
                link(nc.vector.tensor_scalar(ropeq[:], rope[:], float(HD) ** -0.5, None, ALU.mult))

                def rotate(dst, src, table, k):
                    cos = table[:, 0, :].unsqueeze(1).to_broadcast([table.shape[0], k, P])
                    sin = table[:, 1, :].unsqueeze(1).to_broadcast([table.shape[0], k, P])
                    pa, pb = ta[0:table.shape[0], 0:k, :], tb[0:table.shape[0], 0:k, :]
                    link(nc.vector.tensor_tensor(pa, src[:, :, :, 0], cos, ALU.mult))
                    link(nc.vector.tensor_tensor(pb, src[:, :, :, 1], sin, ALU.mult))
                    link(nc.vector.tensor_tensor(dst[:, :, :, 0], pa, pb, ALU.subtract))
                    link(nc.vector.tensor_tensor(pa, src[:, :, :, 0], sin, ALU.mult))
                    link(nc.vector.tensor_tensor(pb, src[:, :, :, 1], cos, ALU.mult))
                    link(nc.vector.tensor_tensor(dst[:, :, :, 1], pa, pb, ALU.add))

                rotate(w["wq"][:].rearrange("p k (i e) -> p k i e", e=2),
                       ps[0][:].rearrange("p (k i e) -> p k i e", k=KT, e=2), ropeq, KT)
                rotate(w["wkb"][0:LAT, :].rearrange("p (k i e) -> p k i e", k=1, e=2),
                       ps[3][0:LAT, 0:D].rearrange("p (k i e) -> p k i e", k=1, e=2), rope[0:LAT], 1)
                link(nc.vector.tensor_copy(w["wvb"][LAT:P, :], ps[3][LAT:P, 0:D]))
                link(nc.vector.tensor_copy(w["wo"][:].rearrange("p k n -> p (k n)"), ps[1][:]))
                link(nc.vector.tensor_copy(w["wa"][:].rearrange("p k n -> p (k n)"), ps[2][:, 0:D]))
                dve.wait_ge(turned, 3)
                for j in range(3):
                    link(nc.vector.tensor_copy(mods[:, 2 * j:2 * j + 2, :],
                                               ps[5 + j][0:B, :].rearrange("p (k n) -> p k n", k=2)))
                scale, gate = mods[:, 1:6:3, :], mods[:, 2:6:3, :]
                link(nc.vector.tensor_scalar(scale, scale, 1.0, None, ALU.add))
                link(nc.vector.tensor_scalar(gs[:], gate, 0.0, 2.0, ALU.is_ge, ALU.mult))
                link(nc.vector.tensor_scalar(gs[:], gs[:], -1.0, None, ALU.add))
                link(nc.vector.tensor_scalar(ga[:], gate, -1.0, None, ALU.mult))
                link(nc.vector.tensor_tensor(ga[:], ga[:], gate, ALU.max))
                link(nc.vector.tensor_scalar(ga[:], ga[:], 0.25, None, ALU.max))
                nc.vector.tensor_tensor(gate, ga[:], gs[:], ALU.mult).then_inc(modm, 1)


def layer_norm_steps(nc, dve, chain, n, steps, x, stats, mv, ve, rstd, tmp):
    for k in steps:
        if k > 0:
            dve.wait_ge(chain.sem, chain.upto(n, k))
        if k == 0:
            for t in range(x.shape[1]):
                last = nc.vector.bn_stats(stats[:, t, :], x[:, t, :])
        elif k == 1:
            nc.vector.memset(tmp, 0.0)
            for t in range(x.shape[1]):
                last = nc.vector.bn_aggr(mv[:, t, :], stats[:, t, :])
        elif k == 2:
            last = nc.vector.tensor_scalar(ve, mv[:, :, 1], LN_EPS, None, ALU.add)
        else:
            last = rsqrt_step(nc, k - 3, ve, rstd, tmp)
        last.then_inc(chain.sem, 1)


LN_INCS = 3 + RSQRT_INCS


def projections(nc, x, ident, w, mod_d, parts_d, v_d):
    with ExitStack() as ctx:
        def sb(name, shape, dt=F32):
            return ctx.enter_context(nc.sbuf_tensor(name, shape, dt))

        def sig(name, per=1):
            return Signal(ctx.enter_context(nc.semaphore("pj_" + name)), per)

        def arrivals(name, per):
            return Arrivals([ctx.enter_context(nc.semaphore(f"pj_{name}{p}")) for p in range(2)], per)

        xt = sb("pj_x", [P, 2, CT, D])
        mrow = sb("pj_mod", [P, 2, 2, D])
        stats, mv = sb("pj_stats", [P, CT, 6]), sb("pj_mv", [P, CT, 2])
        ve, rstd, tmp = sb("pj_ve", [P, CT]), sb("pj_rstd", [P, CT]), sb("pj_tmp", [P, CT])
        xn = sb("pj_xn", [P, 2, CT, D])
        hm = sb("pj_hm", [P, 2, CT, D])
        hT = sb("pj_hT", [P, 2, KT, CH])
        lat = sb("pj_lat", [P, 2, CH])
        parts = sb("pj_parts", [P, 2, 2, 3, KT, CH], BF16)
        res = sb("pj_res", [P, 2, KT, CH])
        vs = sb("pj_v", [P, 2, CT, NH, 2 * HD])
        pH = ctx.enter_context(nc.psum_tensor("pj_pH", [P, KT, CH], F32))
        pL = ctx.enter_context(nc.psum_tensor("pj_pL", [P, CH], F32))
        pQ = ctx.enter_context(nc.psum_tensor("pj_pQ", [P, KT, CH], F32))
        pK = ctx.enter_context(nc.psum_tensor("pj_pK", [P, KT, CH], F32))

        loaded = arrivals("loaded", 32)
        chain = sig("chain", LN_INCS)
        normed = sig("normed")
        modded = sig("modded", 2)
        turned = sig("turned")
        h_ready = sig("h_ready")
        lat_done, lat_ready = sig("lat_done"), sig("lat_ready")
        q_done, k_done, v_done = sig("q_done"), sig("k_done"), sig("v_done")
        hi_ready = sig("hi_ready", 2)
        split = sig("split", 6)
        v_ready = sig("v_ready")
        stored = arrivals("stored", 16 * 7)
        ones = sig("ones")

        def drive(eng, body):
            for n in range(2):
                body(n, n)
            with eng.Fori(1, NC // 2) as i:
                for p in range(2):
                    body(i * 2 + p, p)

        def later(n):
            return not isinstance(n, int) or n >= 2

        def again(n):
            return not isinstance(n, int) or n >= 1

        with nc.Block() as block:
            @block.sync
            def _(sp):
                def load(n, p):
                    if later(n):
                        sp.wait_ge(normed.sem, normed.upto(n - 2))
                        sp.wait_ge(modded.sem, modded.upto(n - 2))
                    sp.dma_start(xt[:, p], rows(x, n)).then_inc(loaded.sems[p], 16)
                    src = mod_d[bass.ds(n // 2, 1), 0:2, :].to_broadcast([P, 2, D])
                    sp.dma_start(mrow[:, p], src).then_inc(loaded.sems[p], 16)

                def store(n, p):
                    sp.wait_ge(split.sem, split.upto(n))
                    for qk in range(2):
                        for part in range(3):
                            dst = parts_d[qk, part].rearrange("(m p) b t -> p m b t", p=P)
                            dst = dst[:, :, bass.ds(n // 2, 1), bass.ds((n % 2) * CH, CH)]
                            sp.dma_start(dst.rearrange("p m b t -> p m (b t)"),
                                         parts[:, p, qk, part]).then_inc(stored.sems[p], 16)
                    sp.wait_ge(v_ready.sem, v_ready.upto(n))
                    sp.dma_start(rows(v_d, n), vs[:, p].rearrange("p t h c -> p t (h c)")).then_inc(stored.sems[p], 16)

                load(0, 0)
                load(1, 1)
                with sp.Fori(0, NC // 2 - 1) as i:
                    for p in range(2):
                        load(i * 2 + 2 + p, p)
                        store(i * 2 + p, p)
                store(NC - 2, 0)
                store(NC - 1, 1)
                sp.wait_ge(stored.sems[0], stored.upto(NC - 2))
                sp.wait_ge(stored.sems[1], stored.upto(NC - 1))

            @block.vector
            def _(dve):
                nc.vector.memset(vs[:, :, :, :, HD:2 * HD], 1.0).then_inc(ones.sem, 1)

                def norm(n, p):
                    dve.wait_ge(loaded.sems[p], loaded.upto(n))
                    layer_norm_steps(nc, dve, chain, n, range(LN_INCS), xt[:, p], stats, mv, ve[:], rstd[:], tmp[:])
                    dve.wait_ge(chain.sem, chain.upto(n))
                    if later(n):
                        dve.wait_ge(modded.sem, modded.upto(n - 2, 1))
                    for t in range(CT):
                        last = nc.vector.tensor_scalar(xn[:, p, t, :], xt[:, p, t, :], mv[:, t, 0:1],
                                                       rstd[:, t:t + 1], ALU.subtract, ALU.mult)
                    last.then_inc(normed.sem, 1)

                def parts_of(n, p):
                    split.begin()
                    for qk, ps in enumerate((pQ, pK)):
                        dve.wait_ge(hi_ready.sem, hi_ready.upto(n, qk + 1))
                        r = res[:, qk].rearrange("p m t -> p (m t)")
                        hi, mid, lo = (parts[:, p, qk, j].rearrange("p m t -> p (m t)") for j in range(3))
                        nc.vector.tensor_tensor(r, ps[:].rearrange("p m t -> p (m t)"), hi,
                                                ALU.subtract).then_inc(split.counted(), 1)
                        dve.wait_ge(split.sem, split.so_far(n))
                        if later(n) and qk == 0:
                            dve.wait_ge(stored.sems[p], stored.upto(n - 2))
                        nc.vector.tensor_copy(mid, r).then_inc(split.counted(), 1)
                        dve.wait_ge(split.sem, split.so_far(n))
                        nc.vector.tensor_tensor(lo, r, mid, ALU.subtract).then_inc(split.counted(), 1)

                norm(0, 0)
                for n in range(2):
                    norm(n + 1, (n + 1) % 2)
                    parts_of(n, n)
                with dve.Fori(0, NC // 2 - 2) as i:
                    for p in range(2):
                        norm(i * 2 + 3 + p, 1 - p)
                        parts_of(i * 2 + 2 + p, p)
                norm(NC - 1, 1)
                parts_of(NC - 2, 0)
                parts_of(NC - 1, 1)

            @block.gpsimd
            def _(pool):
                def body(n, p):
                    pool.wait_ge(normed.sem, normed.upto(n))
                    for t_in, t_out, row, op in ((xn, xn, 1, ALU.mult), (xn, hm, 0, ALU.add)):
                        if row == 0:
                            pool.wait_ge(modded.sem, modded.upto(n, 1))
                            if later(n):
                                pool.wait_ge(turned.sem, turned.upto(n - 2))
                        nc.gpsimd.tensor_tensor(t_out[:, p], t_in[:, p],
                                                mrow[:, p, row, :].unsqueeze(1).to_broadcast([P, CT, D]),
                                                op).then_inc(modded.sem, 1)

                drive(pool, body)

            @block.tensor
            def _(pe):
                def body(n, p):
                    pe.wait_ge(modded.sem, modded.upto(n))
                    if again(n):
                        pe.wait_ge(v_ready.sem, v_ready.upto(n - 1))
                    for t in range(CT):
                        for k in range(KT):
                            last = nc.tensor.transpose(pH[:, k, t * P:(t + 1) * P],
                                                       hm[:, p, t, k * P:(k + 1) * P], ident[:])
                    last.then_inc(turned.sem, 1)
                    pe.wait_ge(h_ready.sem, h_ready.upto(n))
                    if again(n):
                        pe.wait_ge(lat_ready.sem, lat_ready.upto(n - 1))
                    for k in range(KT):
                        last = nc.tensor.matmul(pL[:], w["wa"][:, k, :], hT[:, p, k, :],
                                                start=(k == 0), stop=(k == KT - 1))
                    last.then_inc(lat_done.sem, 1)
                    if again(n):
                        pe.wait_ge(split.sem, split.upto(n - 1, 1))
                    for m in range(KT):
                        for k in range(KT):
                            last = nc.tensor.matmul(pQ[:, m, :], w["wq"][:, k, m * P:(m + 1) * P], hT[:, p, k, :],
                                                    start=(k == 0), stop=(k == KT - 1))
                    last.then_inc(q_done.sem, 1)
                    pe.wait_ge(lat_ready.sem, lat_ready.upto(n))
                    if again(n):
                        pe.wait_ge(split.sem, split.upto(n - 1, 4))
                    for m in range(KT):
                        last = nc.tensor.matmul(pK[:, m, :], w["wkb"][:, m * P:(m + 1) * P], lat[:, p, :],
                                                start=True, stop=True)
                    last.then_inc(k_done.sem, 1)
                    for t in range(CT):
                        last = nc.tensor.matmul(pH[:, t // 2, (t % 2) * D:(t % 2 + 1) * D],
                                                lat[:, p, t * P:(t + 1) * P], w["wvb"][:], start=True, stop=True)
                    last.then_inc(v_done.sem, 1)

                drive(pe, body)

            @block.scalar
            def _(act):
                act.wait_ge(ones.sem, 1)

                def body(n, p):
                    act.wait_ge(turned.sem, turned.upto(n))
                    if later(n):
                        act.wait_ge(q_done.sem, q_done.upto(n - 2))
                    nc.scalar.copy(hT[:, p], pH[:]).then_inc(h_ready.sem, 1)
                    act.wait_ge(lat_done.sem, lat_done.upto(n))
                    if later(n):
                        act.wait_ge(v_done.sem, v_done.upto(n - 2))
                    nc.scalar.copy(lat[:, p], pL[:]).then_inc(lat_ready.sem, 1)
                    if later(n):
                        act.wait_ge(stored.sems[p], stored.upto(n - 2))
                    act.wait_ge(q_done.sem, q_done.upto(n))
                    nc.scalar.copy(parts[:, p, 0, 0], pQ[:]).then_inc(hi_ready.sem, 1)
                    act.wait_ge(k_done.sem, k_done.upto(n))
                    nc.scalar.copy(parts[:, p, 1, 0], pK[:]).then_inc(hi_ready.sem, 1)
                    act.wait_ge(v_done.sem, v_done.upto(n))
                    for j in range(2):
                        last = nc.scalar.copy(vs[:, p, 2 * j:2 * j + 2, :, 0:HD],
                                              pH[:, j, :].rearrange("p (t h c) -> p t h c", t=2, h=NH))
                    last.then_inc(v_ready.sem, 1)

                drive(act, body)


def full_attention(nc, ident, identb, parts_d, v_d, att_d):
    KB = N // P
    MAX_USES = 2 * GH * KB
    STEP_ROWS = MAX_USES // KB
    AHEAD = 2 * STEP_ROWS
    TURN = 2
    NB = 3
    T = 3
    UNITS = 2 * GH

    with ExitStack() as ctx:
        def sb(name, shape, dt=F32):
            return ctx.enter_context(nc.sbuf_tensor(name, shape, dt))

        def sem(name):
            return ctx.enter_context(nc.semaphore("fa_" + name))

        Qs = sb("fa_Q", [P, NB, GH, N], BF16)
        Ks = sb("fa_K", [P, NB, GH, N], BF16)
        V = sb("fa_V", [P, NB, KB, GH, 2 * HD])
        Pr = sb("fa_P", [P, 2, GH, N])
        OT = sb("fa_OT", [P, N])
        mx = sb("fa_mx", [P, GH * KB, 2])
        nm = sb("fa_nm", [P, GH * KB])
        nb = sb("fa_nb", [P, KB, 2, GH], BF16)
        nrow = sb("fa_nrow", [2 * GH, NB, N], BF16)
        rec = sb("fa_rec", [P, 2, 4 * GH])
        att = sb("fa_att", [P, KB, GH * HD])
        pS = ctx.enter_context(nc.psum_tensor("fa_pS", [P, T, 512], F32))
        pR = ctx.enter_context(nc.psum_tensor("fa_pR", [P, T, 512], F32))
        pO = ctx.enter_context(nc.psum_tensor("fa_pO", [P, 2, 512], F32))

        stack_in = Arrivals([sem(f"stack_in{s}") for s in range(NB)], 16 * 12)
        v_in = Arrivals([sem(f"v_in{s}") for s in range(NB)], 16)
        max_in = Arrivals([sem(f"max_in{s}") for s in range(NB)], 32)
        ones = Signal(sem("ones"), 1)
        scored = Signal(sem("scored"), KB * UNITS)
        exped = Signal(sem("exped"), KB * UNITS)
        summed = Signal(sem("summed"), KB)
        o_out = Signal(sem("o_out"), 1)
        row_full, row_free = sem("row_full"), sem("row_free")
        neg = Signal(sem("neg"), 4)
        inverse = Signal(sem("inverse"), 2)
        stored = Signal(sem("stored"), 16)

        PROLOGUE = MAX_USES + TURN + AHEAD
        LOOPS = (GROUPS - 3) // NB

        def first_use(n):
            if isinstance(n, int) and n == 0:
                return PROLOGUE
            uses = PROLOGUE - TURN + (MAX_USES + 2 * TURN) * n
            return uses - AHEAD if is_last(n) else uses

        def divided(n):
            if is_last(n):
                at = first_use(n) + TURN
            else:
                at = first_use(n + 1) + (0 if is_last(n + 1) else 2 * STEP_ROWS)
            return at + TURN

        def maxima_out(n):
            if is_first(n):
                at = MAX_USES
            else:
                at = first_use(n - 1) + MAX_USES - AHEAD
                at = at + (0 if is_first(n - 1) else TURN) + (0 if is_last(n) else STEP_ROWS // 2)
            return at + TURN

        def tile_of(n, s, k):
            at = first_use(n) if isinstance(n, int) else PROLOGUE - TURN + (MAX_USES + 2 * TURN) * s
            return (at + k) % T

        def step_rows(n, s, k):
            ahead = 2 if k >= KB - 2 else 1
            if isinstance(n, int) and n + ahead >= GROUPS:
                return []
            first = (k + 2) % KB * STEP_ROWS
            return [(n + ahead, (s + ahead) % NB, first + j) for j in range(STEP_ROWS)]

        def drive(eng, body):
            body(0, 0)
            with eng.Fori(0, LOOPS) as i:
                for j in range(NB):
                    body(i * NB + 1 + j, (1 + j) % NB)
            for n in range(1 + LOOPS * NB, GROUPS):
                body(n, n % NB)

        def is_first(n):
            return isinstance(n, int) and n == 0

        def is_last(n):
            return isinstance(n, int) and n == GROUPS - 1

        with nc.Block() as block:
            @block.sync
            def _(sp):
                def load(n, s):
                    b, g = n // NG, n % NG
                    if not (isinstance(n, int) and n < NB):
                        sp.wait_ge(scored.sem, scored.upto(n - NB))
                    for stack, qk, order in ((Qs, 0, Q_PARTS), (Ks, 1, K_PARTS)):
                        for slot, part in enumerate(order):
                            src = parts_d[qk, part].rearrange("(g h d) b t -> d g h b t", d=HD, h=GH)
                            src = src[:, bass.ds(g, 1), :, bass.ds(b, 1), :]
                            sp.dma_start(stack[slot * HD:(slot + 1) * HD, s],
                                         src.rearrange("d g h b t -> d (g h) (b t)")).then_inc(stack_in.sems[s], 16)
                    if not (isinstance(n, int) and n < NB):
                        sp.wait_ge(summed.sem, summed.upto(n - NB))
                    src = v_d[bass.ds(b, 1), :, bass.ds(g * (GH * 2 * HD), GH * 2 * HD)]
                    sp.dma_start(V[:, s].rearrange("p k h c -> p k (h c)"),
                                 src.rearrange("b (k p) c -> p (b k) c", p=P)).then_inc(v_in.sems[s], 16)

                def max_rows(n, s):
                    sp.wait_ge(row_free, maxima_out(n))
                    for part in range(2):
                        dst = Qs[SROWS + part:SROWS + part + 1, s]
                        sp.dma_start(dst, nrow[part * GH:(part + 1) * GH, s, :]).then_inc(max_in.sems[s], 16)

                def store(n):
                    sp.wait_ge(row_free, divided(n))
                    b, g = n // NG, n % NG
                    dst = att_d[bass.ds(b, 1), :, bass.ds(g * (GH * HD), GH * HD)]
                    sp.dma_start(dst.rearrange("b (k p) c -> p (b k) c", p=P), att[:]).then_inc(stored.sem, 16)

                load(0, 0)
                load(1, 1)
                max_rows(0, 0)
                load(2, 2)

                def body(n, s):
                    if not is_first(n):
                        if not (isinstance(n, int) and n + 2 >= GROUPS):
                            load(n + 2, (s + 2) % NB)
                        store(n - 1)
                    if not is_last(n):
                        max_rows(n + 1, (s + 1) % NB)

                drive(sp, body)
                store(GROUPS - 1)
                sp.wait_ge(stored.sem, stored.upto(GROUPS - 1))

            @block.tensor
            def _(pe):
                use = [0, 0, 0]

                def row_tile():
                    base, first, k = use
                    if not (isinstance(base, int) and base + k < T):
                        pe.wait_ge(row_free, base + k - T + 1)
                    use[2] += 1
                    return pR[:, (first + k) % T, :]

                def row_scores(n, s, j):
                    h, q, half = j // (2 * KB), j // 2 % KB, j % 2
                    if j == 0:
                        pe.wait_ge(stack_in.sems[s], stack_in.upto(n))
                    nc.tensor.matmul(row_tile(), Qs[0:SROWS, s, h, q * P:(q + 1) * P],
                                     Ks[0:SROWS, s, h, half * 512:(half + 1) * 512],
                                     start=True, stop=True).then_inc(row_full, 1)

                def turn_max(n):
                    pe.wait_ge(neg.sem, neg.upto(n))
                    for half in range(2):
                        r = row_tile()
                        for q in range(4):
                            last = nc.tensor.matmul(r[0:2 * GH, q * P:(q + 1) * P],
                                                    nb[:, half * 4 + q].rearrange("p a h -> p (a h)"), identb[:],
                                                    start=True, stop=True)
                        last.then_inc(row_full, 1)

                def scores(n, s, k, h, half):
                    u = (k * GH + h) * 2 + half
                    if u == 0:
                        pe.wait_ge(max_in.sems[s], max_in.upto(n))
                        if is_first(n):
                            pe.wait_ge(ones.sem, ones.upto(0))
                    if not (is_first(n) and u < T):
                        pe.wait_ge(exped.sem, n * exped.per + u - T + 1)
                    nc.tensor.matmul(pS[:, (s * exped.per + u) % T, :],
                                     Ks[0:SROWS + 2, s, h, k * P:(k + 1) * P],
                                     Qs[0:SROWS + 2, s, h, half * 512:(half + 1) * 512],
                                     start=True, stop=True).then_inc(scored.sem, 1)

                def sums(n, s, k, half):
                    if half == 0:
                        pe.wait_ge(exped.sem, exped.upto(n, (k + 1) * UNITS))
                        if k == 0:
                            pe.wait_ge(v_in.sems[s], v_in.upto(n))
                            if not is_first(n):
                                pe.wait_ge(o_out.sem, o_out.upto(n - 1))
                    for h in range(GH):
                        last = nc.tensor.matmul(pO[h * 32:(h + 1) * 32, half, :], V[:, s, k, h, :],
                                                Pr[:, k % 2, h, half * 512:(half + 1) * 512],
                                                start=(k == 0), stop=(k == KB - 1))
                    if half == 1:
                        last.then_inc(summed.sem, 1)

                def turn_sums(n):
                    pe.wait_ge(o_out.sem, o_out.upto(n))
                    for half in range(2):
                        r = row_tile()
                        for t in range(4):
                            at = (half * 4 + t) * P
                            last = nc.tensor.transpose(r[:, t * P:(t + 1) * P], OT[:, at:at + P], ident[:])
                        last.then_inc(row_full, 1)

                for j in range(MAX_USES):
                    row_scores(0, 0, j)
                turn_max(0)
                for j in range(AHEAD):
                    row_scores(1, 1, j)

                def body(n, s):
                    use[0], use[1], use[2] = first_use(n), tile_of(n, s, 0), 0
                    for k in range(KB):
                        rows = step_rows(n, s, k)
                        for h in range(GH):
                            for half in range(2):
                                scores(n, s, k, h, half)
                                for r in rows[2 * h + half:2 * h + half + 1]:
                                    row_scores(*r)
                                if h % 2 == 1 and half == 0:
                                    if k > 0:
                                        sums(n, s, k - 1, h // 2)
                                    elif not is_first(n):
                                        sums(n - 1, (s - 1) % NB, KB - 1, h // 2)
                            if h == 1 and k == KB - 2 and not is_last(n):
                                turn_max(n + 1)
                        if k == 1 and not is_first(n):
                            turn_sums(n - 1)

                drive(pe, body)
                for half in range(2):
                    sums(GROUPS - 1, (GROUPS - 1) % NB, KB - 1, half)
                use[0], use[1], use[2] = first_use(GROUPS - 1) + TURN, tile_of(GROUPS - 1, 0, TURN), 0
                turn_sums(GROUPS - 1)

            @block.scalar
            def _(act):
                def copy_out(n):
                    act.wait_ge(summed.sem, summed.upto(n))
                    if not is_first(n):
                        act.wait_ge(row_free, divided(n - 1))
                    nc.scalar.copy(OT[:], pO[:].rearrange("p a q -> p (a q)")).then_inc(o_out.sem, 1)

                def body(n, s):
                    for k in range(KB):
                        for h in range(GH):
                            for half in range(2):
                                u = (k * GH + h) * 2 + half
                                act.wait_ge(scored.sem, scored.upto(n, u + 1))
                                if h == 0 and half == 0 and not (is_first(n) and k < 2):
                                    act.wait_ge(summed.sem, n * KB + k - 1)
                                nc.scalar.activation(Pr[:, k % 2, h, half * 512:(half + 1) * 512],
                                                     pS[:, (s * exped.per + u) % T, :],
                                                     ACT.Exp).then_inc(exped.sem, 1)
                        if k == 0 and not is_first(n):
                            copy_out(n - 1)

                drive(act, body)
                copy_out(GROUPS - 1)

            @block.vector
            def _(dve):
                use = [0, 0, 0]
                for s in range(NB):
                    last = nc.vector.memset(Ks[SROWS:SROWS + 2, s], 1.0)
                last.then_inc(ones.sem, 1)

                def row_tile():
                    base, first, k = use
                    dve.wait_ge(row_full, base + k + 1)
                    use[2] += 1
                    return pR[:, (first + k) % T, :]

                def row_max(j):
                    nc.vector.tensor_reduce(mx[:, j // 2, j % 2:j % 2 + 1], row_tile(), AX.X,
                                            ALU.max).then_inc(row_free, 1)

                def negative(n):
                    neg.begin()
                    dve.wait_ge(row_free, use[0] + use[2])
                    nc.vector.tensor_reduce(nm[:], mx[:], AX.X, ALU.max, negate=True).then_inc(neg.counted(), 1)
                    dve.wait_ge(neg.sem, neg.so_far(n))
                    hi = nb[:, :, 0, :].rearrange("p q h -> p h q")
                    lo = nb[:, :, 1, :].rearrange("p q h -> p h q")
                    m = nm[:].rearrange("p (h q) -> p h q", h=GH)
                    nc.vector.tensor_copy(hi, m).then_inc(neg.counted(), 1)
                    dve.wait_ge(neg.sem, neg.so_far(n))
                    nc.vector.tensor_tensor(m, m, hi, ALU.subtract).then_inc(neg.counted(), 1)
                    dve.wait_ge(neg.sem, neg.so_far(n))
                    nc.vector.tensor_copy(lo, m).then_inc(neg.counted(), 1)

                def max_out(n, s):
                    for half in range(2):
                        r = row_tile()
                        nc.vector.tensor_copy(nrow[:, s, half * 512:(half + 1) * 512],
                                              r[0:2 * GH, :]).then_inc(row_free, 1)

                def divide(n):
                    inverse.begin()
                    for half in range(2):
                        r = row_tile().rearrange("p (a c) -> p a c", c=2 * HD)
                        if half == 0 and not is_first(n):
                            dve.wait_ge(stored.sem, stored.upto(n - 1))
                        nc.vector.reciprocal(rec[:, half, :], r[:, :, HD]).then_inc(inverse.counted(), 1)
                        dve.wait_ge(inverse.sem, inverse.so_far(n))
                        dst = att[:, half * 4:(half + 1) * 4, :].rearrange("p t (h c) -> p (t h) c", c=HD)
                        nc.vector.tensor_tensor(dst, r[:, :, 0:HD],
                                                rec[:, half, :].unsqueeze(2).to_broadcast([P, 4 * GH, HD]),
                                                ALU.mult).then_inc(row_free, 1)

                for j in range(MAX_USES):
                    row_max(j)
                negative(0)
                max_out(0, 0)
                for j in range(AHEAD):
                    row_max(j)

                def body(n, s):
                    use[0], use[1], use[2] = first_use(n), tile_of(n, s, 0), 0
                    for k in range(KB):
                        rows = step_rows(n, s, k)
                        turn = k == KB - 2 and not is_last(n)
                        if turn:
                            negative(n + 1)
                        for _, _, j in rows[0:STEP_ROWS // 2]:
                            row_max(j)
                        if turn:
                            max_out(n + 1, (s + 1) % NB)
                        for _, _, j in rows[STEP_ROWS // 2:]:
                            row_max(j)
                        if k == 1 and not is_first(n):
                            divide(n - 1)

                drive(dve, body)
                use[0], use[1], use[2] = first_use(GROUPS - 1) + TURN, tile_of(GROUPS - 1, 0, TURN), 0
                divide(GROUPS - 1)


def attention_out(nc, x, ident, w, mod_d, att_d, x1_d, lo_dst, hi_dst):
    with ExitStack() as ctx:
        def sb(name, shape, dt=F32):
            return ctx.enter_context(nc.sbuf_tensor(name, shape, dt))

        def sig(name, per=1):
            return Signal(ctx.enter_context(nc.semaphore("ao_" + name)), per)

        def arrivals(name, per, bufs=2):
            return Arrivals([ctx.enter_context(nc.semaphore(f"ao_{name}{p}")) for p in range(bufs)], per)

        R = 4
        at = sb("ao_att", [P, R, CT, D])
        xt = sb("ao_x", [P, R, CT, D])
        mrow = sb("ao_mod", [P, R, 3, D])
        aT = sb("ao_aT", [P, KT, CH])
        x1 = sb("ao_x1", [P, 2, CT, D])
        stats, mv = sb("ao_stats", [P, CT, 6]), sb("ao_mv", [P, CT, 2])
        ve, rstd, tmp = sb("ao_ve", [P, CT]), sb("ao_rstd", [P, CT]), sb("ao_tmp", [P, CT])
        xn = sb("ao_xn", [P, 2, CT, D])
        hm = sb("ao_hm", [P, 2, CT, D])
        pT = ctx.enter_context(nc.psum_tensor("ao_pT", [P, KT, CH], F32))
        pY = ctx.enter_context(nc.psum_tensor("ao_pY", [P, CT, D], F32))

        loaded = arrivals("loaded", 48, R)
        turned, aT_ready, projected = sig("turned"), sig("aT_ready"), sig("projected")
        gated = sig("gated", 2)
        chain = sig("chain", LN_INCS)
        normed = sig("normed")
        modded = sig("modded", 2)
        stored = arrivals("stored", 48)

        def later(n):
            return not isinstance(n, int) or n >= 2

        def again(n):
            return not isinstance(n, int) or n >= 1

        def drive(eng, body):
            for n in range(R):
                body(n, n)
            with eng.Fori(1, NC // R) as i:
                for r in range(R):
                    body(i * R + r, r)

        with nc.Block() as block:
            @block.sync
            def _(sp):
                def load(n, p):
                    if not isinstance(n, int):
                        sp.wait_ge(modded.sem, modded.upto(n - R))
                    sp.dma_start(at[:, p], rows(att_d, n)).then_inc(loaded.sems[p], 16)
                    sp.dma_start(xt[:, p], rows(x, n)).then_inc(loaded.sems[p], 16)
                    src = mod_d[bass.ds(n // 2, 1), 2:5, :].to_broadcast([P, 3, D])
                    sp.dma_start(mrow[:, p], src).then_inc(loaded.sems[p], 16)

                def store(n, p):
                    sp.wait_ge(gated.sem, gated.upto(n))
                    sp.dma_start(rows(x1_d, n), x1[:, p]).then_inc(stored.sems[p], 16)
                    sp.wait_ge(modded.sem, modded.upto(n))
                    sp.dma_start(rows(lo_dst, n), hm[:, p, :, 0:P]).then_inc(stored.sems[p], 16)
                    sp.dma_start(padded(hi_dst, n, CH), hm[:, p, :, P:D]).then_inc(stored.sems[p], 16)

                for n in range(R):
                    load(n, n)
                with sp.Fori(0, NC // R - 1) as i:
                    for r in range(R):
                        store(i * R + r, r % 2)
                        load(i * R + R + r, r)
                for n in range(NC - R, NC):
                    store(n, n % 2)
                sp.wait_ge(stored.sems[0], stored.upto(NC - 2))
                sp.wait_ge(stored.sems[1], stored.upto(NC - 1))

            @block.tensor
            def _(pe):
                def body(n, r):
                    pe.wait_ge(loaded.sems[r], loaded.upto(n))
                    if again(n):
                        pe.wait_ge(aT_ready.sem, aT_ready.upto(n - 1))
                    for t in range(CT):
                        for k in range(KT):
                            last = nc.tensor.transpose(pT[:, k, t * P:(t + 1) * P],
                                                       at[:, r, t, k * P:(k + 1) * P], ident[:])
                    last.then_inc(turned.sem, 1)
                    pe.wait_ge(aT_ready.sem, aT_ready.upto(n))
                    if again(n):
                        pe.wait_ge(gated.sem, gated.upto(n - 1, 1))
                    for t in range(CT):
                        for k in range(KT):
                            last = nc.tensor.matmul(pY[:, t, :], aT[:, k, t * P:(t + 1) * P], w["wo"][:, k, :],
                                                    start=(k == 0), stop=(k == KT - 1))
                    last.then_inc(projected.sem, 1)

                drive(pe, body)

            @block.scalar
            def _(act):
                def body(n, r):
                    act.wait_ge(turned.sem, turned.upto(n))
                    if again(n):
                        act.wait_ge(projected.sem, projected.upto(n - 1))
                    nc.scalar.copy(aT[:], pT[:]).then_inc(aT_ready.sem, 1)

                drive(act, body)

            @block.vector
            def _(dve):
                def body(n, r):
                    p = r % 2
                    dve.wait_ge(loaded.sems[r], loaded.upto(n))
                    dve.wait_ge(projected.sem, projected.upto(n))
                    if later(n):
                        dve.wait_ge(stored.sems[p], stored.upto(n - 2))
                    gate = mrow[:, r, 0, :].unsqueeze(1).to_broadcast([P, CT, D])
                    nc.vector.tensor_tensor(x1[:, p], pY[:], gate, ALU.mult).then_inc(gated.sem, 1)
                    dve.wait_ge(gated.sem, gated.upto(n, 1))
                    nc.vector.tensor_tensor(x1[:, p], x1[:, p], xt[:, r], ALU.add).then_inc(gated.sem, 1)
                    dve.wait_ge(gated.sem, gated.upto(n))
                    layer_norm_steps(nc, dve, chain, n, range(LN_INCS), x1[:, p], stats, mv, ve[:], rstd[:], tmp[:])
                    dve.wait_ge(chain.sem, chain.upto(n))
                    if later(n):
                        dve.wait_ge(modded.sem, modded.upto(n - 2, 1))
                    for t in range(CT):
                        last = nc.vector.tensor_scalar(xn[:, p, t, :], x1[:, p, t, :], mv[:, t, 0:1],
                                                       rstd[:, t:t + 1], ALU.subtract, ALU.mult)
                    last.then_inc(normed.sem, 1)

                drive(dve, body)

            @block.gpsimd
            def _(pool):
                def body(n, r):
                    p = r % 2
                    pool.wait_ge(normed.sem, normed.upto(n))
                    for t_in, t_out, row, op in ((xn, xn, 2, ALU.mult), (xn, hm, 1, ALU.add)):
                        if row == 1:
                            pool.wait_ge(modded.sem, modded.upto(n, 1))
                            if later(n):
                                pool.wait_ge(stored.sems[p], stored.upto(n - 2))
                        nc.gpsimd.tensor_tensor(t_out[:, p], t_in[:, p],
                                                mrow[:, r, row, :].unsqueeze(1).to_broadcast([P, CT, D]),
                                                op).then_inc(modded.sem, 1)

                drive(pool, body)


def window_signals(nc, ctx):
    pairs = HEADS // 2
    per = dict(
        x_turned=1, xT_ready=1,
        qk_done=1, v_done=1, v_ready=1,
        squared=1, chain=2 + RSQRT_INCS, scaled=1, rotated=4,
        q_turned=1, k_turned=1, q_ready=1, k_ready=2,
        scored=pairs, masked=pairs, exped=pairs, inverse=pairs, weighted=pairs,
        p_turned=pairs, pT_ready=pairs, summed=pairs, o_ready=1,
        projected=1, added=1,
    )
    signals = {name: Signal(ctx.enter_context(nc.semaphore("wa_" + name)), k) for name, k in per.items()}
    for name, bufs, k in (("x_in", WIN_BUFS, 48), ("stored", 2, 32)):
        signals[name] = Arrivals([ctx.enter_context(nc.semaphore(f"wa_{name}{p}")) for p in range(bufs)], k)
    return signals


def window_attention(nc, a, layer, ident, trig_d, src, dst, s):
    TILES = B * NW
    PAIRS = HEADS // 2
    R = WIN_BUFS
    base = layer * TILES
    lo_s, hi_s = src
    lo_t, hi_t = dst

    with ExitStack() as ctx:
        def sb(name, shape, dt=F32):
            return ctx.enter_context(nc.sbuf_tensor(f"wa{layer}_{name}", shape, dt))

        def pb(name, shape):
            return ctx.enter_context(nc.psum_tensor(f"wa{layer}_{name}", shape, F32))

        wqkv = sb("wqkv", [P, KT, 3 * INNER])
        wo = sb("wo", [P, INNER // P, D])
        trig = sb("trig", [P, NW, 4, DH])
        mask = sb("mask", [P, 2, 2 * WIN])
        xs = sb("xs", [P, R, 2, P])
        xo = sb("xo", [P, R, P])
        xT = sb("xT", [P, KT, P])
        sq = sb("sq", [P, 2 * INNER])
        ss, rn, rt = sb("ss", [P, 2 * HEADS]), sb("rn", [P, 2 * HEADS]), sb("rt", [P, 2 * HEADS])
        qn = sb("qn", [P, 2, HEADS, DH])
        qa = sb("qa", [P, 2, HEADS, DH])
        qb = sb("qb", [P, 2, HEADS, DH])
        qT = sb("qT", [P, 2, PAIRS, P])
        kT = sb("kT", [P, R, PAIRS, 2, P])
        V = sb("V", [P, R, HEADS, DH])
        sm = sb("sm", [P, 2, 2, 2 * WIN])
        mn = sb("mn", [P, 2, HEADS])
        pr = sb("pr", [P, 2, 2, 2 * WIN])
        rs, ri = sb("rs", [P, 2, HEADS]), sb("ri", [P, 2, HEADS])
        pn = sb("pn", [P, 2, 2, 2 * WIN])
        pT = sb("pT", [P, 2, 2, 2, P])
        oT = sb("oT", [P, PAIRS, P])
        x2 = sb("x2", [P, 2, 2, P])
        gate = sb("gate", [P, PAIRS])
        pQK, pV, pM = pb("pQK", [P, 2, INNER]), pb("pV", [P, INNER]), pb("pM", [P, 512])
        pS, pP, pO = pb("pS", [P, 2, 512]), pb("pP", [P, 512]), pb("pO", [P, PAIRS, P])
        pX, pY = pM[:, 0:D], pM[:, D:2 * D]
        w_in = ctx.enter_context(nc.semaphore(f"wa{layer}_w_in"))
        zeroed = ctx.enter_context(nc.semaphore(f"wa{layer}_zeroed"))
        W_LOADS = 4

        def g(n):
            return n + base

        def early(n, k):
            return isinstance(n, int) and n < k

        def within(n):
            return not isinstance(n, int) or 0 <= n < TILES

        def fresh(n, hp):
            return early(n, 1) and layer == 0 and hp < 2

        def drive(eng, body):
            for i in range(NW):
                body(i, i)
            with eng.Fori(1, B) as b:
                for w in range(NW):
                    body(b * NW + w, w)
            for i in range(TILES, TILES + 3):
                body(i, i % NW)

        with nc.Block() as block:
            @block.sync
            def _(sp):
                for dst_, src_ in ((wqkv[:], a["L0_ffn_wqkv"][layer].rearrange("(k p) n -> p k n", p=P)),
                                   (wo[:], a["L0_ffn_wo"][layer].rearrange("(k p) n -> p k n", p=P)),
                                   (trig[:].rearrange("p w a c -> p w (a c)"),
                                    trig_d[layer].rearrange("w p c -> p w c")),
                                   (mask[:], a["mask"].rearrange("w p c -> p w c"))):
                    sp.dma_start(dst_, src_).then_inc(w_in, 16)

                def load(n, r):
                    b, t = n // NW, n % NW
                    flat = lo_s[bass.ds(b, 1), bass.ds(t * P, P), :].rearrange("b p c -> (b p) c")
                    sp.dma_start(xs[:, r, 0, :], flat).then_inc(s["x_in"].sems[r], 16)
                    flat = hi_s[bass.ds(b, 1), bass.ds(t * P, P), :].rearrange("b p c -> (b p) c")
                    sp.dma_start(xs[:, r, 1, :], flat).then_inc(s["x_in"].sems[r], 16)
                    flat = hi_s[bass.ds(b, 1), bass.ds(t * P + 1, P), :].rearrange("b p c -> (b p) c")
                    sp.dma_start(xo[:, r, :], flat).then_inc(s["x_in"].sems[r], 16)

                def store(n, p):
                    sp.wait_ge(s["added"].sem, s["added"].upto(g(n)))
                    b, t = n // NW, n % NW
                    flat = lo_t[bass.ds(b, 1), bass.ds(t * P, P), :].rearrange("b p c -> (b p) c")
                    sp.dma_start(flat, x2[:, p, 0, :]).then_inc(s["stored"].sems[p], 16)
                    flat = hi_t[bass.ds(b, 1), bass.ds(t * P + 1, P), :].rearrange("b p c -> (b p) c")
                    sp.dma_start(flat, x2[:, p, 1, :]).then_inc(s["stored"].sems[p], 16)

                for n in range(R):
                    load(n, n)
                with sp.Fori(0, TILES // R - 1) as i:
                    for r in range(R):
                        store(i * R + r, r % 2)
                        load(i * R + R + r, r)
                for n in range(TILES - R, TILES):
                    store(n, n % 2)
                sp.wait_ge(s["stored"].sems[0], s["stored"].upto(g(TILES - 2)))
                sp.wait_ge(s["stored"].sems[1], s["stored"].upto(g(TILES - 1)))

            @block.tensor
            def _(pe):
                def turn_x(n, r):
                    pe.wait_ge(s["x_in"].sems[r], s["x_in"].upto(g(n)))
                    if not early(n, 2):
                        pe.wait_ge(s["q_ready"].sem, s["q_ready"].upto(g(n - 2)))
                    for k in range(KT):
                        last = nc.tensor.transpose(pX[:, k * P:(k + 1) * P], xs[:, r, k, :], ident[:])
                    last.then_inc(s["x_turned"].sem, 1)

                def project(n, j):
                    if j == 2:
                        pe.wait_ge(s["xT_ready"].sem, s["xT_ready"].upto(g(n)))
                        if not early(n, 2):
                            pe.wait_ge(s["k_ready"].sem, s["k_ready"].upto(g(n - 2)))
                    if j == 0 and not early(n, 1):
                        pe.wait_ge(s["scaled"].sem, s["scaled"].upto(g(n - 1)))
                    for k in range(KT):
                        out = pQK[:, j, :] if j < 2 else pV[:]
                        last = nc.tensor.matmul(out, xT[:, k, :], wqkv[:, k, j * INNER:(j + 1) * INNER],
                                                start=(k == 0), stop=(k == KT - 1))
                    if j == 1:
                        last.then_inc(s["qk_done"].sem, 1)
                    if j == 2:
                        last.then_inc(s["v_done"].sem, 1)

                def turn_qk(n, j):
                    if j == 0:
                        pe.wait_ge(s["rotated"].sem, s["rotated"].upto(g(n)))
                        if within(n + 1):
                            pe.wait_ge(s["xT_ready"].sem, s["xT_ready"].upto(g(n + 1)))
                        if not early(n, 2):
                            pe.wait_ge(s["added"].sem, s["added"].upto(g(n - 2)))
                    elif within(n + 1):
                        pe.wait_ge(s["v_ready"].sem, s["v_ready"].upto(g(n + 1)))
                    dst = pM if j == 0 else pV
                    for hp in range(PAIRS):
                        last = nc.tensor.transpose(dst[:, hp * P:(hp + 1) * P],
                                                   qn[:, j, 2 * hp:2 * hp + 2, :].rearrange("p h c -> p (h c)"),
                                                   ident[:])
                    last.then_inc(s["q_turned" if j == 0 else "k_turned"].sem, 1)

                def scores(n, r, hp):
                    if hp == 0:
                        pe.wait_ge(s["q_ready"].sem, s["q_ready"].upto(g(n)))
                        pe.wait_ge(s["k_ready"].sem, s["k_ready"].upto(g(n)))
                    if not fresh(n, hp):
                        pe.wait_ge(s["masked"].sem, g(n) * PAIRS + hp - 1)
                    out = pS[:, hp % 2, :].rearrange("p (h w k) -> p h w k", h=2, w=2)
                    for w, kr in enumerate(((r - 1) % R, r % R)):
                        last = nc.tensor.matmul(out[:, :, w, :], qT[:, r % 2, hp, :], kT[:, kr, hp],
                                                start=True, stop=True)
                    last.then_inc(s["scored"].sem, 1)

                def turn_p(n, hp):
                    pe.wait_ge(s["weighted"].sem, s["weighted"].upto(g(n), hp + 1))
                    if not fresh(n, hp + 1):
                        pe.wait_ge(s["pT_ready"].sem, g(n) * PAIRS + hp)
                    for hh in range(2):
                        for w in range(2):
                            at = (hh * 2 + w) * P
                            last = nc.tensor.transpose(pP[:, at:at + P], pn[:, hp % 2, hh, w * WIN:(w + 1) * WIN],
                                                       ident[:])
                    last.then_inc(s["p_turned"].sem, 1)

                def values(n, r, hp):
                    pe.wait_ge(s["pT_ready"].sem, s["pT_ready"].upto(g(n), hp + 1))
                    if hp == 0 and not early(n, 1):
                        pe.wait_ge(s["o_ready"].sem, s["o_ready"].upto(g(n - 1)))
                    for w, kr in enumerate(((r - 1) % R, r % R)):
                        for hh in range(2):
                            last = nc.tensor.matmul(pO[hh * DH:(hh + 1) * DH, hp, :], V[:, kr, 2 * hp + hh, :],
                                                    pT[:, hp % 2, hh, w, :], start=(w == 0), stop=(w == 1))
                    last.then_inc(s["summed"].sem, 1)

                def project_out(n):
                    pe.wait_ge(s["o_ready"].sem, s["o_ready"].upto(g(n)))
                    for hp in range(PAIRS):
                        last = nc.tensor.matmul(pY, oT[:, hp, :], wo[:, hp, :],
                                                start=(hp == 0), stop=(hp == PAIRS - 1))
                    last.then_inc(s["projected"].sem, 1)

                pe.wait_ge(w_in, 16 * W_LOADS)
                pe.wait_ge(zeroed, 2)

                def body(i, w):
                    new, mid, att, end = i, i - 1, i - 2, i - 3
                    r_att, r_end = w - 2, w - 3
                    if within(att):
                        scores(att, r_att, 0)
                    if within(new):
                        turn_x(new, w % R)
                    if within(att):
                        scores(att, r_att, 1)
                    if within(end):
                        values(end, r_end, 3)
                    if within(new):
                        project(new, 2)
                    if within(att):
                        scores(att, r_att, 2)
                    if within(end):
                        project_out(end)
                    if within(att):
                        turn_p(att, 0)
                        scores(att, r_att, 3)
                        turn_p(att, 1)
                        values(att, r_att, 0)
                    if within(new):
                        project(new, 0)
                        project(new, 1)
                    if within(mid):
                        turn_qk(mid, 0)
                    if within(att):
                        turn_p(att, 2)
                    if within(mid):
                        turn_qk(mid, 1)
                    if within(att):
                        values(att, r_att, 1)
                        turn_p(att, 3)
                        values(att, r_att, 2)

                drive(pe, body)

            @block.scalar
            def _(act):
                def x_out(n):
                    act.wait_ge(s["x_turned"].sem, s["x_turned"].upto(g(n)))
                    if not early(n, 1):
                        act.wait_ge(s["qk_done"].sem, s["qk_done"].upto(g(n - 1)))
                    nc.scalar.copy(xT[:].rearrange("p k t -> p (k t)"), pX).then_inc(s["xT_ready"].sem, 1)

                def square(n):
                    act.wait_ge(s["qk_done"].sem, s["qk_done"].upto(g(n)))
                    if not early(n, 1):
                        act.wait_ge(s["chain"].sem, s["chain"].upto(g(n - 1), 1))
                    nc.scalar.activation(sq[:].rearrange("p (a c) -> p a c", a=2), pQK[:],
                                         ACT.Square).then_inc(s["squared"].sem, 1)

                def v_out(n, r):
                    act.wait_ge(s["v_done"].sem, s["v_done"].upto(g(n)))
                    if not early(n, R):
                        act.wait_ge(s["summed"].sem, s["summed"].upto(g(n - R + 1)))
                    nc.scalar.copy(V[:, r].rearrange("p h c -> p (h c)"), pV[:]).then_inc(s["v_ready"].sem, 1)

                def q_out(n, p):
                    act.wait_ge(s["q_turned"].sem, s["q_turned"].upto(g(n)))
                    if not early(n, 2):
                        act.wait_ge(s["scored"].sem, s["scored"].upto(g(n - 2)))
                    nc.scalar.copy(qT[:, p].rearrange("p a t -> p (a t)"), pM[:]).then_inc(s["q_ready"].sem, 1)

                def k_out(n, r):
                    act.wait_ge(s["k_turned"].sem, s["k_turned"].upto(g(n)))
                    if not early(n, R):
                        act.wait_ge(s["scored"].sem, s["scored"].upto(g(n - R + 1)))
                    for hh in range(2):
                        at = hh * DH
                        nc.scalar.copy(kT[at:at + DH, r, :, hh, :],
                                       pV[at:at + DH, :].rearrange("p (a t) -> p a t", a=PAIRS))\
                            .then_inc(s["k_ready"].sem, 1)

                def exponentials(n, p, hp):
                    act.wait_ge(s["masked"].sem, s["masked"].upto(g(n), hp + 1))
                    if not fresh(n, hp):
                        act.wait_ge(s["weighted"].sem, g(n) * PAIRS + hp - 1)
                    for hh in range(2):
                        h = 2 * hp + hh
                        last = nc.scalar.activation(pr[:, hp % 2, hh, :], sm[:, hp % 2, hh, :], ACT.Exp,
                                                    bias=mn[:, p, h:h + 1], scale=-1.0,
                                                    accum_out=rs[:, p, h:h + 1])
                    last.then_inc(s["exped"].sem, 1)

                def p_out(n, hp):
                    act.wait_ge(s["p_turned"].sem, s["p_turned"].upto(g(n), hp + 1))
                    if not fresh(n, hp):
                        act.wait_ge(s["summed"].sem, g(n) * PAIRS + hp - 1)
                    nc.scalar.copy(pT[:, hp % 2].rearrange("p h w t -> p (h w t)"),
                                   pP[:]).then_inc(s["pT_ready"].sem, 1)

                def o_out(n):
                    act.wait_ge(s["summed"].sem, s["summed"].upto(g(n)))
                    if not early(n, 1):
                        act.wait_ge(s["projected"].sem, s["projected"].upto(g(n - 1)))
                    nc.scalar.copy(oT[:], pO[:]).then_inc(s["o_ready"].sem, 1)

                act.wait_ge(zeroed, 2)

                def body(i, w):
                    new, mid, att, end = i, i - 1, i - 2, i - 3
                    if within(new):
                        x_out(new)
                    if within(att):
                        exponentials(att, w % 2, 0)
                    if within(end):
                        o_out(end)
                    if within(att):
                        exponentials(att, w % 2, 1)
                    if within(new):
                        v_out(new, w % R)
                    if within(att):
                        p_out(att, 0)
                        exponentials(att, w % 2, 2)
                        p_out(att, 1)
                        exponentials(att, w % 2, 3)
                    if within(new):
                        square(new)
                    if within(mid):
                        q_out(mid, (w - 1) % 2)
                    if within(att):
                        p_out(att, 2)
                    if within(mid):
                        k_out(mid, (w - 1) % R)
                    if within(att):
                        p_out(att, 3)

                drive(act, body)

            @block.gpsimd
            def _(pool):
                def weigh(n, p, hp):
                    pool.wait_ge(s["inverse"].sem, s["inverse"].upto(g(n), hp + 1))
                    if not fresh(n, hp):
                        pool.wait_ge(s["p_turned"].sem, g(n) * PAIRS + hp - 1)
                    inv = ri[:, p, 2 * hp:2 * hp + 2].unsqueeze(2).to_broadcast([P, 2, 2 * WIN])
                    nc.gpsimd.tensor_tensor(pn[:, hp % 2], pr[:, hp % 2], inv, ALU.mult).then_inc(s["weighted"].sem, 1)

                def body(i, w):
                    if within(i - 2):
                        for hp in range(PAIRS):
                            weigh(i - 2, w % 2, hp)

                drive(pool, body)

            @block.vector
            def _(dve):
                nc.vector.memset(kT[:], 0.0).then_inc(zeroed, 1)
                nc.vector.memset(V[:, R - 1], 0.0).then_inc(zeroed, 1)
                dve.wait_ge(w_in, 16 * W_LOADS)

                def masks(n, w, hp):
                    dve.wait_ge(s["scored"].sem, s["scored"].upto(g(n), hp + 1))
                    if not fresh(n, hp):
                        dve.wait_ge(s["exped"].sem, g(n) * PAIRS + hp - 1)
                    nc.vector.memset(gate[:, hp:hp + 1], 0.0)
                    for hh in range(2):
                        h = 2 * hp + hh
                        last = nc.vector.tensor_tensor_reduce(
                            out=sm[:, hp % 2, hh, :], in0=pS[:, hp % 2, hh * 2 * WIN:(hh + 1) * 2 * WIN],
                            in1=mask[:, 0 if w == 0 else 1, :], scale=1.0, scalar=MASKED, op0=ALU.add, op1=ALU.min,
                            accum_out=mn[:, w % 2, h:h + 1])
                    last.then_inc(s["masked"].sem, 1)

                def inverse(n, p, hp):
                    dve.wait_ge(s["exped"].sem, s["exped"].upto(g(n), hp + 1))
                    nc.vector.reciprocal(ri[:, p, 2 * hp:2 * hp + 2],
                                         rs[:, p, 2 * hp:2 * hp + 2]).then_inc(s["inverse"].sem, 1)

                def norms(n, steps):
                    c = s["chain"]
                    for k in steps:
                        if k == 0:
                            dve.wait_ge(s["squared"].sem, s["squared"].upto(g(n)))
                            ins = nc.vector.tensor_reduce(ss[:], sq[:].rearrange("p (h c) -> p h c", c=DH), AX.X,
                                                          ALU.add)
                        else:
                            dve.wait_ge(c.sem, c.upto(g(n), k))
                            if k == 1:
                                ins = nc.vector.tensor_scalar(ss[:], ss[:], NORM_FLOOR, None, ALU.max)
                            else:
                                ins = rsqrt_step(nc, k - 2, ss[:], rn[:], rt[:])
                        ins.then_inc(c.sem, 1)

                def scale(n):
                    dve.wait_ge(s["chain"].sem, s["chain"].upto(g(n)))
                    nc.vector.tensor_tensor(qa[:].rearrange("p a h c -> p (a h) c"),
                                            pQK[:].rearrange("p a (h c) -> p (a h) c", c=DH),
                                            rn[:].unsqueeze(2).to_broadcast([P, 2 * HEADS, DH]),
                                            ALU.mult).then_inc(s["scaled"].sem, 1)

                def rotate(n, w, step):
                    c = s["rotated"]
                    hd = DH // 2
                    if step < 2:
                        at, other = step * hd, hd - step * hd
                        dve.wait_ge(s["scaled"].sem, s["scaled"].upto(g(n)))
                        ins = nc.vector.tensor_tensor(
                            qb[:, :, :, at:at + hd], qa[:, :, :, other:other + hd],
                            trig[:, w, 2:4, at:at + hd].unsqueeze(2).to_broadcast([P, 2, HEADS, hd]), ALU.mult)
                    elif step == 2:
                        dve.wait_ge(c.sem, c.upto(g(n), 2))
                        ins = nc.vector.tensor_tensor(
                            qa[:], qa[:], trig[:, w, 0:2, :].unsqueeze(2).to_broadcast([P, 2, HEADS, DH]), ALU.mult)
                    else:
                        dve.wait_ge(c.sem, c.upto(g(n), 3))
                        if not early(n, 1):
                            dve.wait_ge(s["k_turned"].sem, s["k_turned"].upto(g(n - 1)))
                        ins = nc.vector.tensor_tensor(qn[:], qa[:], qb[:], ALU.add)
                    ins.then_inc(c.sem, 1)

                def add(n, r):
                    dve.wait_ge(s["projected"].sem, s["projected"].upto(g(n)))
                    dve.wait_ge(s["x_in"].sems[r], s["x_in"].upto(g(n)))
                    if not early(n, 2):
                        dve.wait_ge(s["stored"].sems[r % 2], s["stored"].upto(g(n - 2)))
                    nc.vector.tensor_tensor(x2[:, r % 2, 0, :], pY[:, 0:P], xs[:, r, 0, :], ALU.add)
                    nc.vector.tensor_tensor(x2[:, r % 2, 1, :], pY[:, P:D], xo[:, r, :],
                                            ALU.add).then_inc(s["added"].sem, 1)

                LAST = 2 + RSQRT_INCS

                def body(i, w):
                    new, mid, att, end = i, i - 1, i - 2, i - 3
                    w_mid, w_att, w_end = (w - 1) % NW, (w - 2) % NW, (w - 3) % NW
                    if within(mid):
                        norms(mid, range(5, 7))
                    if within(att):
                        masks(att, w_att, 0)
                    if within(mid):
                        norms(mid, range(7, 9))
                    if within(att):
                        masks(att, w_att, 1)
                    if within(mid):
                        norms(mid, range(9, LAST))
                    if within(att):
                        inverse(att, w % 2, 0)
                    if within(mid):
                        scale(mid)
                    if within(att):
                        inverse(att, w % 2, 1)
                    if within(mid):
                        rotate(mid, w_mid, 0)
                        rotate(mid, w_mid, 1)
                    if within(att):
                        masks(att, w_att, 2)
                    if within(end):
                        add(end, w_end % R)
                    if within(mid):
                        rotate(mid, w_mid, 2)
                    if within(att):
                        masks(att, w_att, 3)
                        inverse(att, w % 2, 2)
                    if within(mid):
                        rotate(mid, w_mid, 3)
                    if within(att):
                        inverse(att, w % 2, 3)
                    if within(new):
                        norms(new, range(0, 5))

                drive(dve, body)


def ffn_signals(nc, ctx):
    per = dict(
        chain=LN_INCS, normed=1, biased=2, turned=1, hT_ready=2,
        gated=HB, lifted=HB, gelu=HB, mixed=HB, y_done=1, summed=1, scaled=1, final=1,
    )
    signals = {name: Signal(ctx.enter_context(nc.semaphore("ff_" + name)), k) for name, k in per.items()}
    for name, k in dict(x_in=48, last_in=32, stored=32).items():
        signals[name] = Arrivals([ctx.enter_context(nc.semaphore(f"ff_{name}{p}")) for p in range(2)], k)
    return signals


def feed_forward(nc, a, layer, ident, src, dst, x1_d, mod_d, out, s):
    base = layer * NC
    lo_s, hi_s = src
    final = dst is None

    with ExitStack() as ctx:
        def sb(name, shape, dt=F32):
            return ctx.enter_context(nc.sbuf_tensor(f"ff{layer}_{name}", shape, dt))

        w1 = sb("w1", [P, KT, 2, HB * P])
        w2 = sb("w2", [P, HB, D])
        b1 = sb("b1", [P, 2, HB])
        b2 = sb("b2", [P, D])
        lg, lb = sb("lg", [P, KT]), sb("lb", [P, KT])
        hx = sb("hx", [P, 2, CT, D])
        xo = sb("xo", [P, 2, CT, P])
        xb = sb("xb", [P, 2, CT, D])
        stats, mv = sb("stats", [P, CT, 6]), sb("mv", [P, CT, 2])
        ve, rstd, tmp = sb("ve", [P, CT]), sb("rstd", [P, CT]), sb("tmp", [P, CT])
        hn = sb("hn", [P, 2, CT, D])
        hT = sb("hT", [P, 2, KT, CH])
        gl = sb("gl", [P, 2, CH])
        u = sb("u", [P, HB, CH])
        y = sb("y", [P, 2, CT, D])
        if final:
            x1 = sb("x1", [P, 2, CT, D])
            gb = sb("gb", [P, 2, D])
            yg = sb("yg", [P, CT, D])
            yo = sb("yo", [P, 2, CT, D])
        pH = ctx.enter_context(nc.psum_tensor(f"ff{layer}_pH", [P, KT, CH], F32))
        pG = ctx.enter_context(nc.psum_tensor(f"ff{layer}_pG", [P, 2, CH], F32))
        pA = ctx.enter_context(nc.psum_tensor(f"ff{layer}_pA", [P, 2, CH], F32))
        pY = ctx.enter_context(nc.psum_tensor(f"ff{layer}_pY", [P, CT, D], F32))
        w_in = ctx.enter_context(nc.semaphore(f"ff{layer}_w_in"))
        zeroed = ctx.enter_context(nc.semaphore(f"ff{layer}_zeroed"))
        full = (HB - 1) * P
        LOADS = 10

        def g(n):
            return n + base

        def early(n, k):
            return isinstance(n, int) and n < k

        def drive(eng, body):
            for n in range(2):
                body(n, n)
            with eng.Fori(1, NC // 2) as i:
                for p in range(2):
                    body(i * 2 + p, p)

        with nc.Block() as block:
            @block.sync
            def _(sp):
                sp.wait_ge(zeroed, 3)
                loads = [
                    (w2[:, 0:HB - 1, :], a["L0_ffn_w2"][layer, 0:full].rearrange("(k p) n -> p k n", p=P)),
                    (w2[0:HL, HB - 1, :], a["L0_ffn_w2"][layer, full:HID]),
                    (b2[:], a["L0_ffn_b2"][layer:layer + 1, :].to_broadcast([P, D])),
                ]
                for half in range(2):
                    loads.append((w1[:, :, half, 0:HID],
                                  a["L0_ffn_w1"][layer, :, half * HID:(half + 1) * HID]
                                  .rearrange("(k p) n -> p k n", p=P)))
                for d_, s_ in loads:
                    sp.dma_start(d_, s_).then_inc(w_in, 16)
                with nc.allow_non_contiguous_dma(reason="short vectors, once per layer"):
                    for half in range(2):
                        row = a["L0_ffn_b1"][layer, half * HID:(half + 1) * HID]
                        sp.dma_start(b1[:, half, 0:HB - 1],
                                     row[0:full].rearrange("(k p) -> p k", p=P)).then_inc(w_in, 16)
                        sp.dma_start(b1[0:HL, half, HB - 1:HB],
                                     row[full:HID].rearrange("(p k) -> p k", k=1)).then_inc(w_in, 16)
                    sp.dma_start(lg[:], a["L0_ffn_ln_g"][layer].rearrange("(k p) -> p k", p=P)).then_inc(w_in, 16)
                    sp.dma_start(lb[:], a["L0_ffn_ln_b"][layer].rearrange("(k p) -> p k", p=P)).then_inc(w_in, 16)

                def load(n, p):
                    if not early(n, 2):
                        sp.wait_ge(s["normed"].sem, s["normed"].upto(g(n - 2)))
                        sp.wait_ge(s["biased"].sem, s["biased"].upto(g(n - 2)))
                    sp.dma_start(hx[:, p, :, 0:P], rows(lo_s, n)).then_inc(s["x_in"].sems[p], 16)
                    sp.dma_start(hx[:, p, :, P:D], shifted(hi_s, n, CH)).then_inc(s["x_in"].sems[p], 16)
                    sp.dma_start(xo[:, p], padded(hi_s, n, CH)).then_inc(s["x_in"].sems[p], 16)

                def load_last(n, p):
                    if not early(n, 2):
                        sp.wait_ge(s["final"].sem, s["final"].upto(n - 2))
                    sp.dma_start(x1[:, p], rows(x1_d, n)).then_inc(s["last_in"].sems[p], 16)
                    src_ = mod_d[bass.ds(n // 2, 1), 5, :].to_broadcast([P, D])
                    sp.dma_start(gb[:, p, :], src_).then_inc(s["last_in"].sems[p], 16)

                def store(n, p):
                    if final:
                        sp.wait_ge(s["final"].sem, s["final"].upto(n))
                        for half in range(2):
                            sp.dma_start(rows(out, n)[:, 2 * half:2 * half + 2],
                                         yo[:, p, 2 * half:2 * half + 2]).then_inc(s["stored"].sems[p], 16)
                    else:
                        sp.wait_ge(s["summed"].sem, s["summed"].upto(g(n)))
                        sp.dma_start(rows(dst[0], n), y[:, p, :, 0:P]).then_inc(s["stored"].sems[p], 16)
                        sp.dma_start(padded(dst[1], n, CH), y[:, p, :, P:D]).then_inc(s["stored"].sems[p], 16)

                load(0, 0)
                load(1, 1)
                if final:
                    load_last(0, 0)
                    load_last(1, 1)
                with sp.Fori(0, NC // 2 - 1) as i:
                    for p in range(2):
                        load(i * 2 + 2 + p, p)
                        store(i * 2 + p, p)
                        if final:
                            load_last(i * 2 + 2 + p, p)
                store(NC - 2, 0)
                store(NC - 1, 1)
                sp.wait_ge(s["stored"].sems[0], s["stored"].upto(g(NC - 2)))
                sp.wait_ge(s["stored"].sems[1], s["stored"].upto(g(NC - 1)))

            @block.vector
            def _(dve):
                nc.vector.memset(w1[:, :, :, full:HB * P], 0.0).then_inc(zeroed, 1)
                nc.vector.memset(w2[:, HB - 1, :], 0.0).then_inc(zeroed, 1)
                nc.vector.memset(b1[:], 0.0).then_inc(zeroed, 1)

                def norm(n, p, steps):
                    c = s["chain"]
                    if steps[0] == 0:
                        dve.wait_ge(s["x_in"].sems[p], s["x_in"].upto(g(n)))
                    layer_norm_steps(nc, dve, c, g(n), [k for k in steps if k < LN_INCS], hx[:, p], stats, mv, ve[:],
                                     rstd[:], tmp[:])
                    if steps[-1] == LN_INCS:
                        dve.wait_ge(c.sem, c.upto(g(n)))
                        if not early(n, 2):
                            dve.wait_ge(s["turned"].sem, s["turned"].upto(g(n - 2)))
                        for t in range(CT):
                            last = nc.vector.tensor_scalar(hn[:, p, t, :], hx[:, p, t, :], mv[:, t, 0:1],
                                                           rstd[:, t:t + 1], ALU.subtract, ALU.mult)
                        last.then_inc(s["normed"].sem, 1)

                def mix(n, j):
                    dve.wait_ge(s["gelu"].sem, s["gelu"].upto(g(n), j + 1))
                    dve.wait_ge(s["lifted"].sem, s["lifted"].upto(g(n), j + 1))
                    if j == 0 and not early(n, 1):
                        dve.wait_ge(s["y_done"].sem, s["y_done"].upto(g(n - 1)))
                    nc.vector.scalar_tensor_tensor(out=u[:, j, :], in0=pA[:, j % 2, :], scalar=b1[:, 0, j:j + 1],
                                                   in1=gl[:, j % 2, :], op0=ALU.add,
                                                   op1=ALU.mult).then_inc(s["mixed"].sem, 1)

                def finish(n, p):
                    dve.wait_ge(s["y_done"].sem, s["y_done"].upto(g(n)))
                    dve.wait_ge(s["biased"].sem, s["biased"].upto(g(n)))
                    if not early(n, 2):
                        if final:
                            dve.wait_ge(s["final"].sem, s["final"].upto(n - 2))
                        else:
                            dve.wait_ge(s["stored"].sems[p], s["stored"].upto(g(n - 2)))
                    nc.vector.tensor_tensor(y[:, p], pY[:], xb[:, p], ALU.add).then_inc(s["summed"].sem, 1)

                NORM_PARTS = (range(0, 1), range(1, 4), range(4, 8), range(8, 12), range(12, LN_INCS + 1))

                def body(n, p, following=True):
                    for j in range(HB):
                        mix(n, j)
                        if following and j < len(NORM_PARTS):
                            norm(n + 1, 1 - p, NORM_PARTS[j])
                    finish(n, p)

                norm(0, 0, range(LN_INCS + 1))
                dve.wait_ge(w_in, 16 * 11)
                for n in range(2):
                    body(n, n)
                with dve.Fori(1, NC // 2 - 1) as i:
                    for p in range(2):
                        body(i * 2 + p, p)
                body(NC - 2, 0)
                body(NC - 1, 1, following=False)

            @block.gpsimd
            def _(pool):
                pool.wait_ge(w_in, 16 * 11)

                def body(n, p):
                    pool.wait_ge(s["x_in"].sems[p], s["x_in"].upto(g(n)))
                    if not early(n, 2):
                        pool.wait_ge(s["summed"].sem, s["summed"].upto(g(n - 2)))
                    for half, x in ((0, hx[:, p, :, 0:P]), (1, xo[:, p])):
                        nc.gpsimd.tensor_tensor(xb[:, p, :, half * P:(half + 1) * P], x,
                                                b2[:, half * P:(half + 1) * P].unsqueeze(1).to_broadcast([P, CT, P]),
                                                ALU.add).then_inc(s["biased"].sem, 1)
                    if final:
                        pool.wait_ge(s["summed"].sem, s["summed"].upto(g(n)))
                        pool.wait_ge(s["last_in"].sems[p], s["last_in"].upto(n))
                        if not early(n, 1):
                            pool.wait_ge(s["final"].sem, s["final"].upto(n - 1))
                        nc.gpsimd.tensor_tensor(yg[:], y[:, p], gb[:, p, :].unsqueeze(1).to_broadcast([P, CT, D]),
                                                ALU.mult).then_inc(s["scaled"].sem, 1)
                        pool.wait_ge(s["scaled"].sem, s["scaled"].upto(n))
                        if not early(n, 2):
                            pool.wait_ge(s["stored"].sems[p], s["stored"].upto(g(n - 2)))
                        nc.gpsimd.tensor_tensor(yo[:, p], yg[:], x1[:, p], ALU.add).then_inc(s["final"].sem, 1)

                drive(pool, body)

            @block.tensor
            def _(pe):
                pe.wait_ge(w_in, 16 * 11)

                def turn(n, p):
                    pe.wait_ge(s["normed"].sem, s["normed"].upto(g(n)))
                    if not early(n, 1):
                        pe.wait_ge(s["hT_ready"].sem, s["hT_ready"].upto(g(n - 1)))
                    for t in range(CT):
                        for k in range(KT):
                            last = nc.tensor.transpose(pH[:, k, t * P:(t + 1) * P],
                                                       hn[:, p, t, k * P:(k + 1) * P], ident[:])
                    last.then_inc(s["turned"].sem, 1)

                def up(n, p):
                    pe.wait_ge(s["hT_ready"].sem, s["hT_ready"].upto(g(n)))
                    for j in range(HB):
                        for half, ps, done, freed in ((1, pG, "gated", "gelu"), (0, pA, "lifted", "mixed")):
                            if not (early(n, 1) and layer == 0 and j < 2):
                                pe.wait_ge(s[freed].sem, g(n) * HB + j - 1)
                            for k in range(KT):
                                last = nc.tensor.matmul(ps[:, j % 2, :], w1[:, k, half, j * P:(j + 1) * P],
                                                        hT[:, p, k, :], start=(k == 0), stop=(k == KT - 1))
                            last.then_inc(s[done].sem, 1)

                def down(n, p):
                    pe.wait_ge(s["mixed"].sem, s["mixed"].upto(g(n)))
                    if not early(n, 1):
                        pe.wait_ge(s["summed"].sem, s["summed"].upto(g(n - 1)))
                    for t in range(CT):
                        for j in range(HB):
                            last = nc.tensor.matmul(pY[:, t, :], u[:, j, t * P:(t + 1) * P], w2[:, j, :],
                                                    start=(j == 0), stop=(j == HB - 1))
                    last.then_inc(s["y_done"].sem, 1)

                turn(0, 0)
                for n in range(2):
                    up(n, n)
                    turn(n + 1, (n + 1) % 2)
                    down(n, n)
                with pe.Fori(0, NC // 2 - 2) as i:
                    for p in range(2):
                        up(i * 2 + 2 + p, p)
                        turn(i * 2 + 3 + p, 1 - p)
                        down(i * 2 + 2 + p, p)
                up(NC - 2, 0)
                turn(NC - 1, 1)
                down(NC - 2, 0)
                up(NC - 1, 1)
                down(NC - 1, 1)

            @block.scalar
            def _(act):
                act.wait_ge(w_in, 16 * 11)

                def h_out(n, p):
                    act.wait_ge(s["turned"].sem, s["turned"].upto(g(n)))
                    if not early(n, 2):
                        act.wait_ge(s["lifted"].sem, s["lifted"].upto(g(n - 2)))
                    for k in range(KT):
                        nc.scalar.activation(hT[:, p, k, :], pH[:, k, :], ACT.Identity, bias=lb[:, k:k + 1],
                                             scale=lg[:, k:k + 1]).then_inc(s["hT_ready"].sem, 1)

                def gelus(n, p):
                    for j in range(HB):
                        act.wait_ge(s["gated"].sem, s["gated"].upto(g(n), j + 1))
                        if not (early(n, 1) and layer == 0 and j < 2):
                            act.wait_ge(s["mixed"].sem, g(n) * HB + j - 1)
                        nc.scalar.activation(gl[:, j % 2, :], pG[:, j % 2, :], ACT.Gelu,
                                             bias=b1[:, 1, j:j + 1]).then_inc(s["gelu"].sem, 1)

                h_out(0, 0)
                for n in range(2):
                    gelus(n, n)
                    h_out(n + 1, (n + 1) % 2)
                with act.Fori(0, NC // 2 - 2) as i:
                    for p in range(2):
                        gelus(i * 2 + 2 + p, p)
                        h_out(i * 2 + 3 + p, 1 - p)
                gelus(NC - 2, 0)
                h_out(NC - 1, 1)
                gelus(NC - 1, 1)


_INS = ["L0_attn_x", "L0_attn_wq", "L0_attn_wk_a", "L0_attn_wk_b", "L0_attn_wv_a", "L0_attn_wv_b", "L0_attn_wo",
        "L0_ffn_wqkv", "L0_ffn_q_scale", "L0_ffn_k_scale", "L0_ffn_wo", "L0_ffn_ln_g", "L0_ffn_ln_b", "L0_ffn_w1",
        "L0_ffn_b1", "L0_ffn_w2", "L0_ffn_b2", "L0_c", "L0_wmod"]


def kernel(**inputs):
    import concourse.bacc as bacc
    from concourse.bass_utils import run_bass_kernel_spmd

    nc = bacc.Bacc("TRN2", target_bir_lowering=False, num_devices=1)
    given = {name: np.ascontiguousarray(inputs[name]) for name in _INS}
    given.update(constants())
    arrays, args = {}, {}
    for name, array in given.items():
        arrays[f"in_{name}"] = array
        args[name] = nc.dram_tensor(f"in_{name}", array.shape, mybir.dt.from_np(array.dtype),
                                    kind="ExternalInput").ap()
    out = nc.dram_tensor("out", (B, N, D), F32, kind="ExternalOutput").ap()
    build(nc, args, out)
    r = run_bass_kernel_spmd(nc, [arrays], core_ids=[0])
    return r.results[0]["out"]
```

```python
from contextlib import ExitStack

import numpy as np

import concourse.bass as bass
from concourse import mybir

ALU = mybir.AluOpType
ACT = mybir.ActivationFunctionType
AX = mybir.AxisListType
F32 = mybir.dt.float32
BF16 = mybir.dt.bfloat16
F32R = mybir.dt.float32r
I32 = mybir.dt.int32

P = 128
B, N, D = 8, 1024, 256
KT = D // P
NH, HD = 16, 16
LAT = 64
DEPTH, HEADS, DH = 2, 8, 64
WIN = 128
NW = N // WIN
INNER = HEADS * DH
HID = D * 4 * 2 // 3
HB = -(-HID // P)
HL = HID - (HB - 1) * P
QK_SCALE = 8.0
LN_EPS = 1e-5
NORM_FLOOR = 1e-24
CT = 4
CH = CT * P
NC = B * N // CH
MASKED = 3.0e38
GH = 4
NG = NH // GH
GROUPS = B * NG
Q_PARTS = (0, 1, 2, 0, 1, 0)
K_PARTS = (0, 0, 0, 1, 1, 2)
SROWS = len(Q_PARTS) * HD
RSQRT_SEED = 1597463007.0
HALF_RSQRT_SEED = RSQRT_SEED - 2.0 ** 22
RSQRT_STEPS = 3
RSQRT_INCS = 1 + 3 * RSQRT_STEPS
POOL_RSQRT_INCS = 4 * RSQRT_STEPS
SPLIT_PRODUCTS = ((0, 0), (0, 1), (1, 0))
WIN_BUFS = 4


class Signal:

    def __init__(self, sem, per=1):
        self.sem, self.per, self.k = sem, per, 0

    def upto(self, n, c=None):
        return n * self.per + (self.per if c is None else c)

    def begin(self):
        self.k = 0

    def counted(self):
        self.k += 1
        return self.sem

    def so_far(self, n):
        return n * self.per + self.k


def rsqrt_step(nc, k, x, y, t):
    if k == 0:
        return nc.vector.tensor_scalar(y.bitcast(I32), x.bitcast(I32), -0.5, RSQRT_SEED, ALU.mult, ALU.add)
    if k % 3 == 1:
        return nc.vector.scalar_tensor_tensor(out=t, in0=y, scalar=-0.5, in1=y, op0=ALU.mult, op1=ALU.mult)
    if k % 3 == 2:
        return nc.vector.tensor_tensor(t, t, x, ALU.mult)
    return nc.vector.scalar_tensor_tensor(out=y, in0=t, scalar=1.5, in1=y, op0=ALU.add, op1=ALU.mult)


class Arrivals:

    def __init__(self, sems, per):
        self.sems, self.per = sems, per

    def upto(self, n):
        return n // len(self.sems) * self.per + self.per



def constants():
    f = np.float32
    ident = np.eye(P, dtype=f)
    inv = f(1.0) / f(10000.0) ** (np.arange(0, HD, 2, dtype=f) / f(HD))
    ang = np.arange(NH, dtype=f)[:, None] * inv[None, :]
    rope = np.stack([np.cos(ang).reshape(-1), np.sin(ang).reshape(-1)]).astype(f)
    half = np.arange(0, DH, 2, dtype=f)
    inv2 = f(1.0) / f(10000.0) ** (half / f(DH))
    t = np.arange(N, dtype=f)
    fr = t[:, None] * inv2[None, :]
    fr = np.concatenate([fr, fr], -1)
    base = (half + f(0.4 * DH)) / f(1.4 * DH)
    power = (t - f(N // 2)) / f(WIN // 2)
    xs = base[None, :] ** power[:, None]
    xs = np.concatenate([xs, xs], -1)
    sgn = np.concatenate([-np.ones(DH // 2, f), np.ones(DH // 2, f)])
    c, s = np.cos(fr), np.sin(fr) * sgn
    trig = np.concatenate([c * xs * f(-QK_SCALE), c / xs, s * xs * f(-QK_SCALE), s / xs], -1).astype(f)
    trig = trig.reshape(NW, P, 4 * DH)
    i, j = np.arange(P)[:, None], np.arange(P)[None, :]
    own = np.where(j <= i, 0.0, MASKED)
    prev = np.where(j >= i, 0.0, MASKED)
    mask = np.stack([np.concatenate([prev if w else np.full((P, P), MASKED), own], 1) for w in range(2)])
    return {"ident": ident, "rope": rope, "trig": trig, "mask": mask.astype(f)}


def build(nc, a, out):
    with ExitStack() as ctx:
        def dram(name, shape, dt=F32):
            return nc.dram_tensor(name, shape, dt, kind="Internal").ap()

        mod_d = dram("mod_d", [B, 6, D])
        parts_d = dram("parts_d", [2, 3, D, B, N], BF16)
        v_d = dram("v_d", [B, N, NH * 2 * HD])
        att_d = dram("att_d", [B, N, D])
        x1_d = dram("x1_d", [B, N, D])
        lo_d = [dram(f"lo{s}_d", [B, N, P]) for s in range(2 * DEPTH)]
        hi_d = [dram(f"hi{s}_d", [B, 1 + N, P]) for s in range(2 * DEPTH)]
        trig_d = dram("trig_d", [DEPTH, NW, P, 4 * DH])

        ident = ctx.enter_context(nc.sbuf_tensor("ident", [P, P], F32))
        identb = ctx.enter_context(nc.sbuf_tensor("identb", [P, P], BF16))
        with ExitStack() as first:
            w = {
                "wq": first.enter_context(nc.sbuf_tensor("wqT", [P, KT, D], F32)),
                "wa": first.enter_context(nc.sbuf_tensor("waT", [P, KT, P], F32)),
                "wkb": first.enter_context(nc.sbuf_tensor("wkbT", [P, D], F32)),
                "wvb": first.enter_context(nc.sbuf_tensor("wvbT", [P, D], F32)),
                "wo": first.enter_context(nc.sbuf_tensor("woT", [P, KT, D], F32)),
            }
            setup(nc, a, ident, identb, w, mod_d, trig_d, hi_d)
            projections(nc, a["L0_attn_x"], ident, w, mod_d, parts_d, v_d)
            full_attention(nc, ident, identb, parts_d, v_d, att_d)
            attention_out(nc, a["L0_attn_x"], ident, w, mod_d, att_d, x1_d, lo_d[0], hi_d[0])
        window_sems = ExitStack()
        with window_sems:
            ws = window_signals(nc, window_sems)
            fs = ffn_signals(nc, window_sems)
            for layer in range(DEPTH):
                s = 2 * layer
                window_attention(nc, a, layer, ident, trig_d, (lo_d[s], hi_d[s]), (lo_d[s + 1], hi_d[s + 1]), ws)
                last = layer == DEPTH - 1
                dst = None if last else (lo_d[s + 2], hi_d[s + 2])
                feed_forward(nc, a, layer, ident, (lo_d[s + 1], hi_d[s + 1]), dst, x1_d, mod_d, out, fs)


def rows(x, n):
    flat = x.rearrange("b n c -> (b n) c").rearrange("(q t p) c -> q p t c", p=P, t=CT)
    return flat[bass.ds(n, 1)].rearrange("q p t c -> (q p) t c")


def shifted(x, n, unit):
    per = N // unit
    flat = x[bass.ds(n // per, 1), bass.ds((n % per) * unit, unit), :]
    return flat.rearrange("b (t p) c -> p (b t) c", p=P)


def padded(x, n, unit):
    per = N // unit
    flat = x[bass.ds(n // per, 1), bass.ds((n % per) * unit + 1, unit), :]
    return flat.rearrange("b (t p) c -> p (b t) c", p=P)


def setup(nc, a, ident, identb, w, mod_d, trig_d, hi_d):
    with ExitStack() as ctx:
        def sb(name, shape, dt=F32):
            return ctx.enter_context(nc.sbuf_tensor(name, shape, dt))

        def sem(name):
            return ctx.enter_context(nc.semaphore(name))

        wq_r = sb("wq_r", [P, KT, D])
        wo_r = sb("wo_r", [P, KT, D])
        wa_r = sb("wa_r", [P, D])
        wb_r = sb("wb_r", [P, KT, P])
        rope = sb("rope_b", [P, 2, P])
        ropeq = sb("rope_q", [P, 2, P])
        ta, tb = sb("rope_ta", [P, KT, P]), sb("rope_tb", [P, KT, P])
        cs = sb("c_rows", [B, D])
        ce = sb("c_exp", [B, D])
        cT = sb("c_T", [P, KT, B])
        wmod = sb("wmod_sb", [P, KT, 6 * D])
        mods = sb("mods", [B, 6, D])
        ga, gs = sb("guard_a", [B, 2, D]), sb("guard_s", [B, 2, D])
        trig = sb("trig_base", [P, NW, 4 * DH])
        qks = sb("qk_scales", [P, DEPTH, 4 * DH])
        trl = sb("trig_scaled", [P, DEPTH, NW, 4 * DH])
        zrow = sb("zero_rows", [B, P])
        ps = [ctx.enter_context(nc.psum_tensor(f"ps_set{i}", [P, 512], F32)) for i in range(8)]
        loaded, turned, steps, silu, stored = (sem("set_loaded"), sem("set_turned"), sem("set_steps"),
                                               sem("set_silu"), sem("set_stored"))
        small, modm = sem("set_small"), sem("set_mod")
        n_loads = [0]

        with nc.Block() as block:
            @block.sync
            def _(sp):
                def load(dst, src):
                    sp.dma_start(dst, src).then_inc(loaded, 16)
                    n_loads[0] += 16

                load(ident[:], a["ident"])
                load(cs[:], a["L0_c"])
                load(wmod[:], a["L0_wmod"].rearrange("(k p) n -> p k n", p=P))
                load(wq_r[:], a["L0_attn_wq"].rearrange("(m p) c -> p m c", p=P))
                load(wo_r[:], a["L0_attn_wo"].rearrange("(m p) c -> p m c", p=P))
                load(wa_r[0:LAT, :], a["L0_attn_wk_a"])
                load(wa_r[LAT:P, :], a["L0_attn_wv_a"])
                load(wb_r[:, :, 0:LAT], a["L0_attn_wk_b"].rearrange("(m p) c -> p m c", p=P))
                load(wb_r[:, :, LAT:P], a["L0_attn_wv_b"].rearrange("(m p) c -> p m c", p=P))
                load(rope[:], a["rope"].rearrange("(o t) i -> o t i", o=1).to_broadcast([P, 2, P]))
                load(trig[:], a["trig"].rearrange("w p c -> p w c"))
                hd = DH // 2
                for layer in range(DEPTH):
                    for which, name in enumerate(("L0_ffn_q_scale", "L0_ffn_k_scale")):
                        src = a[name][layer:layer + 1, :]
                        at = which * DH
                        load(qks[:, layer, at:at + DH], src.to_broadcast([P, DH]))
                        at += 2 * DH
                        load(qks[:, layer, at:at + hd], src[:, hd:DH].to_broadcast([P, hd]))
                        load(qks[:, layer, at + hd:at + DH], src[:, 0:hd].to_broadcast([P, hd]))
                sp.wait_ge(small, 1)
                for h in hi_d:
                    sp.dma_start(h[:, 0, :], zrow[:]).then_inc(stored, 16)
                sp.wait_ge(small, 2 + DEPTH)
                sp.dma_start(trig_d.rearrange("l w p c -> p (l w) c"),
                             trl[:].rearrange("p l w c -> p (l w) c")).then_inc(stored, 16)
                sp.wait_ge(modm, 1)
                sp.dma_start(mod_d, mods[:]).then_inc(stored, 16)
                sp.wait_ge(stored, 16 * (len(hi_d) + 2))

            total = n_loads[0]

            @block.scalar
            def _(act):
                act.wait_ge(loaded, total)
                nc.scalar.activation(ce[:], cs[:], ACT.Exp, scale=-1.0).then_inc(silu, 1)

            @block.tensor
            def _(pe):
                pe.wait_ge(loaded, total)
                for k in range(KT):
                    for m in range(KT):
                        nc.tensor.transpose(ps[0][:, k * D + m * P:k * D + (m + 1) * P],
                                            wq_r[:, m, k * P:(k + 1) * P], ident[:])
                        nc.tensor.transpose(ps[1][:, k * D + m * P:k * D + (m + 1) * P],
                                            wo_r[:, m, k * P:(k + 1) * P], ident[:])
                    nc.tensor.transpose(ps[2][:, k * P:(k + 1) * P], wa_r[:, k * P:(k + 1) * P], ident[:])
                    last = nc.tensor.transpose(ps[3][:, k * P:(k + 1) * P], wb_r[:, k, :], ident[:])
                last.then_inc(turned, 1)
                pe.wait_ge(silu, 2)
                for k in range(KT):
                    last = nc.tensor.transpose(ps[4][:, k * B:(k + 1) * B], cs[:, k * P:(k + 1) * P],
                                               ident[0:B, 0:B])
                last.then_inc(turned, 1)
                pe.wait_ge(silu, 3)
                for j in range(3):
                    for k in range(KT):
                        last = nc.tensor.matmul(ps[5 + j][0:B, :], cT[:, k, :], wmod[:, k, j * 512:(j + 1) * 512],
                                                start=(k == 0), stop=(k == KT - 1))
                last.then_inc(turned, 1)

            @block.vector
            def _(dve):
                count = [0]

                def link(ins):
                    ins.then_inc(steps, 1)
                    count[0] += 1
                    dve.wait_ge(steps, count[0])

                link(nc.vector.memset(w["wkb"][:], 0.0))
                link(nc.vector.memset(w["wvb"][:], 0.0))
                nc.vector.memset(zrow[:], 0.0).then_inc(small, 1)
                dve.wait_ge(loaded, total)
                nc.vector.tensor_copy(identb[:], ident[:]).then_inc(small, 1)
                for layer in range(DEPTH):
                    nc.vector.tensor_tensor(trl[:, layer], trig[:],
                                            qks[:, layer, :].unsqueeze(1).to_broadcast([P, NW, 4 * DH]),
                                            ALU.mult).then_inc(small, 1)
                dve.wait_ge(silu, 1)
                link(nc.vector.tensor_scalar(ce[:], ce[:], 1.0, None, ALU.add))
                link(nc.vector.reciprocal(ce[:], ce[:]))
                nc.vector.tensor_tensor(cs[:], cs[:], ce[:], ALU.mult).then_inc(silu, 1)
                dve.wait_ge(turned, 2)
                nc.vector.tensor_copy(cT[:], ps[4][:, 0:KT * B].rearrange("p (k b) -> p k b", k=KT)).then_inc(silu, 1)
                link(nc.vector.tensor_scalar(ropeq[:], rope[:], float(HD) ** -0.5, None, ALU.mult))

                def rotate(dst, src, table, k):
                    cos = table[:, 0, :].unsqueeze(1).to_broadcast([table.shape[0], k, P])
                    sin = table[:, 1, :].unsqueeze(1).to_broadcast([table.shape[0], k, P])
                    pa, pb = ta[0:table.shape[0], 0:k, :], tb[0:table.shape[0], 0:k, :]
                    link(nc.vector.tensor_tensor(pa, src[:, :, :, 0], cos, ALU.mult))
                    link(nc.vector.tensor_tensor(pb, src[:, :, :, 1], sin, ALU.mult))
                    link(nc.vector.tensor_tensor(dst[:, :, :, 0], pa, pb, ALU.subtract))
                    link(nc.vector.tensor_tensor(pa, src[:, :, :, 0], sin, ALU.mult))
                    link(nc.vector.tensor_tensor(pb, src[:, :, :, 1], cos, ALU.mult))
                    link(nc.vector.tensor_tensor(dst[:, :, :, 1], pa, pb, ALU.add))

                rotate(w["wq"][:].rearrange("p k (i e) -> p k i e", e=2),
                       ps[0][:].rearrange("p (k i e) -> p k i e", k=KT, e=2), ropeq, KT)
                rotate(w["wkb"][0:LAT, :].rearrange("p (k i e) -> p k i e", k=1, e=2),
                       ps[3][0:LAT, 0:D].rearrange("p (k i e) -> p k i e", k=1, e=2), rope[0:LAT], 1)
                link(nc.vector.tensor_copy(w["wvb"][LAT:P, :], ps[3][LAT:P, 0:D]))
                link(nc.vector.tensor_copy(w["wo"][:].rearrange("p k n -> p (k n)"), ps[1][:]))
                link(nc.vector.tensor_copy(w["wa"][:].rearrange("p k n -> p (k n)"), ps[2][:, 0:D]))
                dve.wait_ge(turned, 3)
                for j in range(3):
                    link(nc.vector.tensor_copy(mods[:, 2 * j:2 * j + 2, :],
                                               ps[5 + j][0:B, :].rearrange("p (k n) -> p k n", k=2)))
                scale, gate = mods[:, 1:6:3, :], mods[:, 2:6:3, :]
                link(nc.vector.tensor_scalar(scale, scale, 1.0, None, ALU.add))
                link(nc.vector.tensor_scalar(gs[:], gate, 0.0, 2.0, ALU.is_ge, ALU.mult))
                link(nc.vector.tensor_scalar(gs[:], gs[:], -1.0, None, ALU.add))
                link(nc.vector.tensor_scalar(ga[:], gate, -1.0, None, ALU.mult))
                link(nc.vector.tensor_tensor(ga[:], ga[:], gate, ALU.max))
                link(nc.vector.tensor_scalar(ga[:], ga[:], 0.25, None, ALU.max))
                nc.vector.tensor_tensor(gate, ga[:], gs[:], ALU.mult).then_inc(modm, 1)


def layer_norm_steps(nc, dve, chain, n, steps, x, stats, mv, ve, rstd, tmp):
    for k in steps:
        if k > 0:
            dve.wait_ge(chain.sem, chain.upto(n, k))
        if k == 0:
            for t in range(x.shape[1]):
                last = nc.vector.bn_stats(stats[:, t, :], x[:, t, :])
        elif k == 1:
            nc.vector.memset(tmp, 0.0)
            for t in range(x.shape[1]):
                last = nc.vector.bn_aggr(mv[:, t, :], stats[:, t, :])
        elif k == 2:
            last = nc.vector.tensor_scalar(ve, mv[:, :, 1], LN_EPS, None, ALU.add)
        else:
            last = rsqrt_step(nc, k - 3, ve, rstd, tmp)
        last.then_inc(chain.sem, 1)


LN_INCS = 3 + RSQRT_INCS


def projections(nc, x, ident, w, mod_d, parts_d, v_d):
    with ExitStack() as ctx:
        def sb(name, shape, dt=F32):
            return ctx.enter_context(nc.sbuf_tensor(name, shape, dt))

        def sig(name, per=1):
            return Signal(ctx.enter_context(nc.semaphore("pj_" + name)), per)

        def arrivals(name, per, bufs=2):
            return Arrivals([ctx.enter_context(nc.semaphore(f"pj_{name}{p}")) for p in range(bufs)], per)

        R = 4
        xt = sb("pj_x", [P, R, CT, D])
        mrow = sb("pj_mod", [P, R, 2, D])
        stats, mv = sb("pj_stats", [P, CT, 6]), sb("pj_mv", [P, CT, 2])
        ve, rstd, tmp = sb("pj_ve", [P, CT]), sb("pj_rstd", [P, CT]), sb("pj_tmp", [P, CT])
        xn = sb("pj_xn", [P, 2, CT, D])
        hm = sb("pj_hm", [P, 2, CT, D])
        hT = sb("pj_hT", [P, 2, KT, CH])
        lat = sb("pj_lat", [P, 2, CH])
        parts = sb("pj_parts", [P, 2, 2, 3, KT, CH], BF16)
        res = sb("pj_res", [P, 2, KT, CH])
        vs = sb("pj_v", [P, 2, CT, NH, 2 * HD])
        pH = ctx.enter_context(nc.psum_tensor("pj_pH", [P, KT, CH], F32))
        pL = ctx.enter_context(nc.psum_tensor("pj_pL", [P, 2, CH], F32))
        pQ = ctx.enter_context(nc.psum_tensor("pj_pQ", [P, KT, CH], F32))
        pK = ctx.enter_context(nc.psum_tensor("pj_pK", [P, KT, CH], F32))

        loaded = arrivals("loaded", 32, R)
        chain = sig("chain", LN_INCS)
        normed = sig("normed")
        modded = sig("modded", 2)
        turned = sig("turned")
        h_ready = sig("h_ready")
        lat_done, lat_ready = sig("lat_done"), sig("lat_ready")
        q_done, k_done, v_done = sig("q_done"), sig("k_done"), sig("v_done", 2)
        hi_ready = sig("hi_ready", 2)
        split = sig("split", 4)
        lows = sig("lows", 2)
        v_ready = sig("v_ready", 2)
        stored = arrivals("stored", 16 * 7)
        ones = sig("ones")

        def pairs(eng, body):
            for n in range(2):
                body(n, n)
            with eng.Fori(1, NC // 2 - 1) as i:
                for p in range(2):
                    body(i * 2 + p, p)
            for n in range(NC - 2, NC):
                body(n, n % 2, following=n + 1 < NC)

        def rounds(eng, body):
            for n in range(R):
                body(n, n)
            with eng.Fori(1, NC // R - 1) as i:
                for r in range(R):
                    body(i * R + r, r)
            for n in range(NC - R, NC):
                body(n, n % R, following=n + 2 < NC)

        def later(n):
            return not isinstance(n, int) or n >= 2

        def again(n):
            return not isinstance(n, int) or n >= 1

        with nc.Block() as block:
            @block.sync
            def _(sp):
                def load(n, p):
                    if not isinstance(n, int):
                        sp.wait_ge(normed.sem, normed.upto(n - R))
                        sp.wait_ge(modded.sem, modded.upto(n - R))
                    sp.dma_start(xt[:, p], rows(x, n)).then_inc(loaded.sems[p], 16)
                    src = mod_d[bass.ds(n // 2, 1), 0:2, :].to_broadcast([P, 2, D])
                    sp.dma_start(mrow[:, p], src).then_inc(loaded.sems[p], 16)

                def store(n, p):
                    sp.wait_ge(lows.sem, lows.upto(n))
                    for qk in range(2):
                        for part in range(3):
                            dst = parts_d[qk, part].rearrange("(m p) b t -> p m b t", p=P)
                            dst = dst[:, :, bass.ds(n // 2, 1), bass.ds((n % 2) * CH, CH)]
                            sp.dma_start(dst.rearrange("p m b t -> p m (b t)"),
                                         parts[:, p, qk, part]).then_inc(stored.sems[p], 16)
                    sp.wait_ge(v_ready.sem, v_ready.upto(n))
                    sp.dma_start(rows(v_d, n), vs[:, p].rearrange("p t h c -> p t (h c)")).then_inc(stored.sems[p], 16)

                for n in range(R):
                    load(n, n)
                with sp.Fori(0, NC // R - 1) as i:
                    for r in range(R):
                        store(i * R + r, r % 2)
                        load(i * R + R + r, r)
                for n in range(NC - R, NC):
                    store(n, n % 2)
                sp.wait_ge(stored.sems[0], stored.upto(NC - 2))
                sp.wait_ge(stored.sems[1], stored.upto(NC - 1))

            @block.vector
            def _(dve):
                nc.vector.memset(vs[:, :, :, :, HD:2 * HD], 1.0).then_inc(ones.sem, 1)

                def stats_of(n, r, steps):
                    if steps[0] == 0:
                        dve.wait_ge(loaded.sems[r], loaded.upto(n))
                    layer_norm_steps(nc, dve, chain, n, steps, xt[:, r], stats, mv, ve[:], rstd[:], tmp[:])

                def normalize(n, r):
                    dve.wait_ge(chain.sem, chain.upto(n))
                    if later(n):
                        dve.wait_ge(modded.sem, modded.upto(n - 2))
                    for t in range(CT):
                        last = nc.vector.tensor_scalar(xn[:, r % 2, t, :], xt[:, r, t, :], mv[:, t, 0:1],
                                                       rstd[:, t:t + 1], ALU.subtract, ALU.mult)
                    last.then_inc(normed.sem, 1)

                def rest(n, p, qk):
                    dve.wait_ge(hi_ready.sem, hi_ready.upto(n, qk + 1))
                    if again(n):
                        dve.wait_ge(lows.sem, lows.upto(n - 1, qk + 1))
                    nc.vector.tensor_tensor(res[:, qk], (pQ, pK)[qk][:], parts[:, p, qk, 0],
                                            ALU.subtract).then_inc(split.sem, 1)

                def second(n, p, qk):
                    dve.wait_ge(split.sem, split.upto(n, 2 * qk + 1))
                    if later(n) and qk == 0:
                        dve.wait_ge(stored.sems[p], stored.upto(n - 2))
                    nc.vector.tensor_copy(parts[:, p, qk, 1], res[:, qk]).then_inc(split.sem, 1)

                def body(n, r, following=True):
                    if following:
                        stats_of(n + 2, (r + 2) % R, range(0, 4))
                    rest(n, r % 2, 0)
                    if following:
                        stats_of(n + 2, (r + 2) % R, range(4, 6))
                    second(n, r % 2, 0)
                    if following:
                        stats_of(n + 2, (r + 2) % R, range(6, 8))
                    rest(n, r % 2, 1)
                    if following:
                        stats_of(n + 2, (r + 2) % R, range(8, 10))
                    second(n, r % 2, 1)
                    if following:
                        stats_of(n + 2, (r + 2) % R, range(10, LN_INCS))
                        normalize(n + 2, (r + 2) % R)

                for n in range(2):
                    stats_of(n, n, range(LN_INCS))
                    normalize(n, n)
                rounds(dve, body)

            @block.gpsimd
            def _(pool):
                def modulate(n, r):
                    p = r % 2
                    pool.wait_ge(normed.sem, normed.upto(n))
                    for t_in, t_out, row, op in ((xn, xn, 1, ALU.mult), (xn, hm, 0, ALU.add)):
                        if row == 0:
                            pool.wait_ge(modded.sem, modded.upto(n, 1))
                            if later(n):
                                pool.wait_ge(turned.sem, turned.upto(n - 2))
                        nc.gpsimd.tensor_tensor(t_out[:, p], t_in[:, p],
                                                mrow[:, r, row, :].unsqueeze(1).to_broadcast([P, CT, D]),
                                                op).then_inc(modded.sem, 1)

                def third(n, p, qk):
                    pool.wait_ge(split.sem, split.upto(n, 2 * qk + 2))
                    nc.gpsimd.tensor_tensor(parts[:, p, qk, 2], res[:, qk], parts[:, p, qk, 1],
                                            ALU.subtract).then_inc(lows.sem, 1)

                def body(n, r, following=True):
                    third(n, r % 2, 0)
                    third(n, r % 2, 1)
                    if following:
                        modulate(n + 2, (r + 2) % R)

                modulate(0, 0)
                modulate(1, 1)
                rounds(pool, body)

            @block.tensor
            def _(pe):
                def turn(n, p):
                    pe.wait_ge(modded.sem, modded.upto(n))
                    if again(n):
                        pe.wait_ge(h_ready.sem, h_ready.upto(n - 1))
                    for t in range(CT):
                        for k in range(KT):
                            last = nc.tensor.transpose(pH[:, k, t * P:(t + 1) * P],
                                                       hm[:, p, t, k * P:(k + 1) * P], ident[:])
                    last.then_inc(turned.sem, 1)

                def body(n, p, following=True):
                    pe.wait_ge(h_ready.sem, h_ready.upto(n))
                    if again(n):
                        pe.wait_ge(v_ready.sem, v_ready.upto(n - 1, 1))
                    for k in range(KT):
                        last = nc.tensor.matmul(pL[:, 0, :], w["wa"][:, k, :], hT[:, p, k, :],
                                                start=(k == 0), stop=(k == KT - 1))
                    last.then_inc(lat_done.sem, 1)
                    if again(n):
                        pe.wait_ge(split.sem, split.upto(n - 1, 1))
                    for m in range(KT):
                        for k in range(KT):
                            last = nc.tensor.matmul(pQ[:, m, :], w["wq"][:, k, m * P:(m + 1) * P], hT[:, p, k, :],
                                                    start=(k == 0), stop=(k == KT - 1))
                    last.then_inc(q_done.sem, 1)
                    pe.wait_ge(lat_ready.sem, lat_ready.upto(n))
                    if again(n):
                        pe.wait_ge(split.sem, split.upto(n - 1, 3))
                    for m in range(KT):
                        last = nc.tensor.matmul(pK[:, m, :], w["wkb"][:, m * P:(m + 1) * P], lat[:, p, :],
                                                start=True, stop=True)
                    last.then_inc(k_done.sem, 1)
                    if following:
                        turn(n + 1, 1 - p)
                    if again(n):
                        pe.wait_ge(v_ready.sem, v_ready.upto(n - 1))
                    for bank, t in ((0, 2), (0, 3), (1, 0), (1, 1)):
                        last = nc.tensor.matmul(pL[:, bank, (t % 2) * D:(t % 2 + 1) * D],
                                                lat[:, p, t * P:(t + 1) * P], w["wvb"][:], start=True, stop=True)
                        if t % 2 == 1:
                            last.then_inc(v_done.sem, 1)

                turn(0, 0)
                pairs(pe, body)

            @block.scalar
            def _(act):
                act.wait_ge(ones.sem, 1)

                def h_out(n, p):
                    act.wait_ge(turned.sem, turned.upto(n))
                    if later(n):
                        act.wait_ge(q_done.sem, q_done.upto(n - 2))
                    nc.scalar.copy(hT[:, p], pH[:]).then_inc(h_ready.sem, 1)

                def body(n, p, following=True):
                    act.wait_ge(lat_done.sem, lat_done.upto(n))
                    if later(n):
                        act.wait_ge(v_done.sem, v_done.upto(n - 2))
                    nc.scalar.copy(lat[:, p], pL[:, 0, :]).then_inc(lat_ready.sem, 1)
                    if later(n):
                        act.wait_ge(stored.sems[p], stored.upto(n - 2))
                    act.wait_ge(q_done.sem, q_done.upto(n))
                    nc.scalar.copy(parts[:, p, 0, 0], pQ[:]).then_inc(hi_ready.sem, 1)
                    act.wait_ge(k_done.sem, k_done.upto(n))
                    nc.scalar.copy(parts[:, p, 1, 0], pK[:]).then_inc(hi_ready.sem, 1)
                    if following:
                        h_out(n + 1, 1 - p)
                    for bank in range(2):
                        j = 1 - bank
                        act.wait_ge(v_done.sem, v_done.upto(n, bank + 1))
                        nc.scalar.copy(vs[:, p, 2 * j:2 * j + 2, :, 0:HD],
                                       pL[:, bank, :].rearrange("p (t h c) -> p t h c", t=2,
                                                                h=NH)).then_inc(v_ready.sem, 1)

                h_out(0, 0)
                pairs(act, body)


def full_attention(nc, ident, identb, parts_d, v_d, att_d):
    KB = N // P
    MAX_USES = 2 * GH * KB
    STEP_ROWS = MAX_USES // KB
    AHEAD = 2 * STEP_ROWS
    TURN = 2
    TURN_MAX = 1
    MROWS = 32
    NB = 3
    T = 3
    UNITS = 2 * GH

    with ExitStack() as ctx:
        def sb(name, shape, dt=F32):
            return ctx.enter_context(nc.sbuf_tensor(name, shape, dt))

        def sem(name):
            return ctx.enter_context(nc.semaphore("fa_" + name))

        Qs = sb("fa_Q", [P, NB, GH, N], BF16)
        Ks = sb("fa_K", [P, NB, GH, N], BF16)
        V = sb("fa_V", [P, NB, KB, GH, 2 * HD])
        Pr = sb("fa_P", [P, 2, GH, N])
        OT = sb("fa_OT", [P, N])
        mx = sb("fa_mx", [P, GH * KB, 2])
        nm = sb("fa_nm", [P, GH * KB])
        nb = sb("fa_nb", [P, KB, MROWS], BF16)
        nrow = sb("fa_nrow", [2 * MROWS, NB, N // 2], BF16)
        rec = sb("fa_rec", [P, 2, 4 * GH])
        att = sb("fa_att", [P, KB, GH * HD])
        pS = ctx.enter_context(nc.psum_tensor("fa_pS", [P, T, 512], F32))
        pR = ctx.enter_context(nc.psum_tensor("fa_pR", [P, T, 512], F32))
        pO = ctx.enter_context(nc.psum_tensor("fa_pO", [P, 2, 512], F32))

        stack_in = Arrivals([sem(f"stack_in{s}") for s in range(NB)], 16 * 12)
        v_in = Arrivals([sem(f"v_in{s}") for s in range(NB)], 16)
        max_in = Arrivals([sem(f"max_in{s}") for s in range(NB)], 64)
        ones = Signal(sem("ones"), 1)
        scored = Signal(sem("scored"), KB * UNITS)
        exped = Signal(sem("exped"), KB * UNITS)
        summed = Signal(sem("summed"), KB)
        o_out = Signal(sem("o_out"), 1)
        row_full, row_free = sem("row_full"), sem("row_free")
        neg = Signal(sem("neg"), 3)
        inverse = Signal(sem("inverse"), 2)
        stored = Signal(sem("stored"), 16)

        PROLOGUE = MAX_USES + TURN_MAX + AHEAD
        LOOPS = (GROUPS - 3) // NB

        def first_use(n):
            if isinstance(n, int) and n == 0:
                return PROLOGUE
            uses = PROLOGUE - TURN + (MAX_USES + TURN_MAX + TURN) * n
            return uses - AHEAD if is_last(n) else uses

        def divided(n):
            if is_last(n):
                at = first_use(n) + TURN
            else:
                at = first_use(n + 1) + (0 if is_last(n + 1) else 2 * STEP_ROWS)
            return at + TURN

        def maxima_out(n):
            if is_first(n):
                at = MAX_USES
            else:
                at = first_use(n - 1) + MAX_USES - AHEAD
                at = at + (0 if is_first(n - 1) else TURN) + (0 if is_last(n) else STEP_ROWS // 2)
            return at + TURN_MAX

        def tile_of(n, s, k):
            at = first_use(n) if isinstance(n, int) else PROLOGUE - TURN + (MAX_USES + TURN_MAX + TURN) * s
            return (at + k) % T

        def step_rows(n, s, k):
            ahead = 2 if k >= KB - 2 else 1
            if isinstance(n, int) and n + ahead >= GROUPS:
                return []
            first = (k + 2) % KB * STEP_ROWS
            return [(n + ahead, (s + ahead) % NB, first + j) for j in range(STEP_ROWS)]

        def drive(eng, body):
            body(0, 0)
            with eng.Fori(0, LOOPS) as i:
                for j in range(NB):
                    body(i * NB + 1 + j, (1 + j) % NB)
            for n in range(1 + LOOPS * NB, GROUPS):
                body(n, n % NB)

        def is_first(n):
            return isinstance(n, int) and n == 0

        def is_last(n):
            return isinstance(n, int) and n == GROUPS - 1

        with nc.Block() as block:
            @block.sync
            def _(sp):
                def load(n, s):
                    b, g = n // NG, n % NG
                    if not (isinstance(n, int) and n < NB):
                        sp.wait_ge(scored.sem, scored.upto(n - NB))
                    for stack, qk, order in ((Qs, 0, Q_PARTS), (Ks, 1, K_PARTS)):
                        for slot, part in enumerate(order):
                            src = parts_d[qk, part].rearrange("(g h d) b t -> d g h b t", d=HD, h=GH)
                            src = src[:, bass.ds(g, 1), :, bass.ds(b, 1), :]
                            sp.dma_start(stack[slot * HD:(slot + 1) * HD, s],
                                         src.rearrange("d g h b t -> d (g h) (b t)")).then_inc(stack_in.sems[s], 16)
                    if not (isinstance(n, int) and n < NB):
                        sp.wait_ge(summed.sem, summed.upto(n - NB))
                    src = v_d[bass.ds(b, 1), :, bass.ds(g * (GH * 2 * HD), GH * 2 * HD)]
                    sp.dma_start(V[:, s].rearrange("p k h c -> p k (h c)"),
                                 src.rearrange("b (k p) c -> p (b k) c", p=P)).then_inc(v_in.sems[s], 16)

                def max_rows(n, s):
                    sp.wait_ge(row_free, maxima_out(n))
                    for part in range(2):
                        for half in range(2):
                            dst = Qs[SROWS + part:SROWS + part + 1, s, :, half * 512:(half + 1) * 512]
                            src = nrow[half * MROWS + part * GH:half * MROWS + (part + 1) * GH, s, :]
                            sp.dma_start(dst, src).then_inc(max_in.sems[s], 16)

                def store(n):
                    sp.wait_ge(row_free, divided(n))
                    b, g = n // NG, n % NG
                    dst = att_d[bass.ds(b, 1), :, bass.ds(g * (GH * HD), GH * HD)]
                    sp.dma_start(dst.rearrange("b (k p) c -> p (b k) c", p=P), att[:]).then_inc(stored.sem, 16)

                load(0, 0)
                load(1, 1)
                max_rows(0, 0)
                load(2, 2)

                def body(n, s):
                    if not is_first(n):
                        if not (isinstance(n, int) and n + 2 >= GROUPS):
                            load(n + 2, (s + 2) % NB)
                        store(n - 1)
                    if not is_last(n):
                        max_rows(n + 1, (s + 1) % NB)

                drive(sp, body)
                store(GROUPS - 1)
                sp.wait_ge(stored.sem, stored.upto(GROUPS - 1))

            @block.tensor
            def _(pe):
                use = [0, 0, 0]

                def row_tile():
                    base, first, k = use
                    if not (isinstance(base, int) and base + k < T):
                        pe.wait_ge(row_free, base + k - T + 1)
                    use[2] += 1
                    return pR[:, (first + k) % T, :]

                def row_scores(n, s, j):
                    h, q, half = j // (2 * KB), j // 2 % KB, j % 2
                    if j == 0:
                        pe.wait_ge(stack_in.sems[s], stack_in.upto(n))
                    nc.tensor.matmul(row_tile(), Qs[0:SROWS, s, h, q * P:(q + 1) * P],
                                     Ks[0:SROWS, s, h, half * 512:(half + 1) * 512],
                                     start=True, stop=True).then_inc(row_full, 1)

                def turn_max(n):
                    if isinstance(n, int) and n == 0:
                        pe.wait_ge(ones.sem, ones.upto(0))
                    pe.wait_ge(neg.sem, neg.upto(n))
                    r = row_tile()
                    for half in range(2):
                        for q in range(4):
                            last = nc.tensor.matmul(r[half * MROWS:(half + 1) * MROWS, q * P:(q + 1) * P],
                                                    nb[:, half * 4 + q, :], identb[:], start=True, stop=True)
                    last.then_inc(row_full, 1)

                def scores(n, s, k, h, half):
                    u = (k * GH + h) * 2 + half
                    if u == 0:
                        pe.wait_ge(max_in.sems[s], max_in.upto(n))
                        if is_first(n):
                            pe.wait_ge(ones.sem, ones.upto(0))
                    if not (is_first(n) and u < T):
                        pe.wait_ge(exped.sem, n * exped.per + u - T + 1)
                    nc.tensor.matmul(pS[:, (s * exped.per + u) % T, :],
                                     Ks[0:SROWS + 2, s, h, k * P:(k + 1) * P],
                                     Qs[0:SROWS + 2, s, h, half * 512:(half + 1) * 512],
                                     start=True, stop=True).then_inc(scored.sem, 1)

                def sums(n, s, k, half):
                    if half == 0:
                        pe.wait_ge(exped.sem, exped.upto(n, (k + 1) * UNITS))
                        if k == 0:
                            pe.wait_ge(v_in.sems[s], v_in.upto(n))
                            if not is_first(n):
                                pe.wait_ge(o_out.sem, o_out.upto(n - 1))
                    for h in range(GH):
                        last = nc.tensor.matmul(pO[h * 32:(h + 1) * 32, half, :], V[:, s, k, h, :],
                                                Pr[:, k % 2, h, half * 512:(half + 1) * 512],
                                                start=(k == 0), stop=(k == KB - 1))
                    if half == 1:
                        last.then_inc(summed.sem, 1)

                def turn_sums(n):
                    pe.wait_ge(o_out.sem, o_out.upto(n))
                    for half in range(2):
                        r = row_tile()
                        for t in range(4):
                            at = (half * 4 + t) * P
                            last = nc.tensor.transpose(r[:, t * P:(t + 1) * P], OT[:, at:at + P], ident[:])
                        last.then_inc(row_full, 1)

                for j in range(MAX_USES):
                    row_scores(0, 0, j)
                turn_max(0)
                for j in range(AHEAD):
                    row_scores(1, 1, j)

                def body(n, s):
                    use[0], use[1], use[2] = first_use(n), tile_of(n, s, 0), 0
                    for k in range(KB):
                        rows = step_rows(n, s, k)
                        for h in range(GH):
                            for half in range(2):
                                scores(n, s, k, h, half)
                                for r in rows[2 * h + half:2 * h + half + 1]:
                                    row_scores(*r)
                                if h % 2 == 1 and half == 0:
                                    if k > 0:
                                        sums(n, s, k - 1, h // 2)
                                    elif not is_first(n):
                                        sums(n - 1, (s - 1) % NB, KB - 1, h // 2)
                            if h == 1 and k == KB - 2 and not is_last(n):
                                turn_max(n + 1)
                        if k == 1 and not is_first(n):
                            turn_sums(n - 1)

                drive(pe, body)
                for half in range(2):
                    sums(GROUPS - 1, (GROUPS - 1) % NB, KB - 1, half)
                use[0], use[1], use[2] = first_use(GROUPS - 1) + TURN, tile_of(GROUPS - 1, 0, TURN), 0
                turn_sums(GROUPS - 1)

            @block.scalar
            def _(act):
                def copy_out(n):
                    act.wait_ge(summed.sem, summed.upto(n))
                    if not is_first(n):
                        act.wait_ge(row_free, divided(n - 1))
                    nc.scalar.copy(OT[:], pO[:].rearrange("p a q -> p (a q)")).then_inc(o_out.sem, 1)

                def body(n, s):
                    for k in range(KB):
                        for h in range(GH):
                            for half in range(2):
                                u = (k * GH + h) * 2 + half
                                act.wait_ge(scored.sem, scored.upto(n, u + 1))
                                if h == 0 and half == 0 and not (is_first(n) and k < 2):
                                    act.wait_ge(summed.sem, n * KB + k - 1)
                                nc.scalar.activation(Pr[:, k % 2, h, half * 512:(half + 1) * 512],
                                                     pS[:, (s * exped.per + u) % T, :],
                                                     ACT.Exp).then_inc(exped.sem, 1)
                        if k == 0 and not is_first(n):
                            copy_out(n - 1)

                drive(act, body)
                copy_out(GROUPS - 1)

            @block.vector
            def _(dve):
                use = [0, 0, 0]
                nc.vector.memset(nb[:, :, 2 * GH:], 0.0)
                for s in range(NB):
                    last = nc.vector.memset(Ks[SROWS:SROWS + 2, s], 1.0)
                last.then_inc(ones.sem, 1)

                def row_tile():
                    base, first, k = use
                    dve.wait_ge(row_full, base + k + 1)
                    use[2] += 1
                    return pR[:, (first + k) % T, :]

                def row_max(j):
                    nc.vector.tensor_reduce(mx[:, j // 2, j % 2:j % 2 + 1], row_tile(), AX.X,
                                            ALU.max).then_inc(row_free, 1)

                def negative(n):
                    neg.begin()
                    dve.wait_ge(row_free, use[0] + use[2])
                    nc.vector.tensor_reduce(nm[:], mx[:], AX.X, ALU.max, negate=True).then_inc(neg.counted(), 1)
                    dve.wait_ge(neg.sem, neg.so_far(n))
                    hi = nb[:, :, 0:GH].rearrange("p q h -> p h q")
                    lo = nb[:, :, GH:2 * GH].rearrange("p q h -> p h q")
                    m = nm[:].rearrange("p (h q) -> p h q", h=GH)
                    nc.vector.tensor_copy(hi, m).then_inc(neg.counted(), 1)
                    dve.wait_ge(neg.sem, neg.so_far(n))
                    nc.vector.tensor_tensor(lo, m, hi, ALU.subtract).then_inc(neg.counted(), 1)

                def max_out(n, s):
                    r = row_tile()
                    nc.vector.tensor_copy(nrow[:, s, :], r[0:2 * MROWS, :]).then_inc(row_free, 1)

                def divide(n):
                    inverse.begin()
                    for half in range(2):
                        r = row_tile().rearrange("p (a c) -> p a c", c=2 * HD)
                        if half == 0 and not is_first(n):
                            dve.wait_ge(stored.sem, stored.upto(n - 1))
                        nc.vector.reciprocal(rec[:, half, :], r[:, :, HD]).then_inc(inverse.counted(), 1)
                        dve.wait_ge(inverse.sem, inverse.so_far(n))
                        dst = att[:, half * 4:(half + 1) * 4, :].rearrange("p t (h c) -> p (t h) c", c=HD)
                        nc.vector.tensor_tensor(dst, r[:, :, 0:HD],
                                                rec[:, half, :].unsqueeze(2).to_broadcast([P, 4 * GH, HD]),
                                                ALU.mult).then_inc(row_free, 1)

                for j in range(MAX_USES):
                    row_max(j)
                negative(0)
                max_out(0, 0)
                for j in range(AHEAD):
                    row_max(j)

                def body(n, s):
                    use[0], use[1], use[2] = first_use(n), tile_of(n, s, 0), 0
                    for k in range(KB):
                        rows = step_rows(n, s, k)
                        turn = k == KB - 2 and not is_last(n)
                        if turn:
                            negative(n + 1)
                        for _, _, j in rows[0:STEP_ROWS // 2]:
                            row_max(j)
                        if turn:
                            max_out(n + 1, (s + 1) % NB)
                        for _, _, j in rows[STEP_ROWS // 2:]:
                            row_max(j)
                        if k == 1 and not is_first(n):
                            divide(n - 1)

                drive(dve, body)
                use[0], use[1], use[2] = first_use(GROUPS - 1) + TURN, tile_of(GROUPS - 1, 0, TURN), 0
                divide(GROUPS - 1)


def attention_out(nc, x, ident, w, mod_d, att_d, x1_d, lo_dst, hi_dst):
    with ExitStack() as ctx:
        def sb(name, shape, dt=F32):
            return ctx.enter_context(nc.sbuf_tensor(name, shape, dt))

        def sig(name, per=1):
            return Signal(ctx.enter_context(nc.semaphore("ao_" + name)), per)

        def arrivals(name, per, bufs=2):
            return Arrivals([ctx.enter_context(nc.semaphore(f"ao_{name}{p}")) for p in range(bufs)], per)

        R = 4
        at = sb("ao_att", [P, R, CT, D])
        xt = sb("ao_x", [P, R, CT, D])
        mrow = sb("ao_mod", [P, R, 3, D])
        aT = sb("ao_aT", [P, KT, CH])
        x1 = sb("ao_x1", [P, R, CT, D])
        stats, mv = sb("ao_stats", [P, CT, 6]), sb("ao_mv", [P, CT, 2])
        ve, rstd, tmp = sb("ao_ve", [P, CT]), sb("ao_rstd", [P, CT]), sb("ao_tmp", [P, CT])
        xn = sb("ao_xn", [P, 2, CT, D])
        hm = sb("ao_hm", [P, 2, CT, D])
        pT = ctx.enter_context(nc.psum_tensor("ao_pT", [P, KT, CH], F32))
        pY = ctx.enter_context(nc.psum_tensor("ao_pY", [P, CT, D], F32))

        loaded = arrivals("loaded", 48, R)
        turned, aT_ready, projected = sig("turned"), sig("aT_ready"), sig("projected")
        gated = sig("gated", 2)
        chain = sig("chain", LN_INCS)
        normed = sig("normed")
        modded = sig("modded", 2)
        stored = arrivals("stored", 48, R)

        def later(n):
            return not isinstance(n, int) or n >= 2

        def again(n):
            return not isinstance(n, int) or n >= 1

        def drive(eng, body):
            for n in range(R):
                body(n, n)
            with eng.Fori(1, NC // R) as i:
                for r in range(R):
                    body(i * R + r, r)

        with nc.Block() as block:
            @block.sync
            def _(sp):
                def load(n, p):
                    if not isinstance(n, int):
                        sp.wait_ge(modded.sem, modded.upto(n - R))
                    sp.dma_start(at[:, p], rows(att_d, n)).then_inc(loaded.sems[p], 16)
                    sp.dma_start(xt[:, p], rows(x, n)).then_inc(loaded.sems[p], 16)
                    src = mod_d[bass.ds(n // 2, 1), 2:5, :].to_broadcast([P, 3, D])
                    sp.dma_start(mrow[:, p], src).then_inc(loaded.sems[p], 16)

                def store(n, r):
                    sp.wait_ge(gated.sem, gated.upto(n))
                    sp.dma_start(rows(x1_d, n), x1[:, r]).then_inc(stored.sems[r], 16)
                    sp.wait_ge(modded.sem, modded.upto(n))
                    sp.dma_start(rows(lo_dst, n), hm[:, r % 2, :, 0:P]).then_inc(stored.sems[r], 16)
                    sp.dma_start(padded(hi_dst, n, CH), hm[:, r % 2, :, P:D]).then_inc(stored.sems[r], 16)

                for n in range(R):
                    load(n, n)
                with sp.Fori(0, NC // R - 1) as i:
                    for r in range(R):
                        store(i * R + r, r)
                        load(i * R + R + r, r)
                for n in range(NC - R, NC):
                    store(n, n % R)
                for n in range(NC - R, NC):
                    sp.wait_ge(stored.sems[n % R], stored.upto(n))

            @block.tensor
            def _(pe):
                def body(n, r):
                    pe.wait_ge(loaded.sems[r], loaded.upto(n))
                    if again(n):
                        pe.wait_ge(aT_ready.sem, aT_ready.upto(n - 1))
                    for t in range(CT):
                        for k in range(KT):
                            last = nc.tensor.transpose(pT[:, k, t * P:(t + 1) * P],
                                                       at[:, r, t, k * P:(k + 1) * P], ident[:])
                    last.then_inc(turned.sem, 1)
                    pe.wait_ge(aT_ready.sem, aT_ready.upto(n))
                    if again(n):
                        pe.wait_ge(gated.sem, gated.upto(n - 1, 1))
                    for t in range(CT):
                        for k in range(KT):
                            last = nc.tensor.matmul(pY[:, t, :], aT[:, k, t * P:(t + 1) * P], w["wo"][:, k, :],
                                                    start=(k == 0), stop=(k == KT - 1))
                    last.then_inc(projected.sem, 1)

                drive(pe, body)

            @block.scalar
            def _(act):
                def body(n, r):
                    act.wait_ge(turned.sem, turned.upto(n))
                    if again(n):
                        act.wait_ge(projected.sem, projected.upto(n - 1))
                    nc.scalar.copy(aT[:], pT[:]).then_inc(aT_ready.sem, 1)

                drive(act, body)

            @block.vector
            def _(dve):
                def gate(n, r):
                    dve.wait_ge(loaded.sems[r], loaded.upto(n))
                    dve.wait_ge(projected.sem, projected.upto(n))
                    if not (isinstance(n, int) and n < R):
                        dve.wait_ge(stored.sems[r], stored.upto(n - R))
                    row = mrow[:, r, 0, :].unsqueeze(1).to_broadcast([P, CT, D])
                    nc.vector.tensor_tensor(x1[:, r], pY[:], row, ALU.mult).then_inc(gated.sem, 1)

                def add(n, r):
                    dve.wait_ge(gated.sem, gated.upto(n, 1))
                    nc.vector.tensor_tensor(x1[:, r], x1[:, r], xt[:, r], ALU.add).then_inc(gated.sem, 1)

                def stats_of(n, r, steps):
                    if steps[0] == 0:
                        dve.wait_ge(gated.sem, gated.upto(n))
                    layer_norm_steps(nc, dve, chain, n, steps, x1[:, r], stats, mv, ve[:], rstd[:], tmp[:])

                def normalize(n, r):
                    dve.wait_ge(chain.sem, chain.upto(n))
                    if later(n):
                        dve.wait_ge(modded.sem, modded.upto(n - 2))
                    for t in range(CT):
                        last = nc.vector.tensor_scalar(xn[:, r % 2, t, :], x1[:, r, t, :], mv[:, t, 0:1],
                                                       rstd[:, t:t + 1], ALU.subtract, ALU.mult)
                    last.then_inc(normed.sem, 1)

                def body(n, r, following=True):
                    stats_of(n, r, range(0, 6))
                    if following:
                        gate(n + 1, (r + 1) % R)
                    stats_of(n, r, range(6, 8))
                    if following:
                        add(n + 1, (r + 1) % R)
                    stats_of(n, r, range(8, LN_INCS))
                    normalize(n, r)

                gate(0, 0)
                add(0, 0)
                for n in range(R):
                    body(n, n)
                with dve.Fori(1, NC // R - 1) as i:
                    for r in range(R):
                        body(i * R + r, r)
                for n in range(NC - R, NC):
                    body(n, n % R, following=n + 1 < NC)

            @block.gpsimd
            def _(pool):
                def body(n, r):
                    p = r % 2
                    pool.wait_ge(normed.sem, normed.upto(n))
                    for t_in, t_out, row, op in ((xn, xn, 2, ALU.mult), (xn, hm, 1, ALU.add)):
                        if row == 1:
                            pool.wait_ge(modded.sem, modded.upto(n, 1))
                            if later(n):
                                pool.wait_ge(stored.sems[(r - 2) % R], stored.upto(n - 2))
                        nc.gpsimd.tensor_tensor(t_out[:, p], t_in[:, p],
                                                mrow[:, r, row, :].unsqueeze(1).to_broadcast([P, CT, D]),
                                                op).then_inc(modded.sem, 1)

                drive(pool, body)


def window_signals(nc, ctx):
    pairs = HEADS // 2
    per = dict(
        x_turned=1, x_high=1, xT_ready=1,
        qk_done=2, v_done=1, v_ready=1,
        squared=2, chain=4, newton=POOL_RSQRT_INCS, scaled=1, rotated=4,
        q_turned=1, k_turned=1, q_ready=1, k_ready=2,
        scored=pairs, masked=pairs, exped=pairs, inverse=pairs, weighted=pairs,
        p_turned=pairs, pT_ready=pairs, summed=pairs, o_high=1, o_ready=1,
        projected=1, added=1,
    )
    signals = {name: Signal(ctx.enter_context(nc.semaphore("wa_" + name)), k) for name, k in per.items()}
    for name, bufs, k in (("x_in", WIN_BUFS, 48), ("stored", 2, 32)):
        signals[name] = Arrivals([ctx.enter_context(nc.semaphore(f"wa_{name}{p}")) for p in range(bufs)], k)
    return signals


def window_attention(nc, a, layer, ident, trig_d, src, dst, s):
    TILES = B * NW
    PAIRS = HEADS // 2
    R = WIN_BUFS
    base = layer * TILES
    lo_s, hi_s = src
    lo_t, hi_t = dst

    with ExitStack() as ctx:
        def sb(name, shape, dt=F32):
            return ctx.enter_context(nc.sbuf_tensor(f"wa{layer}_{name}", shape, dt))

        def pb(name, shape):
            return ctx.enter_context(nc.psum_tensor(f"wa{layer}_{name}", shape, F32))

        wqkv = sb("wqkv", [P, 2, KT, 3 * INNER], F32R)
        wo = sb("wo", [P, 2, INNER // P, D], F32R)
        wqkv_in = sb("wqkv_in", [P, KT, 3 * INNER])
        wo_in = sb("wo_in", [P, INNER // P, D])
        trig = sb("trig", [P, NW, 4, DH])
        mask = sb("mask", [P, 2, 2 * WIN])
        xs = sb("xs", [P, R, 2, P])
        xo = sb("xo", [P, R, P])
        xT = sb("xT", [P, 2, KT, P], F32R)
        sq = sb("sq", [P, 2 * INNER])
        ss, rn, rt = sb("ss", [P, 2 * HEADS]), sb("rn", [P, 2 * HEADS]), sb("rt", [P, 2 * HEADS])
        three_halves = sb("three_halves", [P, 2 * HEADS])
        qn = sb("qn", [P, 2, HEADS, DH])
        qa = sb("qa", [P, 2, HEADS, DH])
        qb = sb("qb", [P, 2, HEADS, DH])
        qT = sb("qT", [P, 2, PAIRS, P])
        kT = sb("kT", [P, R, PAIRS, 2, P])
        V = sb("V", [P, R, HEADS, DH])
        sm = sb("sm", [P, 2, 2, 2 * WIN])
        mn = sb("mn", [P, 2, HEADS])
        pr = sb("pr", [P, 2, 2, 2 * WIN])
        rs, ri = sb("rs", [P, 2, HEADS]), sb("ri", [P, 2, HEADS])
        pn = sb("pn", [P, 2, 2, 2 * WIN])
        pT = sb("pT", [P, 2, 2, 2, P])
        oT = sb("oT", [P, 2, PAIRS, P], F32R)
        x2 = sb("x2", [P, 2, 2, P])
        gate = sb("gate", [P, PAIRS])
        pQK, pV, pM = pb("pQK", [P, 2, INNER]), pb("pV", [P, INNER]), pb("pM", [P, 512])
        pS, pP, pO = pb("pS", [P, 2, 512]), pb("pP", [P, 512]), pb("pO", [P, PAIRS, P])
        pX, pY = pM[:, 0:D], pM[:, D:2 * D]
        w_in = ctx.enter_context(nc.semaphore(f"wa{layer}_w_in"))
        zeroed = ctx.enter_context(nc.semaphore(f"wa{layer}_zeroed"))
        w_high = ctx.enter_context(nc.semaphore(f"wa{layer}_w_high"))
        w_split = ctx.enter_context(nc.semaphore(f"wa{layer}_w_split"))
        wo_split = ctx.enter_context(nc.semaphore(f"wa{layer}_wo_split"))
        W_LOADS = 4

        def g(n):
            return n + base

        def early(n, k):
            return isinstance(n, int) and n < k

        def within(n):
            return not isinstance(n, int) or 0 <= n < TILES

        def fresh(n, hp):
            return early(n, 1) and layer == 0 and hp < 2

        def drive(eng, body):
            for i in range(NW):
                body(i, i)
            with eng.Fori(1, B) as b:
                for w in range(NW):
                    body(b * NW + w, w)
            for i in range(TILES, TILES + 3):
                body(i, i % NW)

        with nc.Block() as block:
            @block.sync
            def _(sp):
                def load(n, r):
                    b, t = n // NW, n % NW
                    flat = lo_s[bass.ds(b, 1), bass.ds(t * P, P), :].rearrange("b p c -> (b p) c")
                    sp.dma_start(xs[:, r, 0, :], flat).then_inc(s["x_in"].sems[r], 16)
                    flat = hi_s[bass.ds(b, 1), bass.ds(t * P, P), :].rearrange("b p c -> (b p) c")
                    sp.dma_start(xs[:, r, 1, :], flat).then_inc(s["x_in"].sems[r], 16)
                    flat = hi_s[bass.ds(b, 1), bass.ds(t * P + 1, P), :].rearrange("b p c -> (b p) c")
                    sp.dma_start(xo[:, r, :], flat).then_inc(s["x_in"].sems[r], 16)

                def store(n, p):
                    sp.wait_ge(s["added"].sem, s["added"].upto(g(n)))
                    b, t = n // NW, n % NW
                    flat = lo_t[bass.ds(b, 1), bass.ds(t * P, P), :].rearrange("b p c -> (b p) c")
                    sp.dma_start(flat, x2[:, p, 0, :]).then_inc(s["stored"].sems[p], 16)
                    flat = hi_t[bass.ds(b, 1), bass.ds(t * P + 1, P), :].rearrange("b p c -> (b p) c")
                    sp.dma_start(flat, x2[:, p, 1, :]).then_inc(s["stored"].sems[p], 16)

                load(0, 0)
                for dst_, src_ in ((wqkv_in[:], a["L0_ffn_wqkv"][layer].rearrange("(k p) n -> p k n", p=P)),
                                   (wo_in[:], a["L0_ffn_wo"][layer].rearrange("(k p) n -> p k n", p=P)),
                                   (trig[:].rearrange("p w a c -> p w (a c)"),
                                    trig_d[layer].rearrange("w p c -> p w c")),
                                   (mask[:], a["mask"].rearrange("w p c -> p w c"))):
                    sp.dma_start(dst_, src_).then_inc(w_in, 16)
                for n in range(1, R):
                    load(n, n)
                with sp.Fori(0, TILES // R - 1) as i:
                    for r in range(R):
                        store(i * R + r, r % 2)
                        load(i * R + R + r, r)
                for n in range(TILES - R, TILES):
                    store(n, n % 2)
                sp.wait_ge(s["stored"].sems[0], s["stored"].upto(g(TILES - 2)))
                sp.wait_ge(s["stored"].sems[1], s["stored"].upto(g(TILES - 1)))

            @block.tensor
            def _(pe):
                def turn_x(n, r):
                    pe.wait_ge(s["x_in"].sems[r], s["x_in"].upto(g(n)))
                    if not early(n, 2):
                        pe.wait_ge(s["q_ready"].sem, s["q_ready"].upto(g(n - 2)))
                    for k in range(KT):
                        last = nc.tensor.transpose(pX[:, k * P:(k + 1) * P], xs[:, r, k, :], ident[:])
                    last.then_inc(s["x_turned"].sem, 1)

                def project(n, j):
                    if j == 2:
                        pe.wait_ge(s["xT_ready"].sem, s["xT_ready"].upto(g(n)))
                        if not early(n, 2):
                            pe.wait_ge(s["k_ready"].sem, s["k_ready"].upto(g(n - 2)))
                    if isinstance(n, int) and n == 0:
                        pe.wait_ge(w_split, (2, 3, 1)[j])
                    if j == 0 and not early(n, 1):
                        pe.wait_ge(s["scaled"].sem, s["scaled"].upto(g(n - 1)))
                    products = [(k, x, y) for k in range(KT) for x, y in SPLIT_PRODUCTS]
                    for i, (k, x, y) in enumerate(products):
                        out = pQK[:, j, :] if j < 2 else pV[:]
                        last = nc.tensor.matmul(out, xT[:, x, k, :], wqkv[:, y, k, j * INNER:(j + 1) * INNER],
                                                start=(i == 0), stop=(i == len(products) - 1))
                    if j < 2:
                        last.then_inc(s["qk_done"].sem, 1)
                    if j == 2:
                        last.then_inc(s["v_done"].sem, 1)

                def turn_qk(n, j):
                    if j == 0:
                        pe.wait_ge(s["rotated"].sem, s["rotated"].upto(g(n)))
                        if within(n + 1):
                            pe.wait_ge(s["xT_ready"].sem, s["xT_ready"].upto(g(n + 1)))
                        if not early(n, 2):
                            pe.wait_ge(s["added"].sem, s["added"].upto(g(n - 2)))
                    elif within(n + 1):
                        pe.wait_ge(s["v_ready"].sem, s["v_ready"].upto(g(n + 1)))
                    dst = pM if j == 0 else pV
                    for hp in range(PAIRS):
                        last = nc.tensor.transpose(dst[:, hp * P:(hp + 1) * P],
                                                   qn[:, j, 2 * hp:2 * hp + 2, :].rearrange("p h c -> p (h c)"),
                                                   ident[:])
                    last.then_inc(s["q_turned" if j == 0 else "k_turned"].sem, 1)

                def scores(n, r, hp):
                    if isinstance(n, int) and n == 0:
                        pe.wait_ge(zeroed, 2)
                    if hp == 0:
                        pe.wait_ge(s["q_ready"].sem, s["q_ready"].upto(g(n)))
                        pe.wait_ge(s["k_ready"].sem, s["k_ready"].upto(g(n)))
                    if not fresh(n, hp):
                        pe.wait_ge(s["masked"].sem, g(n) * PAIRS + hp - 1)
                    out = pS[:, hp % 2, :].rearrange("p (h w k) -> p h w k", h=2, w=2)
                    for w, kr in enumerate(((r - 1) % R, r % R)):
                        last = nc.tensor.matmul(out[:, :, w, :], qT[:, r % 2, hp, :], kT[:, kr, hp],
                                                start=True, stop=True)
                    last.then_inc(s["scored"].sem, 1)

                def turn_p(n, hp):
                    pe.wait_ge(s["weighted"].sem, s["weighted"].upto(g(n), hp + 1))
                    if not fresh(n, hp + 1):
                        pe.wait_ge(s["pT_ready"].sem, g(n) * PAIRS + hp)
                    for hh in range(2):
                        for w in range(2):
                            at = (hh * 2 + w) * P
                            last = nc.tensor.transpose(pP[:, at:at + P], pn[:, hp % 2, hh, w * WIN:(w + 1) * WIN],
                                                       ident[:])
                    last.then_inc(s["p_turned"].sem, 1)

                def values(n, r, hp):
                    pe.wait_ge(s["pT_ready"].sem, s["pT_ready"].upto(g(n), hp + 1))
                    if hp == 0 and not early(n, 1):
                        pe.wait_ge(s["o_ready"].sem, s["o_ready"].upto(g(n - 1)))
                    for w, kr in enumerate(((r - 1) % R, r % R)):
                        for hh in range(2):
                            last = nc.tensor.matmul(pO[hh * DH:(hh + 1) * DH, hp, :], V[:, kr, 2 * hp + hh, :],
                                                    pT[:, hp % 2, hh, w, :], start=(w == 0), stop=(w == 1))
                    last.then_inc(s["summed"].sem, 1)

                def project_out(n):
                    if isinstance(n, int) and n == 0:
                        pe.wait_ge(wo_split, 1)
                    pe.wait_ge(s["o_ready"].sem, s["o_ready"].upto(g(n)))
                    products = [(hp, x, y) for hp in range(PAIRS) for x, y in SPLIT_PRODUCTS]
                    for i, (hp, x, y) in enumerate(products):
                        last = nc.tensor.matmul(pY, oT[:, x, hp, :], wo[:, y, hp, :],
                                                start=(i == 0), stop=(i == len(products) - 1))
                    last.then_inc(s["projected"].sem, 1)


                def body(i, w):
                    new, mid, att, end = i, i - 1, i - 2, i - 3
                    r_att, r_end = w - 2, w - 3
                    if within(att):
                        scores(att, r_att, 0)
                    if within(new):
                        turn_x(new, w % R)
                    if within(end):
                        values(end, r_end, 3)
                    if within(att):
                        scores(att, r_att, 1)
                    if within(new):
                        project(new, 2)
                    if within(att):
                        scores(att, r_att, 2)
                    if within(end):
                        project_out(end)
                    if within(att):
                        turn_p(att, 0)
                        scores(att, r_att, 3)
                        turn_p(att, 1)
                        values(att, r_att, 0)
                    if within(new):
                        project(new, 0)
                        project(new, 1)
                    if within(mid):
                        turn_qk(mid, 0)
                    if within(att):
                        turn_p(att, 2)
                    if within(mid):
                        turn_qk(mid, 1)
                    if within(att):
                        values(att, r_att, 1)
                        turn_p(att, 3)
                        values(att, r_att, 2)

                drive(pe, body)

            @block.scalar
            def _(act):
                def x_out(n):
                    act.wait_ge(s["x_turned"].sem, s["x_turned"].upto(g(n)))
                    if not early(n, 1):
                        act.wait_ge(s["qk_done"].sem, s["qk_done"].upto(g(n - 1)))
                    nc.scalar.copy(xT[:, 0].rearrange("p k t -> p (k t)"), pX).then_inc(s["x_high"].sem, 1)

                def square(n, j):
                    act.wait_ge(s["qk_done"].sem, s["qk_done"].upto(g(n), j + 1))
                    if not early(n, 1):
                        act.wait_ge(s["chain"].sem, s["chain"].upto(g(n - 1), j + 1))
                    nc.scalar.activation(sq[:, j * INNER:(j + 1) * INNER], pQK[:, j, :],
                                         ACT.Square).then_inc(s["squared"].sem, 1)

                def v_out(n, r):
                    act.wait_ge(s["v_done"].sem, s["v_done"].upto(g(n)))
                    if not early(n, R):
                        act.wait_ge(s["summed"].sem, s["summed"].upto(g(n - R + 1)))
                    nc.scalar.copy(V[:, r].rearrange("p h c -> p (h c)"), pV[:]).then_inc(s["v_ready"].sem, 1)

                def q_out(n, p):
                    act.wait_ge(s["q_turned"].sem, s["q_turned"].upto(g(n)))
                    if not early(n, 2):
                        act.wait_ge(s["scored"].sem, s["scored"].upto(g(n - 2)))
                    nc.scalar.copy(qT[:, p].rearrange("p a t -> p (a t)"), pM[:]).then_inc(s["q_ready"].sem, 1)

                def k_out(n, r):
                    act.wait_ge(s["k_turned"].sem, s["k_turned"].upto(g(n)))
                    if not early(n, R):
                        act.wait_ge(s["scored"].sem, s["scored"].upto(g(n - R + 1)))
                    for hh in range(2):
                        at = hh * DH
                        nc.scalar.copy(kT[at:at + DH, r, :, hh, :],
                                       pV[at:at + DH, :].rearrange("p (a t) -> p a t", a=PAIRS))\
                            .then_inc(s["k_ready"].sem, 1)

                def exponentials(n, p, hp):
                    act.wait_ge(s["masked"].sem, s["masked"].upto(g(n), hp + 1))
                    if not fresh(n, hp):
                        act.wait_ge(s["weighted"].sem, g(n) * PAIRS + hp - 1)
                    for hh in range(2):
                        h = 2 * hp + hh
                        last = nc.scalar.activation(pr[:, hp % 2, hh, :], sm[:, hp % 2, hh, :], ACT.Exp,
                                                    bias=mn[:, p, h:h + 1], scale=-1.0,
                                                    accum_out=rs[:, p, h:h + 1])
                    last.then_inc(s["exped"].sem, 1)

                def p_out(n, hp):
                    act.wait_ge(s["p_turned"].sem, s["p_turned"].upto(g(n), hp + 1))
                    if not fresh(n, hp):
                        act.wait_ge(s["summed"].sem, g(n) * PAIRS + hp - 1)
                    nc.scalar.copy(pT[:, hp % 2].rearrange("p h w t -> p (h w t)"),
                                   pP[:]).then_inc(s["pT_ready"].sem, 1)

                def o_out(n):
                    act.wait_ge(s["summed"].sem, s["summed"].upto(g(n)))
                    if not early(n, 1):
                        act.wait_ge(s["projected"].sem, s["projected"].upto(g(n - 1)))
                    nc.scalar.copy(oT[:, 0], pO[:]).then_inc(s["o_high"].sem, 1)

                act.wait_ge(zeroed, 2)
                act.wait_ge(w_in, 16 * W_LOADS)
                for j in (2, 0, 1):
                    cols = slice(j * INNER, (j + 1) * INNER)
                    nc.scalar.copy(wqkv[:, 0, :, cols], wqkv_in[:, :, cols]).then_inc(w_high, 1)
                nc.scalar.copy(wo[:, 0], wo_in[:]).then_inc(w_high, 1)

                def body(i, w):
                    new, mid, att, end = i, i - 1, i - 2, i - 3
                    if within(new):
                        x_out(new)
                    if within(end):
                        o_out(end)
                    if within(att):
                        exponentials(att, w % 2, 0)
                        exponentials(att, w % 2, 1)
                    if within(new):
                        v_out(new, w % R)
                    if within(att):
                        p_out(att, 0)
                        exponentials(att, w % 2, 2)
                        p_out(att, 1)
                        exponentials(att, w % 2, 3)
                    if within(new):
                        square(new, 0)
                        square(new, 1)
                    if within(mid):
                        q_out(mid, (w - 1) % 2)
                    if within(att):
                        p_out(att, 2)
                    if within(mid):
                        k_out(mid, (w - 1) % R)
                    if within(att):
                        p_out(att, 3)

                drive(act, body)

            @block.gpsimd
            def _(pool):
                def weigh(n, p, hp):
                    pool.wait_ge(s["inverse"].sem, s["inverse"].upto(g(n), hp + 1))
                    if not fresh(n, hp):
                        pool.wait_ge(s["p_turned"].sem, g(n) * PAIRS + hp - 1)
                    inv = ri[:, p, 2 * hp:2 * hp + 2].unsqueeze(2).to_broadcast([P, 2, 2 * WIN])
                    nc.gpsimd.tensor_tensor(pn[:, hp % 2], pr[:, hp % 2], inv, ALU.mult).then_inc(s["weighted"].sem, 1)

                def newton(n):
                    c = s["newton"]
                    pool.wait_ge(s["chain"].sem, s["chain"].upto(g(n)))
                    for k in range(POOL_RSQRT_INCS):
                        if k > 0:
                            pool.wait_ge(c.sem, c.upto(g(n), k))
                        dst_, x, y, op = ((rt, rn, rn, ALU.mult), (rt, rt, ss, ALU.mult),
                                          (rt, three_halves, rt, ALU.subtract), (rn, rn, rt, ALU.mult))[k % 4]
                        nc.gpsimd.tensor_tensor(dst_[:], x[:], y[:], op).then_inc(c.sem, 1)

                pool.wait_ge(w_in, 16 * W_LOADS)
                pool.wait_ge(w_high, 4)
                nc.gpsimd.tensor_tensor(wo[:, 1], wo_in[:], wo[:, 0].bitcast(F32), ALU.subtract).then_inc(wo_split, 1)
                pool.wait_ge(zeroed, 3)

                def body(i, w):
                    if within(i - 2):
                        for hp in range(PAIRS):
                            weigh(i - 2, w % 2, hp)
                    if within(i):
                        newton(i)

                drive(pool, body)

            @block.vector
            def _(dve):
                nc.vector.memset(kT[:], 0.0).then_inc(zeroed, 1)
                nc.vector.memset(V[:, R - 1], 0.0).then_inc(zeroed, 1)
                nc.vector.memset(three_halves[:], 1.5).then_inc(zeroed, 1)
                dve.wait_ge(w_in, 16 * W_LOADS)
                for i, j in enumerate((2, 0, 1)):
                    cols = slice(j * INNER, (j + 1) * INNER)
                    dve.wait_ge(w_high, i + 1)
                    nc.vector.tensor_tensor(wqkv[:, 1, :, cols], wqkv_in[:, :, cols],
                                            wqkv[:, 0, :, cols].bitcast(F32), ALU.subtract).then_inc(w_split, 1)

                def masks(n, w, hp):
                    dve.wait_ge(s["scored"].sem, s["scored"].upto(g(n), hp + 1))
                    if not fresh(n, hp):
                        dve.wait_ge(s["exped"].sem, g(n) * PAIRS + hp - 1)
                    nc.vector.memset(gate[:, hp:hp + 1], 0.0)
                    for hh in range(2):
                        h = 2 * hp + hh
                        last = nc.vector.tensor_tensor_reduce(
                            out=sm[:, hp % 2, hh, :], in0=pS[:, hp % 2, hh * 2 * WIN:(hh + 1) * 2 * WIN],
                            in1=mask[:, 0 if w == 0 else 1, :], scale=1.0, scalar=MASKED, op0=ALU.add, op1=ALU.min,
                            accum_out=mn[:, w % 2, h:h + 1])
                    last.then_inc(s["masked"].sem, 1)

                def inverse(n, p, hp):
                    dve.wait_ge(s["exped"].sem, s["exped"].upto(g(n), hp + 1))
                    nc.vector.reciprocal(ri[:, p, 2 * hp:2 * hp + 2],
                                         rs[:, p, 2 * hp:2 * hp + 2]).then_inc(s["inverse"].sem, 1)

                def norms(n):
                    c = s["chain"]
                    for j in range(2):
                        dve.wait_ge(s["squared"].sem, s["squared"].upto(g(n), j + 1))
                        if j == 0 and not early(n, 1):
                            dve.wait_ge(s["newton"].sem, s["newton"].upto(g(n - 1)))
                        nc.vector.tensor_reduce(ss[:, j * HEADS:(j + 1) * HEADS],
                                                sq[:, j * INNER:(j + 1) * INNER].rearrange("p (h c) -> p h c", c=DH),
                                                AX.X, ALU.add).then_inc(c.sem, 1)
                    dve.wait_ge(c.sem, c.upto(g(n), 2))
                    nc.vector.tensor_scalar(ss[:], ss[:], NORM_FLOOR, 0.5, ALU.max, ALU.mult).then_inc(c.sem, 1)
                    dve.wait_ge(c.sem, c.upto(g(n), 3))
                    if not early(n, 1):
                        dve.wait_ge(s["scaled"].sem, s["scaled"].upto(g(n - 1)))
                    nc.vector.tensor_scalar(rn[:].bitcast(I32), ss[:].bitcast(I32), -0.5, HALF_RSQRT_SEED, ALU.mult,
                                            ALU.add).then_inc(c.sem, 1)

                def split_x(n):
                    dve.wait_ge(s["x_high"].sem, s["x_high"].upto(g(n)))
                    nc.vector.tensor_tensor(xT[:, 1].rearrange("p k t -> p (k t)"), pX,
                                            xT[:, 0].rearrange("p k t -> p (k t)").bitcast(F32),
                                            ALU.subtract).then_inc(s["xT_ready"].sem, 1)

                def split_o(n):
                    dve.wait_ge(s["o_high"].sem, s["o_high"].upto(g(n)))
                    nc.vector.tensor_tensor(oT[:, 1], pO[:], oT[:, 0].bitcast(F32),
                                            ALU.subtract).then_inc(s["o_ready"].sem, 1)

                def scale(n):
                    dve.wait_ge(s["newton"].sem, s["newton"].upto(g(n)))
                    nc.vector.tensor_tensor(qa[:].rearrange("p a h c -> p (a h) c"),
                                            pQK[:].rearrange("p a (h c) -> p (a h) c", c=DH),
                                            rn[:].unsqueeze(2).to_broadcast([P, 2 * HEADS, DH]),
                                            ALU.mult).then_inc(s["scaled"].sem, 1)

                def rotate(n, w, step):
                    c = s["rotated"]
                    hd = DH // 2
                    if step < 2:
                        at, other = step * hd, hd - step * hd
                        dve.wait_ge(s["scaled"].sem, s["scaled"].upto(g(n)))
                        ins = nc.vector.tensor_tensor(
                            qb[:, :, :, at:at + hd], qa[:, :, :, other:other + hd],
                            trig[:, w, 2:4, at:at + hd].unsqueeze(2).to_broadcast([P, 2, HEADS, hd]), ALU.mult)
                    elif step == 2:
                        dve.wait_ge(c.sem, c.upto(g(n), 2))
                        ins = nc.vector.tensor_tensor(
                            qa[:], qa[:], trig[:, w, 0:2, :].unsqueeze(2).to_broadcast([P, 2, HEADS, DH]), ALU.mult)
                    else:
                        dve.wait_ge(c.sem, c.upto(g(n), 3))
                        if not early(n, 1):
                            dve.wait_ge(s["k_turned"].sem, s["k_turned"].upto(g(n - 1)))
                        ins = nc.vector.tensor_tensor(qn[:], qa[:], qb[:], ALU.add)
                    ins.then_inc(c.sem, 1)

                def add(n, r):
                    dve.wait_ge(s["projected"].sem, s["projected"].upto(g(n)))
                    dve.wait_ge(s["x_in"].sems[r], s["x_in"].upto(g(n)))
                    if not early(n, 2):
                        dve.wait_ge(s["stored"].sems[r % 2], s["stored"].upto(g(n - 2)))
                    nc.vector.tensor_tensor(x2[:, r % 2, 0, :], pY[:, 0:P], xs[:, r, 0, :], ALU.add)
                    nc.vector.tensor_tensor(x2[:, r % 2, 1, :], pY[:, P:D], xo[:, r, :],
                                            ALU.add).then_inc(s["added"].sem, 1)

                def body(i, w):
                    new, mid, att, end = i, i - 1, i - 2, i - 3
                    w_mid, w_att, w_end = (w - 1) % NW, (w - 2) % NW, (w - 3) % NW
                    if within(att):
                        masks(att, w_att, 0)
                    if within(new):
                        split_x(new)
                    if within(att):
                        masks(att, w_att, 1)
                    if within(end):
                        split_o(end)
                    if within(att):
                        inverse(att, w % 2, 0)
                    if within(mid):
                        scale(mid)
                    if within(att):
                        inverse(att, w % 2, 1)
                    if within(mid):
                        rotate(mid, w_mid, 0)
                    if within(att):
                        masks(att, w_att, 2)
                    if within(mid):
                        rotate(mid, w_mid, 1)
                    if within(end):
                        add(end, w_end % R)
                    if within(att):
                        masks(att, w_att, 3)
                        inverse(att, w % 2, 2)
                    if within(mid):
                        rotate(mid, w_mid, 2)
                        rotate(mid, w_mid, 3)
                    if within(att):
                        inverse(att, w % 2, 3)
                    if within(new):
                        norms(new)

                drive(dve, body)


def ffn_signals(nc, ctx):
    per = dict(
        chain=LN_INCS, normed=1, biased=2, turned=1, hT_ready=2 * KT, h_split=1,
        gated=HB, lifted=HB, gelu=HB, mixed=HB, u_high=HB, u_split=HB, y_done=1, summed=1, scaled=1, final=1,
    )
    signals = {name: Signal(ctx.enter_context(nc.semaphore("ff_" + name)), k) for name, k in per.items()}
    for name, k in dict(x_in=48, last_in=32, stored=32).items():
        signals[name] = Arrivals([ctx.enter_context(nc.semaphore(f"ff_{name}{p}")) for p in range(2)], k)
    return signals


def feed_forward(nc, a, layer, ident, src, dst, x1_d, mod_d, out, s):
    base = layer * NC
    lo_s, hi_s = src
    final = dst is None

    with ExitStack() as ctx:
        def sb(name, shape, dt=F32):
            return ctx.enter_context(nc.sbuf_tensor(f"ff{layer}_{name}", shape, dt))

        w1 = sb("w1", [P, 2, KT, 2, HB * P], F32R)
        w2 = sb("w2", [P, 2, HB, D], F32R)
        w1_in = sb("w1_in", [P, KT, 2, HB * P])
        w2_in = sb("w2_in", [P, HB, D])
        b1 = sb("b1", [P, 2, HB])
        b2 = sb("b2", [P, D])
        lg, lb = sb("lg", [P, KT]), sb("lb", [P, KT])
        hx = sb("hx", [P, 2, CT, D])
        xo = sb("xo", [P, 2, CT, P])
        xb = sb("xb", [P, 2, CT, D])
        stats, mv = sb("stats", [P, CT, 6]), sb("mv", [P, CT, 2])
        ve, rstd, tmp = sb("ve", [P, CT]), sb("rstd", [P, CT]), sb("tmp", [P, CT])
        hn = sb("hn", [P, 2, CT, D])
        hF = sb("hF", [P, KT, CH])
        hT = sb("hT", [P, 2, 2, KT, CH], F32R)
        gl = sb("gl", [P, 2, CH])
        uF = sb("uF", [P, 2, CH])
        u = sb("u", [P, 2, HB, CH], F32R)
        y = sb("y", [P, 2, CT, D])
        if final:
            x1 = sb("x1", [P, 2, CT, D])
            gb = sb("gb", [P, 2, D])
            yg = sb("yg", [P, CT, D])
            yo = sb("yo", [P, 2, CT, D])
        pH = ctx.enter_context(nc.psum_tensor(f"ff{layer}_pH", [P, KT, CH], F32))
        pG = ctx.enter_context(nc.psum_tensor(f"ff{layer}_pG", [P, 2, CH], F32))
        pA = ctx.enter_context(nc.psum_tensor(f"ff{layer}_pA", [P, 2, CH], F32))
        pY = ctx.enter_context(nc.psum_tensor(f"ff{layer}_pY", [P, CT, D], F32))
        w_in = ctx.enter_context(nc.semaphore(f"ff{layer}_w_in"))
        zeroed = ctx.enter_context(nc.semaphore(f"ff{layer}_zeroed"))
        w_high = ctx.enter_context(nc.semaphore(f"ff{layer}_w_high"))
        w1_split = ctx.enter_context(nc.semaphore(f"ff{layer}_w1_split"))
        w2_split = ctx.enter_context(nc.semaphore(f"ff{layer}_w2_split"))
        full = (HB - 1) * P
        LOADS = 11

        def g(n):
            return n + base

        def early(n, k):
            return isinstance(n, int) and n < k

        def drive(eng, body):
            for n in range(2):
                body(n, n)
            with eng.Fori(1, NC // 2) as i:
                for p in range(2):
                    body(i * 2 + p, p)

        with nc.Block() as block:
            @block.sync
            def _(sp):
                def load(n, p):
                    if not early(n, 2):
                        sp.wait_ge(s["normed"].sem, s["normed"].upto(g(n - 2)))
                        sp.wait_ge(s["biased"].sem, s["biased"].upto(g(n - 2)))
                    sp.dma_start(hx[:, p, :, 0:P], rows(lo_s, n)).then_inc(s["x_in"].sems[p], 16)
                    sp.dma_start(hx[:, p, :, P:D], shifted(hi_s, n, CH)).then_inc(s["x_in"].sems[p], 16)
                    sp.dma_start(xo[:, p], padded(hi_s, n, CH)).then_inc(s["x_in"].sems[p], 16)

                def load_last(n, p):
                    if not early(n, 2):
                        sp.wait_ge(s["final"].sem, s["final"].upto(n - 2))
                    sp.dma_start(x1[:, p], rows(x1_d, n)).then_inc(s["last_in"].sems[p], 16)
                    src_ = mod_d[bass.ds(n // 2, 1), 5, :].to_broadcast([P, D])
                    sp.dma_start(gb[:, p, :], src_).then_inc(s["last_in"].sems[p], 16)

                def store(n, p):
                    if final:
                        sp.wait_ge(s["final"].sem, s["final"].upto(n))
                        for half in range(2):
                            sp.dma_start(rows(out, n)[:, 2 * half:2 * half + 2],
                                         yo[:, p, 2 * half:2 * half + 2]).then_inc(s["stored"].sems[p], 16)
                    else:
                        sp.wait_ge(s["summed"].sem, s["summed"].upto(g(n)))
                        sp.dma_start(rows(dst[0], n), y[:, p, :, 0:P]).then_inc(s["stored"].sems[p], 16)
                        sp.dma_start(padded(dst[1], n, CH), y[:, p, :, P:D]).then_inc(s["stored"].sems[p], 16)

                load(0, 0)
                load(1, 1)
                sp.wait_ge(zeroed, 3)
                loads = [
                    (w2_in[:, 0:HB - 1, :], a["L0_ffn_w2"][layer, 0:full].rearrange("(k p) n -> p k n", p=P)),
                    (w2_in[0:HL, HB - 1, :], a["L0_ffn_w2"][layer, full:HID]),
                    (b2[:], a["L0_ffn_b2"][layer:layer + 1, :].to_broadcast([P, D])),
                ]
                for half in range(2):
                    loads.append((w1_in[:, :, half, 0:HID],
                                  a["L0_ffn_w1"][layer, :, half * HID:(half + 1) * HID]
                                  .rearrange("(k p) n -> p k n", p=P)))
                for d_, s_ in loads:
                    sp.dma_start(d_, s_).then_inc(w_in, 16)
                with nc.allow_non_contiguous_dma(reason="short vectors, once per layer"):
                    for half in range(2):
                        row = a["L0_ffn_b1"][layer, half * HID:(half + 1) * HID]
                        sp.dma_start(b1[:, half, 0:HB - 1],
                                     row[0:full].rearrange("(k p) -> p k", p=P)).then_inc(w_in, 16)
                        sp.dma_start(b1[0:HL, half, HB - 1:HB],
                                     row[full:HID].rearrange("(p k) -> p k", k=1)).then_inc(w_in, 16)
                    sp.dma_start(lg[:], a["L0_ffn_ln_g"][layer].rearrange("(k p) -> p k", p=P)).then_inc(w_in, 16)
                    sp.dma_start(lb[:], a["L0_ffn_ln_b"][layer].rearrange("(k p) -> p k", p=P)).then_inc(w_in, 16)
                if final:
                    load_last(0, 0)
                    load_last(1, 1)
                with sp.Fori(0, NC // 2 - 1) as i:
                    for p in range(2):
                        load(i * 2 + 2 + p, p)
                        store(i * 2 + p, p)
                        if final:
                            load_last(i * 2 + 2 + p, p)
                store(NC - 2, 0)
                store(NC - 1, 1)
                sp.wait_ge(s["stored"].sems[0], s["stored"].upto(g(NC - 2)))
                sp.wait_ge(s["stored"].sems[1], s["stored"].upto(g(NC - 1)))

            @block.vector
            def _(dve):
                nc.vector.memset(w1_in[:, :, :, full:HB * P], 0.0).then_inc(zeroed, 1)
                nc.vector.memset(w2_in[:, HB - 1, :], 0.0).then_inc(zeroed, 1)
                nc.vector.memset(b1[:], 0.0).then_inc(zeroed, 1)

                def norm(n, p, steps):
                    c = s["chain"]
                    if steps[0] == 0:
                        dve.wait_ge(s["x_in"].sems[p], s["x_in"].upto(g(n)))
                    layer_norm_steps(nc, dve, c, g(n), [k for k in steps if k < LN_INCS], hx[:, p], stats, mv, ve[:],
                                     rstd[:], tmp[:])
                    if steps[-1] == LN_INCS:
                        dve.wait_ge(c.sem, c.upto(g(n)))
                        if not early(n, 2):
                            dve.wait_ge(s["turned"].sem, s["turned"].upto(g(n - 2)))
                        for t in range(CT):
                            last = nc.vector.tensor_scalar(hn[:, p, t, :], hx[:, p, t, :], mv[:, t, 0:1],
                                                           rstd[:, t:t + 1], ALU.subtract, ALU.mult)
                        last.then_inc(s["normed"].sem, 1)

                def mix(n, j):
                    dve.wait_ge(s["gelu"].sem, s["gelu"].upto(g(n), j + 1))
                    dve.wait_ge(s["lifted"].sem, s["lifted"].upto(g(n), j + 1))
                    if not (early(n, 1) and layer == 0 and j < 2):
                        dve.wait_ge(s["u_split"].sem, g(n) * HB + j - 1)
                    nc.vector.scalar_tensor_tensor(out=uF[:, j % 2, :], in0=pA[:, j % 2, :], scalar=b1[:, 0, j:j + 1],
                                                   in1=gl[:, j % 2, :], op0=ALU.add,
                                                   op1=ALU.mult).then_inc(s["mixed"].sem, 1)

                def split_h(n, p):
                    dve.wait_ge(s["hT_ready"].sem, s["hT_ready"].upto(g(n)))
                    if not early(n, 2):
                        dve.wait_ge(s["lifted"].sem, s["lifted"].upto(g(n - 2)))
                    nc.vector.tensor_tensor(hT[:, p, 1], hF[:], hT[:, p, 0].bitcast(F32),
                                            ALU.subtract).then_inc(s["h_split"].sem, 1)

                def finish(n, p):
                    dve.wait_ge(s["y_done"].sem, s["y_done"].upto(g(n)))
                    dve.wait_ge(s["biased"].sem, s["biased"].upto(g(n)))
                    if not early(n, 2):
                        if final:
                            dve.wait_ge(s["final"].sem, s["final"].upto(n - 2))
                        else:
                            dve.wait_ge(s["stored"].sems[p], s["stored"].upto(g(n - 2)))
                    nc.vector.tensor_tensor(y[:, p], pY[:], xb[:, p], ALU.add).then_inc(s["summed"].sem, 1)

                NORM_PARTS = (range(0, 1), range(1, 4), range(4, 8), range(8, 12), range(12, LN_INCS + 1))

                def body(n, p, following=True):
                    for j in range(HB):
                        mix(n, j)
                        if following and j < len(NORM_PARTS):
                            norm(n + 1, 1 - p, NORM_PARTS[j])
                    if following:
                        split_h(n + 1, 1 - p)
                    finish(n, p)

                norm(0, 0, range(LN_INCS + 1))
                split_h(0, 0)
                dve.wait_ge(w_in, 16 * LOADS)
                dve.wait_ge(w_high, 2)
                nc.vector.tensor_tensor(w2[:, 1], w2_in[:], w2[:, 0].bitcast(F32), ALU.subtract).then_inc(w2_split, 1)
                for n in range(2):
                    body(n, n)
                with dve.Fori(1, NC // 2 - 1) as i:
                    for p in range(2):
                        body(i * 2 + p, p)
                body(NC - 2, 0)
                body(NC - 1, 1, following=False)

            @block.gpsimd
            def _(pool):
                pool.wait_ge(w_in, 16 * LOADS)
                pool.wait_ge(w_high, 1)
                nc.gpsimd.tensor_tensor(w1[:, 1], w1_in[:], w1[:, 0].bitcast(F32), ALU.subtract).then_inc(w1_split, 1)

                def body(n, p):
                    pool.wait_ge(s["x_in"].sems[p], s["x_in"].upto(g(n)))
                    if not early(n, 2):
                        pool.wait_ge(s["summed"].sem, s["summed"].upto(g(n - 2)))
                    for half, x in ((0, hx[:, p, :, 0:P]), (1, xo[:, p])):
                        nc.gpsimd.tensor_tensor(xb[:, p, :, half * P:(half + 1) * P], x,
                                                b2[:, half * P:(half + 1) * P].unsqueeze(1).to_broadcast([P, CT, P]),
                                                ALU.add).then_inc(s["biased"].sem, 1)
                    for j in range(HB):
                        pool.wait_ge(s["u_high"].sem, s["u_high"].upto(g(n), j + 1))
                        nc.gpsimd.tensor_tensor(u[:, 1, j, :], uF[:, j % 2, :], u[:, 0, j, :].bitcast(F32),
                                                ALU.subtract).then_inc(s["u_split"].sem, 1)
                    if final:
                        pool.wait_ge(s["summed"].sem, s["summed"].upto(g(n)))
                        pool.wait_ge(s["last_in"].sems[p], s["last_in"].upto(n))
                        if not early(n, 1):
                            pool.wait_ge(s["final"].sem, s["final"].upto(n - 1))
                        nc.gpsimd.tensor_tensor(yg[:], y[:, p], gb[:, p, :].unsqueeze(1).to_broadcast([P, CT, D]),
                                                ALU.mult).then_inc(s["scaled"].sem, 1)
                        pool.wait_ge(s["scaled"].sem, s["scaled"].upto(n))
                        if not early(n, 2):
                            pool.wait_ge(s["stored"].sems[p], s["stored"].upto(g(n - 2)))
                        nc.gpsimd.tensor_tensor(yo[:, p], yg[:], x1[:, p], ALU.add).then_inc(s["final"].sem, 1)

                drive(pool, body)

            @block.tensor
            def _(pe):
                pe.wait_ge(w_in, 16 * LOADS)

                def turn(n, p):
                    pe.wait_ge(s["normed"].sem, s["normed"].upto(g(n)))
                    if not early(n, 1):
                        pe.wait_ge(s["hT_ready"].sem, s["hT_ready"].upto(g(n - 1)))
                    for t in range(CT):
                        for k in range(KT):
                            last = nc.tensor.transpose(pH[:, k, t * P:(t + 1) * P],
                                                       hn[:, p, t, k * P:(k + 1) * P], ident[:])
                    last.then_inc(s["turned"].sem, 1)

                def up(n, p):
                    pe.wait_ge(s["h_split"].sem, s["h_split"].upto(g(n)))
                    for j in range(HB):
                        for half, ps, done, freed in ((1, pG, "gated", "gelu"), (0, pA, "lifted", "mixed")):
                            if not (early(n, 1) and layer == 0 and j < 2):
                                pe.wait_ge(s[freed].sem, g(n) * HB + j - 1)
                            products = [(k, x, y) for k in range(KT) for x, y in SPLIT_PRODUCTS]
                            for i, (k, x, y) in enumerate(products):
                                last = nc.tensor.matmul(ps[:, j % 2, :], w1[:, x, k, half, j * P:(j + 1) * P],
                                                        hT[:, p, y, k, :], start=(i == 0),
                                                        stop=(i == len(products) - 1))
                            last.then_inc(s[done].sem, 1)

                def down(n, p):
                    if not early(n, 1):
                        pe.wait_ge(s["summed"].sem, s["summed"].upto(g(n - 1)))
                    for j in range(HB):
                        pe.wait_ge(s["u_split"].sem, s["u_split"].upto(g(n), j + 1))
                        for t in range(CT):
                            for i, (x, y) in enumerate(SPLIT_PRODUCTS):
                                last = nc.tensor.matmul(pY[:, t, :], u[:, x, j, t * P:(t + 1) * P], w2[:, y, j, :],
                                                        start=(j == 0 and i == 0 and t % 2 == 0),
                                                        stop=(j == HB - 1 and i == len(SPLIT_PRODUCTS) - 1 and t % 2 == 1))
                    last.then_inc(s["y_done"].sem, 1)

                turn(0, 0)
                pe.wait_ge(w1_split, 1)
                pe.wait_ge(w2_split, 1)
                for n in range(2):
                    up(n, n)
                    turn(n + 1, (n + 1) % 2)
                    down(n, n)
                with pe.Fori(0, NC // 2 - 2) as i:
                    for p in range(2):
                        up(i * 2 + 2 + p, p)
                        turn(i * 2 + 3 + p, 1 - p)
                        down(i * 2 + 2 + p, p)
                up(NC - 2, 0)
                turn(NC - 1, 1)
                down(NC - 2, 0)
                up(NC - 1, 1)
                down(NC - 1, 1)

            @block.scalar
            def _(act):
                act.wait_ge(w_in, 16 * LOADS)
                nc.scalar.copy(w1[:, 0], w1_in[:]).then_inc(w_high, 1)
                nc.scalar.copy(w2[:, 0], w2_in[:]).then_inc(w_high, 1)

                def h_out(n, p):
                    act.wait_ge(s["turned"].sem, s["turned"].upto(g(n)))
                    if not early(n, 1):
                        act.wait_ge(s["h_split"].sem, s["h_split"].upto(g(n - 1)))
                    if not early(n, 2):
                        act.wait_ge(s["lifted"].sem, s["lifted"].upto(g(n - 2)))
                    for k in range(KT):
                        for dst_ in (hF[:, k, :], hT[:, p, 0, k, :]):
                            nc.scalar.activation(dst_, pH[:, k, :], ACT.Identity, bias=lb[:, k:k + 1],
                                                 scale=lg[:, k:k + 1]).then_inc(s["hT_ready"].sem, 1)

                def gelu(n, j):
                    act.wait_ge(s["gated"].sem, s["gated"].upto(g(n), j + 1))
                    if not (early(n, 1) and layer == 0 and j < 2):
                        act.wait_ge(s["mixed"].sem, g(n) * HB + j - 1)
                    nc.scalar.activation(gl[:, j % 2, :], pG[:, j % 2, :], ACT.Gelu,
                                         bias=b1[:, 1, j:j + 1]).then_inc(s["gelu"].sem, 1)

                def u_high(n, j):
                    act.wait_ge(s["mixed"].sem, s["mixed"].upto(g(n), j + 1))
                    if j == 0 and not early(n, 1):
                        act.wait_ge(s["y_done"].sem, s["y_done"].upto(g(n - 1)))
                    nc.scalar.copy(u[:, 0, j, :], uF[:, j % 2, :]).then_inc(s["u_high"].sem, 1)

                def body(n, p, following=True):
                    gelu(n, 0)
                    for j in range(1, HB):
                        gelu(n, j)
                        u_high(n, j - 1)
                    u_high(n, HB - 1)
                    if following:
                        h_out(n + 1, 1 - p)

                h_out(0, 0)
                for n in range(2):
                    body(n, n)
                with act.Fori(1, NC // 2 - 1) as i:
                    for p in range(2):
                        body(i * 2 + p, p)
                body(NC - 2, 0)
                body(NC - 1, 1, following=False)


_INS = ["L0_attn_x", "L0_attn_wq", "L0_attn_wk_a", "L0_attn_wk_b", "L0_attn_wv_a", "L0_attn_wv_b", "L0_attn_wo",
        "L0_ffn_wqkv", "L0_ffn_q_scale", "L0_ffn_k_scale", "L0_ffn_wo", "L0_ffn_ln_g", "L0_ffn_ln_b", "L0_ffn_w1",
        "L0_ffn_b1", "L0_ffn_w2", "L0_ffn_b2", "L0_c", "L0_wmod"]


def kernel(**inputs):
    import concourse.bacc as bacc
    from concourse.bass_utils import run_bass_kernel_spmd

    nc = bacc.Bacc("TRN2", target_bir_lowering=False, num_devices=1)
    given = {name: np.ascontiguousarray(inputs[name]) for name in _INS}
    given.update(constants())
    arrays, args = {}, {}
    for name, array in given.items():
        arrays[f"in_{name}"] = array
        args[name] = nc.dram_tensor(f"in_{name}", array.shape, mybir.dt.from_np(array.dtype),
                                    kind="ExternalInput").ap()
    out = nc.dram_tensor("out", (B, N, D), F32, kind="ExternalOutput").ap()
    build(nc, args, out)
    r = run_bass_kernel_spmd(nc, [arrays], core_ids=[0])
    return r.results[0]["out"]
```
